# Optimizing a Trainium2 kernel written in Bass

```python
import numpy as np
import jax
import jax.numpy as jnp

def _softmax(x, axis=-1):
    return jax.nn.softmax(x, axis=axis)

def _gelu(x):
    return jax.nn.gelu(x, approximate=True)

def _silu(x):
    return jax.nn.silu(x)

def _sigmoid(x):
    return jax.nn.sigmoid(x)

def _layernorm(x, axis=-1, eps=1e-05):
    m = jnp.mean(x, axis=axis, keepdims=True)
    v = jnp.var(x, axis=axis, keepdims=True)
    return (x - m) / jnp.sqrt(v + eps)

def _scatter_add(tgt, idx, src, axis=0):
    return tgt.at[idx].add(src)

def _segment_sum(src, seg, n):
    return jax.ops.segment_sum(src, seg, n)
kernel_name = 'mk_gnn_resnorm_d4_gnn_r8_897eba'

def setup_inputs(seed: int=0):
    np.random.seed(seed)
    _w = jnp.asarray

    def _rec_inputs():
        import jax
        import jax.numpy as jnp
        _gk = jax.random.key(seed)
        x = -0.0001006 + 1 * jax.random.normal(jax.random.fold_in(_gk, 1), (6250, 96), jnp.float32)
        _s = jax.random.randint(jax.random.fold_in(_gk, 2), (50000,), 0, 6250, jnp.int32)
        _d = jax.random.randint(jax.random.fold_in(_gk, 3), (50000,), 0, 6250, jnp.int32)
        _loop = jnp.arange(6250, dtype=jnp.int32)
        src = jnp.concatenate([_s, _d, _loop])
        dst = jnp.concatenate([_d, _s, _loop])
        _o = jnp.argsort(dst, stable=True)
        src = src[_o]
        dst = dst[_o]
        edge_attr_17 = jax.random.uniform(jax.random.fold_in(_gk, 12), (106250, 17), jnp.float32, 0.0, 1)
        edge_attr_96 = 5.93493e-05 + 1.00006 * jax.random.normal(jax.random.fold_in(_gk, 13), (106250, 96), jnp.float32)
        return (x, src, dst, edge_attr_17, edge_attr_96)
    x, src, dst, edge_attr_17, edge_attr_96 = _rec_inputs()

    def _L0_gnn_setup():
        import jax, jax.numpy as jnp
        import numpy as np
        N = 6250
        E = 100000
        D = 96
        ED = 17
        key = jax.random.key(seed)
        ks = jax.random.split(key, 12)
        x = jax.random.normal(ks[0], (N, D), dtype=jnp.float32)
        edge_index = jax.random.randint(ks[1], (2, E), 0, N, dtype=jnp.int64)
        edge_attr = jax.random.uniform(ks[2], (E, ED), dtype=jnp.float32)
        s = 1.0 / np.sqrt(ED)
        W1 = jax.random.uniform(ks[3], (D, ED), jnp.float32, -s, s)
        b1 = jax.random.uniform(ks[4], (D,), jnp.float32, -s, s)
        s = 1.0 / np.sqrt(D)
        W2 = jax.random.uniform(ks[5], (D, D), jnp.float32, -s, s)
        b2 = jax.random.uniform(ks[6], (D,), jnp.float32, -s, s)
        Ws = jax.random.uniform(ks[7], (D, D), jnp.float32, -s, s)
        bs = jax.random.uniform(ks[8], (D,), jnp.float32, -s, s)
        Wn = jax.random.uniform(ks[9], (D, D), jnp.float32, -s, s)
        bn = jax.random.uniform(ks[10], (D,), jnp.float32, -s, s)
        return {'x': x, 'edge_index': edge_index, 'edge_attr': edge_attr, 'W1': W1, 'b1': b1, 'W2': W2, 'b2': b2, 'Ws': Ws, 'bs': bs, 'Wn': Wn, 'bn': bn}
    _L0_gnn_all = _L0_gnn_setup()
    _L0_gnn_in = {k: v for k, v in _L0_gnn_all.items() if k in ('W1', 'b1', 'W2', 'b2', 'Ws', 'bs', 'Wn', 'bn')}
    del _L0_gnn_all

    def _L1_gnn_setup():
        import jax, jax.numpy as jnp
        import numpy as np
        N_NODES = 6250
        N_EDGES = 100000
        D_IN = 96
        D_HID = 96
        D_OUT = 96

        def _mean_agg(x, src, dst, n_nodes):
            msg = x[src]
            summed = jax.ops.segment_sum(msg, dst, num_segments=n_nodes)
            deg = jax.ops.segment_sum(jnp.ones((src.shape[0],), x.dtype), dst, num_segments=n_nodes)
            return summed / jnp.maximum(deg, 1.0)[:, None]

        def _sage_conv(x, src, dst, W_self, W_neigh, b):
            agg = _mean_agg(x, src, dst, x.shape[0])
            return x @ W_self + agg @ W_neigh + b
        key = jax.random.key(seed)
        ks = jax.random.split(key, 9)
        s = 0.05
        return {'x': jax.random.normal(ks[0], (N_NODES, D_IN), jnp.float32), 'src': jax.random.randint(ks[1], (N_EDGES,), 0, N_NODES), 'dst': jax.random.randint(ks[2], (N_EDGES,), 0, N_NODES), 'W_self1': jax.random.normal(ks[3], (D_IN, D_HID), jnp.float32) * s, 'W_neigh1': jax.random.normal(ks[4], (D_IN, D_HID), jnp.float32) * s, 'b1': jnp.zeros((D_HID,), jnp.float32), 'W_self2': jax.random.normal(ks[5], (D_HID, D_OUT), jnp.float32) * s, 'W_neigh2': jax.random.normal(ks[6], (D_HID, D_OUT), jnp.float32) * s, 'b2': jnp.zeros((D_OUT,), jnp.float32)}
    _L1_gnn_all = _L1_gnn_setup()
    _L1_gnn_in = {k: v for k, v in _L1_gnn_all.items() if k in ('W_self1', 'W_neigh1', 'b1', 'W_self2', 'W_neigh2', 'b2')}
    del _L1_gnn_all

    def _L2_gnn_setup():
        import jax, jax.numpy as jnp
        import numpy as np
        N_NODES = 6250
        N_EDGES = 100000
        IN_DIM = 96
        NUM_HEADS = 8
        HEAD_DIM = IN_DIM // NUM_HEADS
        key = jax.random.key(seed)
        ks = jax.random.split(key, 11)
        s = 1.0 / np.sqrt(IN_DIM)
        return {'x': jax.random.normal(ks[0], (N_NODES, IN_DIM), dtype=jnp.float32), 'edge_index': jax.random.randint(ks[1], (2, N_EDGES), 0, N_NODES, dtype=jnp.int64), 'edge_attr': jax.random.normal(ks[2], (N_EDGES, IN_DIM), dtype=jnp.float32), 'Wq': jax.random.normal(ks[3], (IN_DIM, IN_DIM), dtype=jnp.float32) * s, 'bq': jax.random.normal(ks[4], (IN_DIM,), dtype=jnp.float32) * s, 'Wk': jax.random.normal(ks[5], (IN_DIM, IN_DIM), dtype=jnp.float32) * s, 'bk': jax.random.normal(ks[6], (IN_DIM,), dtype=jnp.float32) * s, 'We': jax.random.normal(ks[7], (IN_DIM, IN_DIM), dtype=jnp.float32) * s, 'be': jax.random.normal(ks[8], (IN_DIM,), dtype=jnp.float32) * s, 'Wv': jax.random.normal(ks[9], (IN_DIM, IN_DIM), dtype=jnp.float32) * s, 'bv': jax.random.normal(ks[10], (IN_DIM,), dtype=jnp.float32) * s}
    _L2_gnn_all = _L2_gnn_setup()
    _L2_gnn_in = {k: v for k, v in _L2_gnn_all.items() if k in ('Wq', 'bq', 'Wk', 'bk', 'We', 'be', 'Wv', 'bv')}
    del _L2_gnn_all

    def _L3_gnn_setup():
        import jax, jax.numpy as jnp
        import numpy as np
        N = 6250
        E = 100000
        D = 96

        def _mean_aggr(h, src, dst, num_nodes):
            msgs = h[src]
            summed = jax.ops.segment_sum(msgs, dst, num_segments=num_nodes)
            deg = jax.ops.segment_sum(jnp.ones((src.shape[0],), h.dtype), dst, num_segments=num_nodes)
            return summed / jnp.maximum(deg, 1.0)[:, None]

        def _sage_conv(h, src, dst, Wl, bl, Wr, num_nodes):
            agg = _mean_aggr(h, src, dst, num_nodes)
            return agg @ Wl.T + bl + h @ Wr.T
        key = jax.random.key(seed)
        ks = jax.random.split(key, 8)
        s = 1.0 / np.sqrt(D)
        return {'x': jax.random.normal(ks[0], (N, D), dtype=jnp.float32), 'edge_index': jax.random.randint(ks[1], (2, E), 0, N, dtype=jnp.int64), 'Wl1': jax.random.normal(ks[2], (D, D), dtype=jnp.float32) * s, 'bl1': jnp.zeros((D,), dtype=jnp.float32), 'Wr1': jax.random.normal(ks[3], (D, D), dtype=jnp.float32) * s, 'Wl2': jax.random.normal(ks[4], (D, D), dtype=jnp.float32) * s, 'bl2': jnp.zeros((D,), dtype=jnp.float32), 'Wr2': jax.random.normal(ks[5], (D, D), dtype=jnp.float32) * s}
    _L3_gnn_all = _L3_gnn_setup()
    _L3_gnn_in = {k: v for k, v in _L3_gnn_all.items() if k in ('Wl1', 'bl1', 'Wr1', 'Wl2', 'bl2', 'Wr2')}
    del _L3_gnn_all
    return {'x': x, 'src': src, 'dst': dst, 'edge_attr_17': edge_attr_17, 'edge_attr_96': edge_attr_96, 'L0_gnn_W1': _L0_gnn_in['W1'], 'L0_gnn_b1': _L0_gnn_in['b1'], 'L0_gnn_W2': _L0_gnn_in['W2'], 'L0_gnn_b2': _L0_gnn_in['b2'], 'L0_gnn_Ws': _L0_gnn_in['Ws'], 'L0_gnn_bs': _L0_gnn_in['bs'], 'L0_gnn_Wn': _L0_gnn_in['Wn'], 'L0_gnn_bn': _L0_gnn_in['bn'], 'L1_gnn_W_self1': _L1_gnn_in['W_self1'], 'L1_gnn_W_neigh1': _L1_gnn_in['W_neigh1'], 'L1_gnn_b1': _L1_gnn_in['b1'], 'L1_gnn_W_self2': _L1_gnn_in['W_self2'], 'L1_gnn_W_neigh2': _L1_gnn_in['W_neigh2'], 'L1_gnn_b2': _L1_gnn_in['b2'], 'L2_gnn_Wq': _L2_gnn_in['Wq'], 'L2_gnn_bq': _L2_gnn_in['bq'], 'L2_gnn_Wk': _L2_gnn_in['Wk'], 'L2_gnn_bk': _L2_gnn_in['bk'], 'L2_gnn_We': _L2_gnn_in['We'], 'L2_gnn_be': _L2_gnn_in['be'], 'L2_gnn_Wv': _L2_gnn_in['Wv'], 'L2_gnn_bv': _L2_gnn_in['bv'], 'L3_gnn_Wl1': _L3_gnn_in['Wl1'], 'L3_gnn_bl1': _L3_gnn_in['bl1'], 'L3_gnn_Wr1': _L3_gnn_in['Wr1'], 'L3_gnn_Wl2': _L3_gnn_in['Wl2'], 'L3_gnn_bl2': _L3_gnn_in['bl2'], 'L3_gnn_Wr2': _L3_gnn_in['Wr2']}

def reference(x, src, dst, edge_attr_17, edge_attr_96, L0_gnn_W1, L0_gnn_b1, L0_gnn_W2, L0_gnn_b2, L0_gnn_Ws, L0_gnn_bs, L0_gnn_Wn, L0_gnn_bn, L1_gnn_W_self1, L1_gnn_W_neigh1, L1_gnn_b1, L1_gnn_W_self2, L1_gnn_W_neigh2, L1_gnn_b2, L2_gnn_Wq, L2_gnn_bq, L2_gnn_Wk, L2_gnn_bk, L2_gnn_We, L2_gnn_be, L2_gnn_Wv, L2_gnn_bv, L3_gnn_Wl1, L3_gnn_bl1, L3_gnn_Wr1, L3_gnn_Wl2, L3_gnn_bl2, L3_gnn_Wr2):
    import jax
    import jax.numpy as jnp

    def _L0_gnn_ref(x, edge_index, edge_attr, W1, b1, W2, b2, Ws, bs, Wn, bn):
        import jax, jax.numpy as jnp
        import numpy as np
        N = 6250
        E = 100000
        D = 96
        ED = 17
        src, dst = (edge_index[0], edge_index[1])
        h = jax.nn.relu(edge_attr @ W1.T + b1)
        w = h @ W2.T + b2
        msg = w * x[src]
        agg = jax.ops.segment_sum(msg, dst, num_segments=x.shape[0])
        return jax.nn.relu(x @ Ws.T + bs + agg @ Wn.T + bn)

    def _L1_gnn_ref(x, src, dst, W_self1, W_neigh1, b1, W_self2, W_neigh2, b2):
        import jax, jax.numpy as jnp
        import numpy as np
        N_NODES = 6250
        N_EDGES = 100000
        D_IN = 96
        D_HID = 96
        D_OUT = 96

        def _mean_agg(x, src, dst, n_nodes):
            msg = x[src]
            summed = jax.ops.segment_sum(msg, dst, num_segments=n_nodes)
            deg = jax.ops.segment_sum(jnp.ones((src.shape[0],), x.dtype), dst, num_segments=n_nodes)
            return summed / jnp.maximum(deg, 1.0)[:, None]

        def _sage_conv(x, src, dst, W_self, W_neigh, b):
            agg = _mean_agg(x, src, dst, x.shape[0])
            return x @ W_self + agg @ W_neigh + b
        h = _sage_conv(x, src, dst, W_self1, W_neigh1, b1)
        h = jax.nn.relu(h)
        h = _sage_conv(h, src, dst, W_self2, W_neigh2, b2)
        return h

    def _L2_gnn_ref(x, edge_index, edge_attr, Wq, bq, Wk, bk, We, be, Wv, bv):
        import jax, jax.numpy as jnp
        import numpy as np
        N_NODES = 6250
        N_EDGES = 100000
        IN_DIM = 96
        NUM_HEADS = 8
        HEAD_DIM = IN_DIM // NUM_HEADS
        N = x.shape[0]
        H, D = (NUM_HEADS, HEAD_DIM)
        Q_h = (x @ Wq + bq).reshape(N, H, D)
        K_h = (x @ Wk + bk).reshape(N, H, D)
        V_h = (x @ Wv + bv).reshape(N, H, D)
        E = (edge_attr @ We + be).reshape(-1, H, D)
        src_idx = edge_index[0]
        dst_idx = edge_index[1]
        src = K_h[src_idx]
        dest = Q_h[dst_idx]
        score = src * dest / jnp.sqrt(jnp.asarray(D, x.dtype))
        score = score * E
        score = jnp.exp(jnp.clip(score.sum(-1, keepdims=True), -5.0, 5.0))
        msg = V_h[src_idx] * score
        wV = jax.ops.segment_sum(msg, dst_idx, num_segments=N)
        Z = jax.ops.segment_sum(score, dst_idx, num_segments=N)
        h_out = wV / (Z + 1e-06)
        return h_out.reshape(N, H * D)

    def _L3_gnn_ref(x, edge_index, Wl1, bl1, Wr1, Wl2, bl2, Wr2):
        import jax, jax.numpy as jnp
        import numpy as np
        N = 6250
        E = 100000
        D = 96

        def _mean_aggr(h, src, dst, num_nodes):
            msgs = h[src]
            summed = jax.ops.segment_sum(msgs, dst, num_segments=num_nodes)
            deg = jax.ops.segment_sum(jnp.ones((src.shape[0],), h.dtype), dst, num_segments=num_nodes)
            return summed / jnp.maximum(deg, 1.0)[:, None]

        def _sage_conv(h, src, dst, Wl, bl, Wr, num_nodes):
            agg = _mean_aggr(h, src, dst, num_nodes)
            return agg @ Wl.T + bl + h @ Wr.T
        src, dst = (edge_index[0], edge_index[1])
        n = x.shape[0]
        h = _sage_conv(x, src, dst, Wl1, bl1, Wr1, n)
        h = jax.nn.relu(h)
        h = _sage_conv(h, src, dst, Wl2, bl2, Wr2, n)
        return h
    edge_index = jnp.stack([src, dst])
    x = _layernorm(x + _L0_gnn_ref(x, edge_index, edge_attr_17, L0_gnn_W1, L0_gnn_b1, L0_gnn_W2, L0_gnn_b2, L0_gnn_Ws, L0_gnn_bs, L0_gnn_Wn, L0_gnn_bn), axis=-1)
    x = _layernorm(x + _L1_gnn_ref(x, src, dst, L1_gnn_W_self1, L1_gnn_W_neigh1, L1_gnn_b1, L1_gnn_W_self2, L1_gnn_W_neigh2, L1_gnn_b2), axis=-1)
    x = _layernorm(x + _L2_gnn_ref(x, edge_index, edge_attr_96, L2_gnn_Wq, L2_gnn_bq, L2_gnn_Wk, L2_gnn_bk, L2_gnn_We, L2_gnn_be, L2_gnn_Wv, L2_gnn_bv), axis=-1)
    x = _layernorm(x + _L3_gnn_ref(x, edge_index, L3_gnn_Wl1, L3_gnn_bl1, L3_gnn_Wr1, L3_gnn_Wl2, L3_gnn_bl2, L3_gnn_Wr2), axis=-1)
    return x

_drawn_inputs = setup_inputs


def setup_inputs(seed=0):
    import zlib

    import numpy as np

    out = dict(_drawn_inputs(seed))
    spreads = {'L1_gnn_b1': (0.0, 0.1),
     'L1_gnn_b2': (0.0, 0.1),
     'L3_gnn_bl1': (0.0, 0.1),
     'L3_gnn_bl2': (0.0, 0.1)}
    factors = {}
    for name, (base, spread) in spreads.items():
        noise = np.random.default_rng([zlib.crc32(name.encode()), seed]).standard_normal(out[name].shape)
        drawn = base * np.exp(spread * noise) if base else spread * noise
        out[name] = jnp.asarray(drawn.astype(out[name].dtype))
    for name, factor in factors.items():
        out[name] = (out[name] * factor).astype(out[name].dtype)
    return out
```

```python
import concourse.bass as bass
from concourse import mybir
from contextlib import ExitStack

F32 = mybir.dt.float32
BF16 = mybir.dt.bfloat16
I32 = mybir.dt.int32
ALU = mybir.AluOpType
ACT = mybir.ActivationFunctionType
AX = mybir.AxisListType

P = 128
D = 96
ATTR = 17
HEADS = 8
HD = D // HEADS
N = 6250
E = 106250
TILES = -(-N // P)
NP = TILES * P
T = 4
GE = T * P
SLOTS = 4
BODIES = -(-E // (GE * SLOTS))
GROUPS = BODIES * SLOTS
EP = GROUPS * GE
WIN = 64
WIDE = 448
WIDES = NP // WIDE
TILE_LAG = 5
AHEAD = 2
HIGH = D + HEADS
EPS = 1e-5
PARTS = 3
CREDIT = 4

GATED, SAGE, ATTEND = "gated", "sage", "attend"
ROUNDS = [(GATED, "first"), (SAGE, "hidden"), (SAGE, "project"), (ATTEND, "attended"),
          (SAGE, "hidden"), (SAGE, "output")]
LAYER_SRC = {"first": "x", "hidden": "x", "project": "h", "output": "h"}
NORMED = [r for r, (_, n) in enumerate(ROUNDS) if n != "hidden"]
BLENDED = [r for r, (_, n) in enumerate(ROUNDS) if n in ("hidden", "project", "output")]
HIDDEN = [r for r, (_, n) in enumerate(ROUNDS) if n == "hidden"]
WEIGHTED = [r for r, (k, _) in enumerate(ROUNDS) if k != SAGE]
STORED = [r for r, (_, n) in enumerate(ROUNDS) if n != "project"]
SELF = [r for r, (_, n) in enumerate(ROUNDS) if n != "attended"]

W_NAMES = ["gate2", "self0", "bias0", "neigh0", "selfs1", "neigh1", "selfs2", "neigh2", "edge",
           "key", "value", "query", "selfs4", "neigh4", "selfs5", "neigh5"]
W_COL = {n: i * (D + 1) for i, n in enumerate(W_NAMES)}
W_WIDTH = len(W_NAMES) * (D + 1) + 1
ROUND_W = {1: ("selfs1", "neigh1"), 2: ("selfs2", "neigh2"), 4: ("selfs4", "neigh4"), 5: ("selfs5", "neigh5")}
C_IDENT, C_IOTA, C_WIDE, C_LIMIT = 0, P, P + WIDE, P + WIDE + WIDES
C_EPS = C_LIMIT + BODIES
C_NODE = C_EPS + 1
C_WIDTH = C_NODE + 1


def build(nc, x, src, dst, dst_row, base, attr17, attr96, gate1, weights, consts, out):
    with ExitStack() as ctx:
        def sb(name, shape, dt=F32):
            return ctx.enter_context(nc.sbuf_tensor(name, shape, dt))

        def sem(name):
            return ctx.enter_context(nc.semaphore(name))

        table = {r: nc.dram_tensor(f"table{r}", (NP, D), F32).ap() for r in (0, 1, 3, 4)}
        table_kv = nc.dram_tensor("table_kv", (NP, 2 * D), F32).ap()
        table_q = nc.dram_tensor("table_q", (NP, D), F32).ap()
        table_qp = nc.dram_tensor("table_qp", (NP, PARTS * D), BF16).ap()
        gathered_from = {0: x, 1: table[0], 2: table[1], 3: table_kv, 4: table[3], 5: table[4]}
        stored_to = {**table, 5: out}

        acc = sb("acc", [HIGH, NP])
        xs_all = sb("x_all", [P, TILES * D])
        hs_all = sb("h_all", [P, TILES * D])
        inv_deg = sb("inv_deg", [P, TILES])
        src_idx = sb("src_idx", [P, (GROUPS + AHEAD) * T], I32)
        dst_idx = sb("dst_idx", [P, (GROUPS + AHEAD) * T], I32)
        dst_f = sb("dst_f", [P, GROUPS * T])
        rel = sb("rel", [P, GROUPS * T])
        base_int = sb("base_int", [P, GROUPS], I32)
        base_f = sb("base_f", [P, GROUPS])
        wts = sb("wts", [D + 1, W_WIDTH])
        w_gate1 = sb("w_gate1", [ATTR, D])
        con = sb("con", [P, C_WIDTH])
        zeros = sb("zeros", [P, P])
        worst = sb("worst", [P, 4])
        worst_row = sb("worst_row", [1, 2])
        near_flag = sb("near_flag", [1, 1], I32)
        per = range(SLOTS)
        staged = [sb(f"staged{q}", [P, T], I32) for q in per]
        staged_dst = [sb(f"staged_dst{q}", [P, T], I32) for q in per]
        rows = [sb(f"rows{q}", [P, T * 2 * D]) for q in per]
        msg = [sb(f"msg{q}", [P, T, HIGH]) for q in per]
        onehot = [sb(f"onehot{q}", [P, T, WIN]) for q in per]
        attr_n = [sb(f"attr_n{q}", [ATTR, GE]) for q in per]
        attr_w = [sb(f"attr_w{q}", [D + 1, GE]) for q in per]
        q_win = [sb(f"q_win{q}", [WIN, PARTS * D], BF16) for q in per]
        dst_wide = [sb(f"dst_wide{q}", [WIN, GE], I32) for q in per]
        win_node = sb("win_node", [WIN, GROUPS])
        q_rows = sb("q_rows", [P, T * D])
        hidden = [sb(f"hidden{i}", [D + 1, GE]) for i in range(2)]
        onehot_t = [sb(f"onehot_t{i}", [WIN, GE], BF16) for i in range(2)]
        prod = sb("prod", [P, T, D])
        score = sb("score", [P, T, HEADS])
        capped = [sb(f"capped{i}", [P, T, HEADS]) for i in range(2)]
        wide_rel = sb("wide_rel", [P, T])
        wide_hot = sb("wide_hot", [P, T, WIDE])
        acc_tile = sb("acc_tile", [HIGH, P])
        x_tile = sb("x_tile", [P, D])
        x_turn = sb("x_turn", [D + 1, P])
        new_turn = sb("new_turn", [D + 1, P])
        degree = sb("degree", [P, 1])
        averaged = sb("averaged", [P, D])
        blend = sb("blend", [P, D])
        resid = sb("resid", [P, D])
        stats = sb("stats", [P, 6])
        moments = sb("moments", [P, 2])
        root = sb("root", [P, 1])
        rstd = sb("rstd", [P, 1])
        denom = sb("denom", [P, HEADS])
        inv_denom = sb("inv_denom", [P, HEADS])
        new_tile = sb("new_tile", [P, D])
        kvq_tile = sb("kvq_tile", [P, 3 * D])
        q_rest = sb("q_rest", [P, 2, D])
        q_parts = sb("q_parts", [P, PARTS, D], BF16)

        bank = [ctx.enter_context(nc.psum_tensor(f"bank{i}", [P, 512], F32)) for i in range(8)]
        TURN, NODE = bank[6], bank[7]

        loaded = sem("loaded"); x_landed = sem("x_landed"); cleared = sem("cleared")
        prep = sem("prep"); worst_turned = sem("worst_turned"); ready = sem("ready")
        rows_landed = [sem(f"rows_landed{q}") for q in per]
        q_rows_landed = sem("q_rows_landed")
        attr_landed = [sem(f"attr_landed{q}") for q in per]
        q_win_landed = [sem(f"q_win_landed{q}") for q in per]
        idx_staged = sem("idx_staged")
        waits_passed = {e.engine: sem(f"waits_passed_{n}") for n, e in (("pe", nc.tensor), ("act", nc.scalar), ("dve", nc.vector), ("pool", nc.gpsimd))}
        onehot_made = sem("onehot_made"); hidden_summed = sem("hidden_summed"); hidden_made = sem("hidden_made")
        weights_summed = sem("weights_summed"); msg_made = sem("msg_made")
        group_summed = sem("group_summed"); group_added = sem("group_added")
        onehot_t_made = sem("onehot_t_made")
        dst_wide_landed = [sem(f"dst_wide_landed{q}") for q in per]; q_part_made = sem("q_part_made")
        query_summed = sem("query_summed"); key_scaled = sem("key_scaled"); products_made = sem("products_made")
        score_summed = sem("score_summed"); score_low = sem("score_low"); capped_made = sem("capped_made")
        exp_made = sem("exp_made")
        wide_rel_made = sem("wide_rel_made"); wide_hot_made = sem("wide_hot_made")
        wide_summed = sem("wide_summed"); wide_added = sem("wide_added")
        acc_staged = sem("acc_staged"); acc_zeroed = sem("acc_zeroed"); x_staged = sem("x_staged")
        x_turned = sem("x_turned"); x_turn_made = sem("x_turn_made"); node_summed = sem("node_summed")
        degree_made = sem("degree_made"); averaged_made = sem("averaged_made"); blended = sem("blended"); resid_made = sem("resid_made")
        stats_made = sem("stats_made"); moments_made = sem("moments_made"); root_made = sem("root_made"); rstd_made = sem("rstd_made")
        denom_made = sem("denom_made"); inv_denom_made = sem("inv_denom_made"); attended = sem("attended")
        node_made = sem("node_made"); node_kept = sem("node_kept"); table_stored = sem("table_stored")
        new_turned = sem("new_turned"); new_turn_made = sem("new_turn_made")
        kvq_summed = sem("kvq_summed"); kvq_made = sem("kvq_made")
        kv_stored = sem("kv_stored"); q_stored = sem("q_stored")

        ident = con[:, C_IDENT:C_IDENT + P]

        def w(name, k=D + 1, n=D):
            return wts[0:k, W_COL[name]:W_COL[name] + n]

        def group(r, b, q, of=None, back=0):
            k = r if of is None else of.index(r)
            return b * SLOTS + (k * GROUPS + q + 1 + CREDIT - back)

        def tile(r, j, of=None, back=0):
            k = r if of is None else of.index(r)
            return j + (k * TILES + 1 + CREDIT - back)

        def body(r, b, of=None, back=0):
            k = r if of is None else of.index(r)
            return b + (k * BODIES + 1 - back)

        def q_part(j, step):
            return j * 5 + (CREDIT + 1 + step)

        def window(r, b, q, v, back=0):
            return b * (SLOTS * WIDES) + v + ((r * GROUPS + q) * WIDES + 1 + CREDIT - back)

        def start(eng, *sems):
            for s in sems:
                eng.sem_inc(s, CREDIT)

        def passed(eng):
            eng.sem_inc(waits_passed[eng.engine], 1)

        def schedule(eng, r, near, groups, nodes):
            if near:
                with eng.Fori(0, TILE_LAG) as b:
                    groups(b, lambda place: None)
                with eng.Fori(TILE_LAG, BODIES) as b:
                    groups(b, lambda place: nodes(place, b - TILE_LAG, b))
                for j in range(BODIES - TILE_LAG, TILES):
                    for place in range(SLOTS + 1):
                        nodes(place, j, BODIES)
            else:
                with eng.Fori(0, BODIES) as b:
                    groups(b, lambda place: None)
                with eng.Fori(0, TILES - 1) as j:
                    for place in range(SLOTS + 1):
                        nodes(place, j, BODIES)
                for place in range(SLOTS + 1):
                    nodes(place, TILES - 1, BODIES)

        def window_starts(eng, b):
            _, starts = nc.values_load_multi_w_load_instructions(
                base_int[0:1, bass.ds(b * SLOTS, SLOTS)], engines=[eng.engine], min_val=0, max_val=NP - WIN)
            return starts

        def either(eng, program):
            eng.wait_ge(ready, 1)
            near = eng.value_load(near_flag[0:1, 0:1], min_val=0, max_val=1)
            with eng.If(near):
                program(True)
            with eng.Else():
                program(False)

        block = ctx.enter_context(nc.Block())

        @block.sync
        def _(sp):
            sp.dma_start(dst_idx[:, :], dst).then_inc(loaded, 16)
            sp.dma_start(base_int[:, :], base.partition_broadcast(P)).then_inc(loaded, 16)
            sp.dma_start(con[:, :], consts).then_inc(loaded, 16)
            sp.dma_start(src_idx[:, :], src).then_inc(loaded, 16)
            sp.dma_start(wts[:, :], weights).then_inc(loaded, 16)
            sp.dma_start(w_gate1[:, :], gate1).then_inc(loaded, 16)
            sp.dma_start(xs_all[:, :].rearrange("p (j d) -> p j d", d=D),
                         x.rearrange("(j p) d -> p j d", p=P)).then_inc(x_landed, 16)

            def program(near):
                for r, (kind, _) in enumerate(ROUNDS):
                    if kind == SAGE:
                        continue
                    if kind == ATTEND:
                        sp.wait_ge(q_stored, 16 * TILES + 16)
                    with sp.Fori(0, BODIES) as b:
                        starts = window_starts(sp, b) if kind == ATTEND and near else None
                        for q in per:
                            if kind == GATED:
                                sp.wait_ge(hidden_summed, group(r, b, q, [0], SLOTS))
                                sp.dma_start(attr_n[q][:, :], attr17[:, bass.ds((b * SLOTS + q) * GE, GE)]).then_inc(attr_landed[q], 16)
                            else:
                                sp.wait_ge(weights_summed, group(r, b, q, WEIGHTED, SLOTS))
                                sp.dma_start(attr_w[q][0:D, :], attr96[:, bass.ds((b * SLOTS + q) * GE, GE)]).then_inc(attr_landed[q], 16)
                                if near:
                                    sp.wait_ge(onehot_t_made, group(r, b, q, [r], SLOTS))
                                    sp.dma_start(dst_wide[q][:, :], dst_row[:, bass.ds((b * SLOTS + q) * GE, GE)].partition_broadcast(WIN)).then_inc(dst_wide_landed[q], 16)
                                    sp.wait_ge(query_summed, group(r, b, q, [r], SLOTS))
                                    sp.dma_start(q_win[q][:, :], table_qp[bass.ds(starts[q], WIN), :]).then_inc(q_win_landed[q], 16)

            either(sp, program)
            sp.wait_ge(table_stored, 16 * TILES * len(STORED) + 16)

        @block.gpsimd
        def _(pool):
            def program(near):
                for r, (kind, _) in enumerate(ROUNDS):
                    if kind == ATTEND:
                        pool.wait_ge(kv_stored, 16 * TILES + 16)
                        pool.wait_ge(q_stored, 16 * TILES + 16)
                    elif r:
                        pool.wait_ge(table_stored, 16 * TILES * (STORED.index(r - 1) + 1) + 16)
                    width = 2 * D if kind == ATTEND else D
                    with pool.Fori(0, BODIES) as b:
                        for q in per:
                            pool.wait_ge(idx_staged, group(r, b, q))
                            passed(pool)
                            for t in range(T):
                                pool.indirect_dma_start(
                                    out=rows[q][:, t * width:(t + 1) * width], out_offset=None, in_=gathered_from[r],
                                    in_offset=bass.IndirectOffsetOnAxis(ap=staged[q][:, t:t + 1], axis=0),
                                ).then_inc(rows_landed[q], 16)
                            if kind == ATTEND and not near:
                                pool.wait_ge(products_made, group(r, b, q, [r], 1))
                                passed(pool)
                                for t in range(T):
                                    pool.indirect_dma_start(
                                        out=q_rows[:, t * D:(t + 1) * D], out_offset=None, in_=table_q,
                                        in_offset=bass.IndirectOffsetOnAxis(ap=staged_dst[q][:, t:t + 1], axis=0),
                                    ).then_inc(q_rows_landed, 16)

            either(pool, program)

        @block.scalar
        def _(act):
            start(act, idx_staged, exp_made, acc_staged, acc_zeroed, x_staged,
                  x_turn_made, root_made, node_kept, new_turn_made, kvq_made)
            for s in (table_stored, kv_stored, q_stored):
                act.sem_inc(s, 16)

            def groups(r, near):
                kind = ROUNDS[r][0]

                def run(b, node):
                    for q in per:
                        node(q)
                        n = q + AHEAD
                        act.wait_ge(group_summed, group(r, b, n, back=SLOTS))
                        passed(act)
                        cols = bass.ds((b * SLOTS + n) * T, T)
                        if not near:
                            nc.scalar.copy(staged_dst[n % SLOTS][:, :], dst_idx[:, cols])
                        nc.scalar.copy(staged[n % SLOTS][:, :], src_idx[:, cols]).then_inc(idx_staged, 1)
                        if kind == ATTEND:
                            act.wait_ge(capped_made, group(r, b, q, [r]))
                            act.wait_ge(group_summed, group(r, b, q, back=SLOTS))
                            nc.scalar.activation(msg[q][:, :, D:HIGH], capped[q % 2][:, :, :], ACT.Exp).then_inc(exp_made, 1)
                    node(SLOTS)
                return run

            def nodes(r, near):
                what = ROUNDS[r][1]
                operand = hs_all if LAYER_SRC.get(what) == "h" else xs_all

                def run(place, j, b):
                    cols = slice(j * P, (j + 1) * P) if isinstance(j, int) else bass.ds(j * P, P)
                    feats = slice(j * D, (j + 1) * D) if isinstance(j, int) else bass.ds(j * D, D)
                    if place == 0:
                        act.wait_ge(group_added, group(r, b, 0, back=1))
                        act.wait_ge(node_made, tile(r, j, back=1))
                        passed(act)
                        nc.scalar.copy(acc_tile[:, :], acc[:, cols]).then_inc(acc_staged, 1)
                        if r in SELF:
                            nc.scalar.copy(x_tile[:, :], operand[:, feats]).then_inc(x_staged, 1)
                    if place == 1:
                        act.wait_ge(acc_staged, tile(r, j))
                        passed(act)
                        nc.scalar.copy(acc[:, cols], zeros[0:HIGH, :]).then_inc(acc_zeroed, 1)
                    if place == 1 and r in SELF:
                        act.wait_ge(x_turned, tile(r, j, SELF))
                        nc.scalar.copy(x_turn[0:D, :], TURN[0:D, 0:P]).then_inc(x_turn_made, 1)
                    if place == 3 and r in NORMED:
                        act.wait_ge(moments_made, tile(r, j, NORMED))
                        act.wait_ge(node_made, tile(r, j, back=1))
                        nc.scalar.activation(root[:, :], moments[:, 1:2], ACT.Sqrt, bias=con[:, C_EPS:C_EPS + 1]).then_inc(root_made, 1)
                    if place == SLOTS:
                        act.wait_ge(node_made, tile(r, j))
                        if what != "output":
                            passed(act)
                            kept = hs_all if what == "hidden" else xs_all
                            nc.scalar.copy(kept[:, feats], new_tile[:, :]).then_inc(node_kept, 1)
                        if what != "project":
                            k = N - j * P if isinstance(j, int) and what == "output" and j == TILES - 1 else P
                            act.dma_start(stored_to[r][slice(j * P, j * P + k) if isinstance(j, int) else bass.ds(j * P, k), :],
                                          new_tile[0:k, :]).then_inc(table_stored, 16)
                    if place == SLOTS and what == "project":
                        at = slice(j * P, (j + 1) * P) if isinstance(j, int) else bass.ds(j * P, P)
                        act.wait_ge(new_turned, tile(r, j, [r]))
                        nc.scalar.copy(new_turn[0:D, :], TURN[0:D, 0:P]).then_inc(new_turn_made, 1)
                        act.wait_ge(kvq_summed, tile(r, j, [r]))
                        act.wait_ge(kv_stored, 16 * j + 16)
                        act.wait_ge(q_stored, 16 * j + 16)
                        nc.scalar.copy(kvq_tile[:, 0:2 * D], NODE[:, 0:2 * D])
                        nc.scalar.mul(kvq_tile[:, 2 * D:3 * D], NODE[:, 2 * D:3 * D], float(HD) ** -0.5).then_inc(kvq_made, 1)
                        act.wait_ge(kvq_made, tile(r, j, [r]))
                        act.dma_start(table_kv[at, :], kvq_tile[:, 0:2 * D]).then_inc(kv_stored, 16)
                        if near:
                            act.wait_ge(q_part_made, q_part(j, 4))
                            act.dma_start(table_qp[at, :], q_parts[:, :, :].rearrange("p k d -> p (k d)")).then_inc(q_stored, 16)
                        else:
                            act.dma_start(table_q[at, :], kvq_tile[:, 2 * D:3 * D]).then_inc(q_stored, 16)
                return run

            def program(near):
                for q in range(AHEAD):
                    if not near:
                        nc.scalar.copy(staged_dst[q][:, :], dst_idx[:, q * T:(q + 1) * T])
                    nc.scalar.copy(staged[q][:, :], src_idx[:, q * T:(q + 1) * T]).then_inc(idx_staged, 1)
                act.wait_ge(x_landed, 16)
                for r in range(len(ROUNDS)):
                    schedule(act, r, near, groups(r, near), nodes(r, near))

            either(act, program)

        @block.vector
        def _(dve):
            start(dve, hidden_made, onehot_t_made, q_part_made, onehot_made, msg_made, group_added, key_scaled, products_made, score_summed, score_low,
                  capped_made, wide_rel_made, wide_hot_made, wide_added, degree_made, averaged_made, blended, resid_made, stats_made,
                  moments_made, rstd_made, denom_made, inv_denom_made, attended, node_made)
            nc.vector.memset(acc[:, :], 0.0)
            nc.vector.memset(zeros[:, :], 0.0)
            nc.vector.memset(x_turn[D:D + 1, :], 1.0)
            nc.vector.memset(new_turn[D:D + 1, :], 1.0)
            for i in range(2):
                nc.vector.memset(hidden[i][D:D + 1, :], 1.0)
            for q in per:
                nc.vector.memset(attr_w[q][D:D + 1, :], 1.0)
                nc.vector.memset(msg[q][:, :, D:D + 1], 1.0)
            nc.vector.memset(worst[:, 3:4], 0.0).then_inc(cleared, 1)
            dve.wait_ge(cleared, 1)

            steps = [0]

            def then(ins):
                steps[0] += 1
                ins.then_inc(prep, 1)
                dve.wait_ge(prep, steps[0])

            dve.wait_ge(loaded, 16 * 6)
            then(nc.vector.tensor_copy(base_f[:, :], base_int[:, :]))
            then(nc.vector.tensor_scalar(base_f[:, :], base_f[:, :], float(NP - WIN), None, ALU.min))
            then(nc.vector.tensor_copy(base_int[:, :], base_f[:, :]))
            then(nc.vector.tensor_scalar(win_node[:, :], base_f[0:WIN, :], con[0:WIN, C_NODE:C_NODE + 1], None, ALU.add))
            then(nc.vector.tensor_copy(dst_f[:, :], dst_idx[:, 0:GROUPS * T]))
            by_body = [P, BODIES, SLOTS * T]
            then(nc.vector.tensor_tensor(rel[:, :].rearrange("p (b t) -> p b t", t=SLOTS * T),
                                         dst_f[:, :].rearrange("p (b t) -> p b t", t=SLOTS * T),
                                         con[:, C_LIMIT:C_LIMIT + BODIES].unsqueeze(2).to_broadcast(by_body), ALU.subtract))
            then(nc.vector.tensor_reduce(worst[:, 0:1], rel[:, :], AX.X, ALU.min))
            then(nc.vector.tensor_tensor(rel[:, :].rearrange("p (g t) -> p g t", t=T),
                                         dst_f[:, :].rearrange("p (g t) -> p g t", t=T),
                                         base_f[:, :].unsqueeze(2).to_broadcast([P, GROUPS, T]), ALU.subtract))
            then(nc.vector.tensor_reduce(worst[:, 1:2], rel[:, :], AX.X, ALU.min))
            then(nc.vector.tensor_reduce(worst[:, 2:3], rel[:, :], AX.X, ALU.max))
            then(nc.vector.tensor_scalar(worst[:, 2:3], worst[:, 2:3], -1.0, float(WIN - 1), ALU.mult, ALU.add))
            then(nc.vector.tensor_reduce(worst[:, 3:4], worst[:, 0:3], AX.X, ALU.min))
            then(nc.vector.tensor_tensor(w("self0"), w("self0"), w("bias0"), ALU.add))
            dve.wait_ge(worst_turned, 1)
            then(nc.vector.tensor_reduce(worst_row[:, 0:1], TURN[0:1, 0:P], AX.X, ALU.min))
            then(nc.vector.tensor_scalar(worst_row[:, 1:2], worst_row[:, 0:1], 0.0, None, ALU.is_ge))
            nc.vector.tensor_copy(near_flag[:, :], worst_row[:, 1:2]).then_inc(ready, 1)

            iota = con[:, C_IOTA:C_IOTA + WIDE]

            def groups(r, near):
                kind = ROUNDS[r][0]
                high = {GATED: D + 1, SAGE: D, ATTEND: HIGH}[kind]

                def hot(b, q):
                    dve.wait_ge(group_summed, group(r, b, q, back=SLOTS))
                    nc.vector.tensor_tensor(
                        onehot[q][:, :, :], iota[:, 0:WIN].unsqueeze(1).to_broadcast([P, T, WIN]),
                        rel[:, bass.ds((b * SLOTS + q) * T, T)].unsqueeze(2).to_broadcast([P, T, WIN]),
                        ALU.is_equal).then_inc(onehot_made, 1)

                def hide(b, q):
                    dve.wait_ge(hidden_summed, group(r, b, q, [0]))
                    dve.wait_ge(weights_summed, group(r, b, q, WEIGHTED, 2))
                    nc.vector.tensor_scalar(hidden[q % 2][0:D, :], bank[q % 2][0:D, :], wts[0:D, W_WIDTH - 1:W_WIDTH],
                                            0.0, ALU.add, ALU.max).then_inc(hidden_made, 1)

                def hot_t(b, q):
                    dve.wait_ge(dst_wide_landed[q], body(r, b, [r]) * 16)
                    dve.wait_ge(query_summed, group(r, b, q, [r], 2))
                    nc.vector.tensor_scalar(onehot_t[q % 2][:, :], dst_wide[q][:, :], win_node[:, bass.ds(b * SLOTS + q, 1)],
                                            None, ALU.is_equal).then_inc(onehot_t_made, 1)

                def gate(b, q):
                    dve.wait_ge(weights_summed, group(r, b, q, WEIGHTED))
                    dve.wait_ge(rows_landed[q], body(r, b) * (16 * T))
                    dve.wait_ge(group_summed, group(r, b, q, back=SLOTS))
                    nc.vector.tensor_tensor(msg[q][:, :, 0:D], bank[2 + q % 2][:, 0:T * D].rearrange("p (t d) -> p t d", d=D),
                                            rows[q][:, 0:T * D].rearrange("p (t d) -> p t d", d=D),
                                            ALU.mult).then_inc(msg_made, 1)

                def attend_scores(b, q):
                    kv = rows[q][:, :].rearrange("p (t d) -> p t d", d=2 * D)
                    dve.wait_ge(weights_summed, group(r, b, q, WEIGHTED))
                    dve.wait_ge(rows_landed[q], body(r, b) * (16 * T))
                    nc.vector.tensor_tensor(prod[:, :, :], bank[q % 2][:, 0:T * D].rearrange("p (t d) -> p t d", d=D),
                                            kv[:, :, 0:D], ALU.mult).then_inc(key_scaled, 1)
                    if near:
                        queries = bank[2 + q % 2][:, 0:T * D]
                        dve.wait_ge(query_summed, group(r, b, q, [r]))
                    else:
                        queries = q_rows[:, :]
                        dve.wait_ge(q_rows_landed, (b * SLOTS + q + 1) * (16 * T))
                    dve.wait_ge(key_scaled, group(r, b, q, [r]))
                    nc.vector.tensor_tensor(prod[:, :, :], prod[:, :, :], queries.rearrange("p (t d) -> p t d", d=D),
                                            ALU.mult).then_inc(products_made, 1)
                    dve.wait_ge(products_made, group(r, b, q, [r]))
                    nc.vector.tensor_reduce(score[:, :, :], prod[:, :, :].rearrange("p t (h d) -> p t h d", d=HD),
                                            AX.X, ALU.add).then_inc(score_summed, 1)
                    dve.wait_ge(score_summed, group(r, b, q, [r]))
                    nc.vector.tensor_scalar(capped[q % 2][:, :, :], score[:, :, :], 5.0, -5.0, ALU.min,
                                            ALU.max).then_inc(capped_made, 1)

                def attend_values(b, q):
                    kv = rows[q][:, :].rearrange("p (t d) -> p t d", d=2 * D)
                    dve.wait_ge(exp_made, group(r, b, q, [r]))
                    nc.vector.tensor_tensor(
                        msg[q][:, :, 0:D].rearrange("p t (h d) -> p t h d", d=HD),
                        kv[:, :, D:2 * D].rearrange("p t (h d) -> p t h d", d=HD),
                        msg[q][:, :, D:HIGH].unsqueeze(3).to_broadcast([P, T, HEADS, HD]), ALU.mult).then_inc(msg_made, 1)

                def add(b, q, starts):
                    dve.wait_ge(group_summed, group(r, b, q))
                    dve.wait_ge(group_added, group(r, b, q, back=1))
                    at = acc[0:high, bass.ds(starts[q], WIN)]
                    nc.vector.tensor_tensor(at, at, bank[4 + q % 2][0:high, 0:WIN], ALU.add).then_inc(group_added, 1)

                def add_wide(b, q):
                    with dve.Fori(0, WIDES) as v:
                        dve.wait_ge(wide_summed, window(r, b, q, v, 1))
                        nc.vector.tensor_scalar(wide_rel[:, :], dst_f[:, bass.ds((b * SLOTS + q) * T, T)],
                                                con[:, bass.ds(v + C_WIDE, 1)], None, ALU.subtract).then_inc(wide_rel_made, 1)
                        dve.wait_ge(wide_rel_made, window(r, b, q, v))
                        nc.vector.tensor_tensor(wide_hot[:, :, :], iota.unsqueeze(1).to_broadcast([P, T, WIDE]),
                                                wide_rel[:, :].unsqueeze(2).to_broadcast([P, T, WIDE]),
                                                ALU.is_equal).then_inc(wide_hot_made, 1)
                        dve.wait_ge(wide_summed, window(r, b, q, v))
                        dve.wait_ge(wide_added, window(r, b, q, v, 1))
                        at = acc[0:high, bass.ds(v * WIDE, WIDE)]
                        nc.vector.tensor_tensor(at, at, bank[4][0:high, 0:WIDE], ALU.add).then_inc(wide_added, 1)
                    dve.wait_ge(wide_added, window(r, b, q, WIDES - 1))
                    dve.sem_inc(group_added, 1)

                def run(b, node):
                    starts = window_starts(dve, b) if near else None
                    def ahead(q):
                        if near and kind == ATTEND:
                            hot_t(b, q)
                        if kind == GATED:
                            hide(b, q)
                        if near:
                            hot(b, q)

                    ahead(0)
                    for q in per:
                        if q + 1 < SLOTS:
                            ahead(q + 1)
                        if kind == GATED:
                            gate(b, q)
                        if kind == ATTEND:
                            attend_scores(b, q)
                        if kind == ATTEND and near and q:
                            attend_values(b, q - 1)
                        behind = 2 if kind == ATTEND else 1
                        if near and q >= behind:
                            add(b, q - behind, starts)
                        if not near:
                            if kind == ATTEND:
                                attend_values(b, q)
                            add_wide(b, q)
                        node(q)
                    if near:
                        if kind == ATTEND:
                            attend_values(b, SLOTS - 1)
                            add(b, SLOTS - 2, starts)
                        add(b, SLOTS - 1, starts)
                    node(SLOTS)
                return run

            def nodes(r, near):
                what = ROUNDS[r][1]

                def sums(j):
                    one = slice(j, j + 1) if isinstance(j, int) else bass.ds(j, 1)
                    feats = slice(j * D, (j + 1) * D) if isinstance(j, int) else bass.ds(j * D, D)
                    dve.wait_ge(node_summed, tile(r, j))
                    if what == "first":
                        nc.vector.tensor_scalar(degree[:, :], NODE[:, D:D + 1], 1.0, None, ALU.max).then_inc(degree_made, 1)
                        nc.vector.scalar_tensor_tensor(out=resid[:, :], in0=NODE[:, 0:D], scalar=0.0, in1=x_tile[:, :],
                                                       op0=ALU.max, op1=ALU.add).then_inc(resid_made, 1)
                        dve.wait_ge(degree_made, tile(r, j, [0]))
                        nc.vector.reciprocal(inv_deg[:, one], degree[:, :])
                    elif what == "attended":
                        nc.vector.tensor_scalar(denom[:, :], NODE[:, D:HIGH], 1e-6, None, ALU.add).then_inc(denom_made, 1)
                        dve.wait_ge(denom_made, tile(r, j, [r]))
                        nc.vector.reciprocal(inv_denom[:, :], denom[:, :]).then_inc(inv_denom_made, 1)
                        dve.wait_ge(inv_denom_made, tile(r, j, [r]))
                        nc.vector.tensor_tensor(blend[:, :].rearrange("p (h d) -> p h d", d=HD),
                                                NODE[:, 0:D].rearrange("p (h d) -> p h d", d=HD),
                                                inv_denom[:, :].unsqueeze(2).to_broadcast([P, HEADS, HD]),
                                                ALU.mult).then_inc(attended, 1)
                        dve.wait_ge(attended, tile(r, j, [r]))
                        nc.vector.tensor_tensor(resid[:, :], blend[:, :], xs_all[:, feats], ALU.add).then_inc(resid_made, 1)
                    else:
                        if what == "hidden":
                            nc.vector.tensor_scalar(averaged[:, :], NODE[:, D:2 * D], inv_deg[:, one], None,
                                                    ALU.mult).then_inc(averaged_made, 1)
                            dve.wait_ge(averaged_made, tile(r, j, BLENDED))
                            nc.vector.tensor_tensor(blend[:, :], averaged[:, :], NODE[:, 0:D], ALU.add).then_inc(blended, 1)
                            dve.wait_ge(blended, tile(r, j, HIDDEN))
                        else:
                            nc.vector.scalar_tensor_tensor(out=averaged[:, :], in0=NODE[:, D:2 * D], scalar=inv_deg[:, one],
                                                           in1=xs_all[:, feats], op0=ALU.mult,
                                                           op1=ALU.add).then_inc(averaged_made, 1)
                            dve.wait_ge(averaged_made, tile(r, j, BLENDED))
                            nc.vector.tensor_tensor(resid[:, :], averaged[:, :], NODE[:, 0:D], ALU.add).then_inc(resid_made, 1)
                    if r in NORMED:
                        dve.wait_ge(resid_made, tile(r, j, NORMED))
                        nc.vector.bn_stats(stats[:, :], resid[:, :]).then_inc(stats_made, 1)
                        dve.wait_ge(stats_made, tile(r, j, NORMED))
                        passed(dve)
                        nc.vector.bn_aggr(moments[:, :], stats[:, :]).then_inc(moments_made, 1)
                        dve.wait_ge(moments_made, tile(r, j, NORMED))

                def finish(j):
                    if r in NORMED:
                        dve.wait_ge(root_made, tile(r, j, NORMED))
                        nc.vector.reciprocal(rstd[:, :], root[:, :]).then_inc(rstd_made, 1)
                        dve.wait_ge(rstd_made, tile(r, j, NORMED))
                    if r:
                        dve.wait_ge(table_stored, stored_before(r, j))
                        if r in KEPT:
                            dve.wait_ge(node_kept, tile(r, j, KEPT, 1))
                        else:
                            dve.wait_ge(node_kept, TILES * len(KEPT) + CREDIT)
                    else:
                        dve.wait_ge(node_kept, tile(r, j, KEPT, 1))
                        dve.wait_ge(table_stored, 16 * j + 16)
                    if what == "project":
                        dve.wait_ge(new_turned, tile(r, j, [r], 1))
                    if what == "hidden":
                        nc.vector.tensor_scalar(new_tile[:, :], blend[:, :], 0.0, None, ALU.max).then_inc(node_made, 1)
                    else:
                        nc.vector.tensor_scalar(new_tile[:, :], resid[:, :], moments[:, 0:1], rstd[:, 0:1],
                                                ALU.subtract, ALU.mult).then_inc(node_made, 1)

                def split_q(j):
                    def step(ins, n):
                        ins.then_inc(q_part_made, 1)
                        dve.wait_ge(q_part_made, q_part(j, n))

                    q_all = kvq_tile[:, 2 * D:3 * D]
                    dve.wait_ge(kvq_made, tile(r, j, [r]))
                    dve.wait_ge(q_stored, j * 16 + 16)
                    step(nc.vector.tensor_copy(q_parts[:, 0, :], q_all), 0)
                    step(nc.vector.tensor_tensor(q_rest[:, 0, :], q_all, q_parts[:, 0, :], ALU.subtract), 1)
                    step(nc.vector.tensor_copy(q_parts[:, 1, :], q_rest[:, 0, :]), 2)
                    step(nc.vector.tensor_tensor(q_rest[:, 1, :], q_rest[:, 0, :], q_parts[:, 1, :], ALU.subtract), 3)
                    step(nc.vector.tensor_copy(q_parts[:, 2, :], q_rest[:, 1, :]), 4)

                def run(place, j, b):
                    if place == 2:
                        sums(j)
                    if place == 3:
                        finish(j)
                    if place == SLOTS and what == "project" and near:
                        split_q(j)
                return run

            def program(near):
                for r in range(len(ROUNDS)):
                    if r:
                        dve.wait_ge(acc_zeroed, TILES * r + CREDIT)
                    schedule(dve, r, near, groups(r, near), nodes(r, near))

            either(dve, program)

        @block.tensor
        def _(pe):
            start(pe, hidden_summed, weights_summed, group_summed, query_summed, wide_summed,
                  x_turned, node_summed, new_turned, kvq_summed)
            pe.wait_ge(prep, 12)
            nc.tensor.transpose(TURN[0:1, 0:P], worst[:, 3:4], ident).then_inc(worst_turned, 1)

            def groups(r, near):
                kind = ROUNDS[r][0]
                high = {GATED: D + 1, SAGE: D, ATTEND: HIGH}[kind]

                def edge_hidden(b, q):
                    pe.wait_ge(attr_landed[q], body(r, b, WEIGHTED) * 16)
                    pe.wait_ge(hidden_made, group(r, b, q, [0], 2))
                    nc.tensor.matmul(bank[q % 2][0:D, :], w_gate1[:, :], attr_n[q][:, :], start=True,
                                     stop=True).then_inc(hidden_summed, 1)

                def edge_weights(b, q):
                    if kind == GATED:
                        pe.wait_ge(hidden_made, group(r, b, q, [0]))
                        pe.wait_ge(msg_made, group(r, b, q, WEIGHTED, 2))
                        lhs, rhs, to = hidden[q % 2], w("gate2"), bank[2 + q % 2]
                    else:
                        pe.wait_ge(attr_landed[q], body(r, b, WEIGHTED) * 16)
                        pe.wait_ge(key_scaled, group(r, b, q, [r], 2))
                        lhs, rhs, to = attr_w[q], w("edge"), bank[q % 2]
                    for t in range(T):
                        mm = nc.tensor.matmul(to[:, t * D:(t + 1) * D], lhs[:, t * P:(t + 1) * P], rhs, start=True, stop=True)
                    mm.then_inc(weights_summed, 1)

                def edge_queries(b, q):
                    pe.wait_ge(onehot_t_made, group(r, b, q, [r]))
                    pe.wait_ge(q_win_landed[q], body(r, b, [r]) * 16)
                    pe.wait_ge(products_made, group(r, b, q, [r], 2))
                    for t in range(T):
                        for k in range(PARTS):
                            mm = nc.tensor.matmul(bank[2 + q % 2][:, t * D:(t + 1) * D], onehot_t[q % 2][:, t * P:(t + 1) * P],
                                                  q_win[q][:, k * D:(k + 1) * D], start=(k == 0), stop=(k == PARTS - 1))
                    mm.then_inc(query_summed, 1)

                def summed(q, t):
                    return rows[q][:, t * D:(t + 1) * D] if kind == SAGE else msg[q][:, t, 0:high]

                def have_messages(b, q):
                    if kind == SAGE:
                        pe.wait_ge(rows_landed[q], body(r, b) * (16 * T))
                    else:
                        pe.wait_ge(msg_made, group(r, b, q, WEIGHTED))

                def sum_group(b, q):
                    have_messages(b, q)
                    pe.wait_ge(onehot_made, group(r, b, q))
                    pe.wait_ge(group_added, group(r, b, q, back=2))
                    for t in range(T):
                        mm = nc.tensor.matmul(bank[4 + q % 2][0:high, 0:WIN], summed(q, t), onehot[q][:, t, :],
                                              start=(t == 0), stop=(t == T - 1))
                    mm.then_inc(group_summed, 1)

                def sum_wide(b, q):
                    have_messages(b, q)
                    passed(pe)
                    with pe.Fori(0, WIDES) as v:
                        pe.wait_ge(wide_hot_made, window(r, b, q, v))
                        pe.wait_ge(wide_added, window(r, b, q, v, 1))
                        for t in range(T):
                            mm = nc.tensor.matmul(bank[4][0:high, 0:WIDE], summed(q, t), wide_hot[:, t, :],
                                                  start=(t == 0), stop=(t == T - 1))
                        mm.then_inc(wide_summed, 1)
                    pe.wait_ge(wide_summed, window(r, b, q, WIDES - 1))
                    pe.sem_inc(group_summed, 1)

                def ahead(b, q):
                    if kind == GATED:
                        edge_hidden(b, q)
                    if kind == ATTEND:
                        edge_weights(b, q)
                        if near:
                            edge_queries(b, q)

                def run(b, node):
                    ahead(b, 0)
                    for q in per:
                        node(q)
                        if q + 1 < SLOTS:
                            ahead(b, q + 1)
                        if kind == GATED:
                            edge_weights(b, q)
                        if near and kind != SAGE and q:
                            sum_group(b, q - 1)
                        if near and kind == SAGE:
                            sum_group(b, q)
                        if not near:
                            sum_wide(b, q)
                    if near and kind != SAGE:
                        sum_group(b, SLOTS - 1)
                    node(SLOTS)
                return run

            def nodes(r, near):
                what = ROUNDS[r][1]

                def run(place, j, b):
                    if place == 1 and r in SELF:
                        pe.wait_ge(x_staged, tile(r, j, SELF))
                        nc.tensor.transpose(TURN[0:D, 0:P], x_tile[:, :], ident).then_inc(x_turned, 1)
                    if place == 2:
                        pe.wait_ge(acc_staged, tile(r, j))
                        pe.wait_ge(node_made, tile(r, j, back=1))
                        if what == "attended":
                            nc.tensor.transpose(NODE[:, 0:HIGH], acc_tile[:, :], ident[0:HIGH, 0:HIGH]).then_inc(node_summed, 1)
                            return
                        pe.wait_ge(x_turn_made, tile(r, j, SELF))
                        if what == "first":
                            nc.tensor.matmul(NODE[:, 0:D + 1], x_turn[:, :], w("self0", n=D + 1), start=True, stop=False)
                            nc.tensor.matmul(NODE[:, 0:D + 1], acc_tile[0:D + 1, :], w("neigh0", n=D + 1), start=False,
                                             stop=True).then_inc(node_summed, 1)
                        else:
                            if what == "project":
                                pe.wait_ge(kvq_made, tile(r, j, [r], 1))
                            own, neigh = ROUND_W[r]
                            nc.tensor.matmul(NODE[:, 0:D], x_turn[:, :], w(own), start=True, stop=True)
                            nc.tensor.matmul(NODE[:, D:2 * D], acc_tile[0:D, :], w(neigh, k=D), start=True,
                                             stop=True).then_inc(node_summed, 1)
                    if place == SLOTS and what == "project":
                        pe.wait_ge(node_made, tile(r, j))
                        pe.wait_ge(new_turn_made, tile(r, j, [r], 1))
                        nc.tensor.transpose(TURN[0:D, 0:P], new_tile[:, :], ident).then_inc(new_turned, 1)
                        pe.wait_ge(new_turn_made, tile(r, j, [r]))
                        for i, name in enumerate(("key", "value", "query")):
                            mm = nc.tensor.matmul(NODE[:, i * D:(i + 1) * D], new_turn[:, :], w(name), start=True, stop=True)
                        mm.then_inc(kvq_summed, 1)
                return run

            def program(near):
                for r in range(len(ROUNDS)):
                    schedule(pe, r, near, groups(r, near), nodes(r, near))

            either(pe, program)


KEPT = [r for r, (_, n) in enumerate(ROUNDS) if n != "output"]


def stored_before(r, j):
    if r in STORED:
        return j * 16 + (STORED.index(r) * TILES * 16 + 16)
    return STORED.index(r - 1) * TILES * 16 + TILES * 16 + 16


def kernel(**inputs):
    import numpy as np
    import concourse.bacc as _bacc
    from concourse.bass_utils import run_bass_kernel_spmd as _run

    v = {k: np.asarray(a) for k, a in inputs.items()}
    f = np.float32

    def by_tile(a, fill):
        a = np.concatenate([a, np.full(EP - E, fill, a.dtype)])
        a = a.reshape(GROUPS * T, P).T
        return np.ascontiguousarray(np.concatenate([a, a[:, :AHEAD * T]], axis=1))

    dst = np.concatenate([v["dst"], np.full(EP - E, N, v["dst"].dtype)])
    packed = np.zeros((D + 1, W_WIDTH), f)

    def put(name, matrix, bias=None):
        packed[0:D, W_COL[name]:W_COL[name] + D] = matrix
        if bias is not None:
            packed[D, W_COL[name]:W_COL[name] + D] = bias

    put("gate2", v["L0_gnn_W2"].T, v["L0_gnn_b2"])
    put("self0", v["L0_gnn_Ws"].T, v["L0_gnn_bs"])
    packed[D, W_COL["bias0"]:W_COL["bias0"] + D] = v["L0_gnn_bn"]
    put("neigh0", v["L0_gnn_Wn"].T)
    packed[D, W_COL["neigh0"] + D] = 1.0
    put("selfs1", v["L1_gnn_W_self1"], v["L1_gnn_b1"])
    put("neigh1", v["L1_gnn_W_neigh1"])
    put("selfs2", v["L1_gnn_W_self2"], v["L1_gnn_b2"])
    put("neigh2", v["L1_gnn_W_neigh2"])
    put("edge", v["L2_gnn_We"], v["L2_gnn_be"])
    put("key", v["L2_gnn_Wk"], v["L2_gnn_bk"])
    put("value", v["L2_gnn_Wv"], v["L2_gnn_bv"])
    put("query", v["L2_gnn_Wq"], v["L2_gnn_bq"])
    put("selfs4", v["L3_gnn_Wr1"].T, v["L3_gnn_bl1"])
    put("neigh4", v["L3_gnn_Wl1"].T)
    put("selfs5", v["L3_gnn_Wr2"].T, v["L3_gnn_bl2"])
    put("neigh5", v["L3_gnn_Wl2"].T)
    packed[0:D, W_WIDTH - 1] = v["L0_gnn_b1"]

    con = np.zeros((P, C_WIDTH), f)
    con[:, C_IDENT:C_IDENT + P] = np.eye(P, dtype=f)
    con[:, C_IOTA:C_IOTA + WIDE] = np.arange(WIDE, dtype=f)
    con[:, C_WIDE:C_WIDE + WIDES] = np.arange(WIDES, dtype=f) * WIDE
    con[:, C_LIMIT:C_LIMIT + BODIES] = (np.arange(BODIES, dtype=f) - (TILE_LAG - 1)) * P

    con[:, C_EPS] = EPS
    con[:, C_NODE] = np.arange(P, dtype=f)

    arrays = {
        "x": np.concatenate([v["x"], np.zeros((NP - N, D), f)]),
        "src": by_tile(v["src"], 0),
        "dst": by_tile(v["dst"], N),
        "dst_row": dst.reshape(1, EP),
        "base": np.ascontiguousarray(dst[::GE].reshape(1, GROUPS)),
        "attr17": np.ascontiguousarray(np.concatenate([v["edge_attr_17"].T, np.zeros((ATTR, EP - E), f)], axis=1)),
        "attr96": np.ascontiguousarray(np.concatenate([v["edge_attr_96"].T, np.zeros((D, EP - E), f)], axis=1)),
        "gate1": np.ascontiguousarray(v["L0_gnn_W1"].T),
        "weights": packed,
        "consts": con,
    }
    nc = _bacc.Bacc("TRN2", target_bir_lowering=False, num_devices=1)
    args = {n: nc.dram_tensor(f"in_{n}", a.shape, mybir.dt.from_np(a.dtype), kind="ExternalInput").ap()
            for n, a in arrays.items()}
    out = nc.dram_tensor("out_x", (N, D), F32, kind="ExternalOutput").ap()
    build(nc, out=out, **args)
    r = _run(nc, [{f"in_{n}": a for n, a in arrays.items()}], core_ids=[0])
    return r.results[0]["out_x"]
```

```python
import concourse.bass as bass
from concourse import mybir
from contextlib import ExitStack

F32 = mybir.dt.float32
BF16 = mybir.dt.bfloat16
I32 = mybir.dt.int32
ALU = mybir.AluOpType
ACT = mybir.ActivationFunctionType
AX = mybir.AxisListType

P = 128
D = 96
ATTR = 17
HEADS = 8
HD = D // HEADS
N = 6250
E = 106250
TILES = -(-N // P)
NP = TILES * P
T = 4
GE = T * P
SLOTS = 4
BODIES = -(-E // (GE * SLOTS))
GROUPS = BODIES * SLOTS
EP = GROUPS * GE
WIN = 64
WIDE = 448
WIDES = NP // WIDE
TILE_LAG = 5
AHEAD = 2
HIGH = D + HEADS
EPS = 1e-5
BLOCK = 16
BLOCKS = P // BLOCK
BT = 3
CODES = BLOCK * TILES
RING = 4
CHUNKS = 4
PIECES = BLOCKS
PIECE_K = [TILES * g // PIECES for g in range(PIECES + 1)]
PARTS = 3
CREDIT = 4

GATED, SAGE, ATTEND = "gated", "sage", "attend"
ROUNDS = [(GATED, "first"), (SAGE, "hidden"), (SAGE, "project"), (ATTEND, "attended"),
          (SAGE, "hidden"), (SAGE, "output")]
LAYER_SRC = {"first": "x", "hidden": "x", "project": "h", "output": "h"}
NORMED = [r for r, (_, n) in enumerate(ROUNDS) if n != "hidden"]
BLENDED = [r for r, (_, n) in enumerate(ROUNDS) if n in ("hidden", "project", "output")]
SUMMED = [2, 5]
HIDDEN = [r for r, (_, n) in enumerate(ROUNDS) if n == "hidden"]
WEIGHTED = [r for r, (k, _) in enumerate(ROUNDS) if k != SAGE]
BUILD = 1
LOADING = [2, 4, 5]
BEFORE = {1: 0, 2: 1, 4: 3, 5: 4}
CODE_STEPS = 5
SERVED = {0: 1, 1: 2, 3: 4, 4: 5}
RUNS = {
    True: dict(edge=WEIGHTED, own=[0], kept=[0, 2, 3], stored=[5], turned=[0, 1, 2, 3, 4]),
    False: dict(edge=list(range(6)), own=[r for r, (_, n) in enumerate(ROUNDS) if n != "attended"],
                kept=[0, 1, 2, 3, 4], stored=[0, 1, 3, 4, 5], turned=[2]),
}

W_NAMES = ["gate2", "self0", "bias0", "neigh0", "selfs1", "neigh1", "selfs2", "neigh2", "edge",
           "key", "value", "query", "selfs4", "neigh4", "selfs5", "neigh5"]
W_COL = {n: i * (D + 1) for i, n in enumerate(W_NAMES)}
W_WIDTH = len(W_NAMES) * (D + 1) + 1
ROUND_W = {1: ("selfs1", "neigh1"), 2: ("selfs2", "neigh2"), 4: ("selfs4", "neigh4"), 5: ("selfs5", "neigh5")}
C_IDENT, C_IOTA, C_WIDE, C_LIMIT = 0, P, P + WIDE, P + WIDE + WIDES
C_EPS = C_LIMIT + BODIES
C_NODE = C_EPS + 1
C_SHIFT = C_NODE + 1
C_CUM = C_SHIFT + TILES * BLOCKS
C_TRI = C_CUM + BLOCKS + 1
C_WIDTH = C_TRI + TILES


def build(nc, x, src, dst, dst_next, pairs, codes, dst_row, base, attr17, attr96, gate1, weights, consts, out):
    with ExitStack() as ctx:
        def sb(name, shape, dt=F32):
            return ctx.enter_context(nc.sbuf_tensor(name, shape, dt))

        def sem(name):
            return ctx.enter_context(nc.semaphore(name))

        table = {r: nc.dram_tensor(f"table{r}", (NP, D), F32).ap() for r in (0, 1, 3, 4)}
        table_kv = nc.dram_tensor("table_kv", (NP, 2 * D), F32).ap()
        table_q = nc.dram_tensor("table_q", (NP, D), F32).ap()
        table_qp = nc.dram_tensor("table_qp", (NP, PARTS * D), BF16).ap()
        matrix = nc.dram_tensor("matrix", (NP, NP), BF16).ap()
        block_starts = nc.dram_tensor("block_starts", (TILES, BLOCKS), I32).ap()
        gathered_from = {0: x, 1: table[0], 2: table[1], 3: table_kv, 4: table[3], 5: table[4]}
        stored_to = {**table, 5: out}

        y_a = sb("y_a", [P, TILES * PARTS * D], BF16)
        shared_y = sb("shared_y", [P, TILES * PARTS * D // 2])
        y_b = shared_y[:, :].bitcast(BF16)
        acc = shared_y[0:HIGH, 0:NP]
        y_of = {1: y_a, 2: y_b, 4: y_a, 5: y_b}
        xs_all = sb("x_all", [P, TILES * D])
        hs_all = sb("h_all", [P, TILES * D])
        own_all = hs_all
        inv_deg = sb("inv_deg", [P, TILES])
        src_idx = sb("src_idx", [P, (GROUPS + AHEAD) * T], I32)
        dst_idx = sb("dst_idx", [P, (GROUPS + AHEAD) * T], I32)
        dst_f = sb("dst_f", [P, GROUPS * T])
        rel = sb("rel", [P, GROUPS * T])
        base_int = sb("base_int", [P, GROUPS], I32)
        base_f = sb("base_f", [P, GROUPS])
        wts = sb("wts", [D + 1, W_WIDTH])
        w_gate1 = sb("w_gate1", [ATTR, D])
        con = sb("con", [P, C_WIDTH])
        zeros = sb("zeros", [P, P])
        worst = sb("worst", [P, 7])
        worst_row = sb("worst_row", [1, 2])
        near_flag = sb("near_flag", [1, 1], I32)
        per = range(SLOTS)
        shared_strip = [sb(f"shared_strip{i}", [P, TILES * P // 2]) for i in range(2)]
        strip = [t[:, :].bitcast(BF16) for t in shared_strip]
        staged = [sb(f"staged{q}", [P, T], I32) for q in per]
        staged_dst = [sb(f"staged_dst{q}", [P, T], I32) for q in per]
        rows = [sb(f"rows{q}", [P, T * 2 * D]) for q in per]
        msg = [sb(f"msg{q}", [P, T, HIGH]) for q in per]
        onehot = [sb(f"onehot{q}", [P, T, WIN]) for q in per]
        attr_n = [shared_strip[1][0:ATTR, q * GE:(q + 1) * GE] for q in per]
        attr_w = [sb(f"attr_w{q}", [D + 1, GE]) for q in per]
        q_win = [sb(f"q_win{q}", [WIN, PARTS * D], BF16) for q in per]
        dst_wide = [shared_strip[0][0:WIN, q * GE:(q + 1) * GE].bitcast(I32) for q in per]
        win_node = sb("win_node", [WIN, GROUPS])
        q_rows = sb("q_rows", [P, T * D])
        hidden = [sb(f"hidden{i}", [D + 1, GE]) for i in range(2)]
        onehot_t = [sb(f"onehot_t{i}", [WIN, GE], BF16) for i in range(2)]
        prod = sb("prod", [P, T, D])
        score = sb("score", [P, T, HEADS])
        capped = [sb(f"capped{i}", [P, T, HEADS]) for i in range(2)]
        wide_rel = sb("wide_rel", [P, T])
        ring_words = max(T * WIDE, RING * (CODES + P) // 2)
        shared_hot = sb("shared_hot", [P, ring_words])
        wide_hot = shared_hot[:, 0:T * WIDE].rearrange("p (t n) -> p t n", t=T)
        ring = shared_hot[:, :].bitcast(BF16)
        code_hot = [ring[:, i * CODES:(i + 1) * CODES] for i in range(RING)]
        low_hot = [ring[:, RING * CODES + i * P:RING * CODES + (i + 1) * P] for i in range(RING)]
        dst_next_idx = shared_hot[:, 0:GROUPS * T].bitcast(I32)
        code_iota = sb("code_iota", [P, CODES], mybir.dt.float16)
        deg_all = sb("deg_all", [P, TILES])
        before = sb("before", [TILES, BLOCKS + 1])
        tiles_before = sb("tiles_before", [TILES, 1])
        starts_f = sb("starts_f", [TILES, BLOCKS])
        starts_int = sb("starts_int", [TILES, BLOCKS], I32)
        starts_row = sb("starts_row", [1, TILES * BLOCKS], I32)
        pair = [sb(f"pair{i}", [P, BLOCKS * BT * 2], I32) for i in range(2)]
        high_int = sb("high_int", [P, BLOCKS * BT], I32)
        low_int = sb("low_int", [P, BLOCKS * BT], I32)
        code_raw = sb("code_raw", [P, BLOCKS * BT])
        code = [sb(f"code{i}", [P, BLOCKS * BT]) for i in range(2)]
        low = [sb(f"low{i}", [P, BLOCKS * BT]) for i in range(2)]
        folded_sum = sb("folded_sum", [P, D])
        y_tile = sb("y_tile", [P, D])
        y_rest = sb("y_rest", [P, D])
        acc_tile = sb("acc_tile", [HIGH, P])
        x_tile = sb("x_tile", [P, D])
        x_turn = sb("x_turn", [D + 1, P])
        new_turn = sb("new_turn", [D + 1, P])
        degree = sb("degree", [P, 1])
        averaged = sb("averaged", [P, D])
        blend = sb("blend", [P, D])
        resid = sb("resid", [P, D])
        stats = sb("stats", [P, 6])
        moments = sb("moments", [P, 2])
        root = sb("root", [P, 1])
        rstd = sb("rstd", [P, 1])
        denom = sb("denom", [P, HEADS])
        inv_denom = sb("inv_denom", [P, HEADS])
        new_tile = sb("new_tile", [P, D])
        kvq_tile = sb("kvq_tile", [P, 3 * D])
        q_rest = sb("q_rest", [P, 2, D])
        q_parts = sb("q_parts", [P, PARTS, D], BF16)

        bank = [ctx.enter_context(nc.psum_tensor(f"bank{i}", [P, 512], F32)) for i in range(8)]
        PRODUCT = [bank[4], bank[5]]
        TURN, NODE = bank[6], bank[7]

        loaded = sem("loaded"); x_landed = sem("x_landed"); cleared = sem("cleared")
        prep = sem("prep"); worst_turned = sem("worst_turned"); ready = sem("ready")
        rows_landed = [sem(f"rows_landed{q}") for q in per]
        q_rows_landed = sem("q_rows_landed")
        attr_landed = [sem(f"attr_landed{q}") for q in per]
        q_win_landed = [sem(f"q_win_landed{q}") for q in per]
        idx_staged = sem("idx_staged")
        waits_passed = {e.engine: sem(f"waits_passed_{n}") for n, e in (("pe", nc.tensor), ("act", nc.scalar), ("dve", nc.vector), ("pool", nc.gpsimd))}
        onehot_made = sem("onehot_made"); hidden_summed = sem("hidden_summed"); hidden_made = sem("hidden_made")
        weights_summed = sem("weights_summed"); msg_made = sem("msg_made")
        group_summed = sem("group_summed"); group_added = sem("group_added")
        onehot_t_made = sem("onehot_t_made")
        dst_wide_landed = [sem(f"dst_wide_landed{q}") for q in per]; q_part_made = sem("q_part_made")
        query_summed = sem("query_summed"); key_scaled = sem("key_scaled"); products_made = sem("products_made")
        score_summed = sem("score_summed"); score_low = sem("score_low"); capped_made = sem("capped_made")
        exp_made = sem("exp_made")
        wide_rel_made = sem("wide_rel_made"); wide_hot_made = sem("wide_hot_made")
        wide_summed = sem("wide_summed"); wide_added = sem("wide_added")
        acc_staged = sem("acc_staged"); acc_zeroed = sem("acc_zeroed"); x_staged = sem("x_staged")
        x_turned = sem("x_turned"); x_turn_made = sem("x_turn_made"); node_summed = sem("node_summed")
        degree_made = sem("degree_made"); averaged_made = sem("averaged_made"); blended = sem("blended"); resid_made = sem("resid_made")
        stats_made = sem("stats_made"); moments_made = sem("moments_made"); root_made = sem("root_made"); rstd_made = sem("rstd_made")
        denom_made = sem("denom_made"); inv_denom_made = sem("inv_denom_made"); attended = sem("attended")
        node_made = sem("node_made"); node_kept = sem("node_kept"); table_stored = sem("table_stored")
        new_turned = sem("new_turned"); new_turn_made = sem("new_turn_made")
        kvq_summed = sem("kvq_summed"); kvq_made = sem("kvq_made")
        degrees_turned = sem("degrees_turned"); starts_made = sem("starts_made"); starts_stored = sem("starts_stored")
        starts_landed = sem("starts_landed"); pair_landed = [sem(f"pair_landed{i}") for i in range(2)]
        code_step = sem("code_step"); hot_made = sem("hot_made"); hot_summed = sem("hot_summed")
        block_kept = sem("block_kept"); strip_stored = [sem(f"strip_stored{i}") for i in range(2)]
        chunk_landed = [[sem(f"chunk_landed{i}_{c}") for c in range(CHUNKS)] for i in range(2)]
        chunk_summed = sem("chunk_summed"); folded = sem("folded"); acc_cleared = sem("acc_cleared")
        served_summed = sem("served_summed"); served_kept = sem("served_kept"); y_part_made = sem("y_part_made")
        kv_stored = sem("kv_stored"); q_stored = sem("q_stored")

        ident = con[:, C_IDENT:C_IDENT + P]

        def w(name, k=D + 1, n=D):
            return wts[0:k, W_COL[name]:W_COL[name] + n]

        plan = {}

        def group(r, b, q, of=None, back=0):
            k = (of or plan["edge"]).index(r)
            return b * SLOTS + (k * GROUPS + q + 1 + CREDIT - back)

        def tile(r, j, of=None, back=0):
            k = r if of is None else of.index(r)
            return j + (k * TILES + 1 + CREDIT - back)

        def body(r, b, of=None, back=0):
            k = (of or plan["edge"]).index(r)
            return b + (k * BODIES + 1 - back)

        def block_of(j, g):
            return j * BLOCKS + (g + 1 + CREDIT)

        def hot_of(j, g, i, back=0):
            return j * (BLOCKS * BT) + (g * BT + i + 1 + CREDIT - back)

        def chunk_of(r, j, c=CHUNKS - 1):
            return j * CHUNKS + (BLENDED.index(r) * TILES * CHUNKS + c + 1)

        def loads_of(r, p, half):
            return half * 16 + (LOADING.index(r) * ((TILES + 1 - p) // 2) + 1) * 16

        def y_step(r, j, n):
            return j * 4 + (list(SERVED).index(r) * TILES * 4 + CREDIT + 1 + n)

        def q_part(j, step):
            return j * 5 + (CREDIT + 1 + step)

        def window(r, b, q, v, back=0):
            return b * (SLOTS * WIDES) + v + ((r * GROUPS + q) * WIDES + 1 + CREDIT - back)

        def start(eng, *sems):
            for s in sems:
                eng.sem_inc(s, CREDIT)

        def passed(eng):
            eng.sem_inc(waits_passed[eng.engine], 1)

        def schedule(eng, r, near, groups, nodes, served):
            if near:
                def places(j, b):
                    def run(place):
                        if not isinstance(j, int) or j:
                            served(place, j - 1)
                        nodes(place, j, b)
                    return run

                with eng.Fori(0, TILE_LAG) as b:
                    groups(b, lambda place: None)
                with eng.Fori(TILE_LAG, TILE_LAG + 1) as b:
                    groups(b, lambda place: nodes(place, b - TILE_LAG, b))
                with eng.Fori(TILE_LAG + 1, BODIES) as b:
                    groups(b, places(b - TILE_LAG, b))
                for j in range(BODIES - TILE_LAG, TILES):
                    for place in range(SLOTS + 1):
                        places(j, BODIES)(place)
                for place in range(SLOTS + 1):
                    served(place, TILES - 1)
            else:
                def whole(j):
                    for place in range(SLOTS + 1):
                        nodes(place, j, BODIES)
                    for place in range(SLOTS + 1):
                        served(place, j)

                with eng.Fori(0, BODIES) as b:
                    groups(b, lambda place: None)
                with eng.Fori(0, TILES - 1) as j:
                    whole(j)
                whole(TILES - 1)

        def dense(eng, r, step):
            lag = 1 if r == BUILD else 0

            def at(s, parity, half):
                def j(back):
                    if isinstance(s, int) and not 0 <= s - back < TILES:
                        return None
                    n = s - back if isinstance(s, int) else half * 2 + (parity - back)
                    return n, (parity - back) % 2, half + (parity - back) // 2
                step(j, lag)

            for s in range(4):
                at(s, s % 2, s // 2)
            with eng.Fori(2, TILES // 2) as half:
                for parity in range(2):
                    at(half * 2 + parity, parity, half)
            for s in range(TILES - TILES % 2, TILES + lag + 2):
                at(s, s % 2, s // 2)

        def window_starts(eng, b):
            _, starts = nc.values_load_multi_w_load_instructions(
                base_int[0:1, bass.ds(b * SLOTS, SLOTS)], engines=[eng.engine], min_val=0, max_val=NP - WIN)
            return starts

        def either(eng, program):
            eng.wait_ge(ready, 1)
            near = eng.value_load(near_flag[0:1, 0:1], min_val=0, max_val=1)
            with eng.If(near):
                plan.update(RUNS[True])
                program(True)
            with eng.Else():
                plan.update(RUNS[False])
                program(False)

        block = ctx.enter_context(nc.Block())

        @block.sync
        def _(sp):
            sp.dma_start(dst_idx[:, :], dst).then_inc(loaded, 16)
            sp.dma_start(base_int[:, :], base.partition_broadcast(P)).then_inc(loaded, 16)
            sp.dma_start(con[:, :], consts).then_inc(loaded, 16)
            sp.dma_start(dst_next_idx, dst_next).then_inc(loaded, 16)
            sp.dma_start(code_iota[:, :], codes).then_inc(loaded, 16)
            sp.dma_start(src_idx[:, :], src).then_inc(loaded, 16)
            sp.dma_start(wts[:, :], weights).then_inc(loaded, 16)
            sp.dma_start(w_gate1[:, :], gate1).then_inc(loaded, 16)
            sp.dma_start(xs_all[:, :].rearrange("p (j d) -> p j d", d=D),
                         x.rearrange("(j p) d -> p j d", p=P)).then_inc(x_landed, 16)

            last_use = {2: (chunk_summed, chunk_of(1, TILES - 1)), 4: (onehot_t_made, GROUPS + CREDIT),
                        5: (chunk_summed, chunk_of(4, TILES - 1))}

            def find_starts():
                sp.wait_ge(starts_made, 3)
                sp.dma_start(block_starts, starts_int[:, :]).then_inc(starts_stored, 16)
                sp.wait_ge(starts_stored, 16)
                sp.dma_start(starts_row[:, :], block_starts.rearrange("(o j) b -> o (j b)", o=1)).then_inc(starts_landed, 16)
                sp.wait_ge(starts_landed, 16)

            def build(j, lag):
                if j(0):
                    n, p, half = j(0)
                    if not isinstance(n, int) or n >= 2:
                        sp.wait_ge(code_step, n * CODE_STEPS + (CREDIT - CODE_STEPS))
                    for g in range(0, BLOCKS, 4):
                        _, four = nc.values_load_multi_w_load_instructions(
                            starts_row[0:1, slice(n * BLOCKS + g, n * BLOCKS + g + 4) if isinstance(n, int) else bass.ds(n * BLOCKS + g, 4)],
                            engines=[sp.engine], min_val=0, max_val=2 * EP)
                        for i in range(4):
                            sp.dma_start(pair[p][:, (g + i) * 2 * BT:(g + i + 1) * 2 * BT],
                                         pairs[0:1, bass.ds(four[i], 2 * BT * P)].rearrange("o (p c) -> (o p) c", p=P)).then_inc(pair_landed[p], 16)
                if j(2):
                    store(*j(2))

            def store(n, p, half):
                sp.wait_ge(block_kept, block_of(n, BLOCKS - 1))
                rows_at = slice(n * P, (n + 1) * P) if isinstance(n, int) else bass.ds(n * P, P)
                sp.dma_start(matrix[rows_at, :], strip[p][:, 0:NP]).then_inc(strip_stored[p], 16)

            def load(r):
                def step(j, lag):
                    if not j(0):
                        return
                    n, p, half = j(0)
                    rows_at = slice(n * P, (n + 1) * P) if isinstance(n, int) else bass.ds(n * P, P)
                    for c in range(CHUNKS):
                        if isinstance(n, int) and n < 2:
                            sp.wait_ge(*last_use[r])
                        else:
                            sp.wait_ge(chunk_summed, chunk_of(r, n, c) - 2 * CHUNKS)
                        cols = slice(PIECE_K[2 * c] * P, PIECE_K[2 * c + 2] * P)
                        sp.dma_start(strip[p][:, cols], matrix[rows_at, cols]).then_inc(chunk_landed[p][c], 16)
                return step

            def program(near):
                for r, (kind, _) in enumerate(ROUNDS):
                    if kind == SAGE:
                        if near and r == BUILD:
                            find_starts()
                            dense(sp, r, build)
                            for p in range(2):
                                sp.wait_ge(strip_stored[p], 16 * ((TILES + 1 - p) // 2))
                        elif near:
                            dense(sp, r, load(r))
                        continue
                    if kind == ATTEND:
                        sp.wait_ge(q_stored, 16 * TILES + 16)
                    with sp.Fori(0, BODIES) as b:
                        starts = window_starts(sp, b) if kind == ATTEND and near else None
                        for q in per:
                            if kind == GATED:
                                sp.wait_ge(hidden_summed, group(r, b, q, [0], SLOTS))
                                sp.dma_start(attr_n[q][:, :], attr17[:, bass.ds((b * SLOTS + q) * GE, GE)]).then_inc(attr_landed[q], 16)
                            else:
                                sp.wait_ge(weights_summed, group(r, b, q, WEIGHTED, SLOTS))
                                sp.dma_start(attr_w[q][0:D, :], attr96[:, bass.ds((b * SLOTS + q) * GE, GE)]).then_inc(attr_landed[q], 16)
                                if near:
                                    sp.wait_ge(onehot_t_made, group(r, b, q, [r], SLOTS))
                                    sp.dma_start(dst_wide[q][:, :], dst_row[:, bass.ds((b * SLOTS + q) * GE, GE)].partition_broadcast(WIN)).then_inc(dst_wide_landed[q], 16)
                                    sp.wait_ge(query_summed, group(r, b, q, [r], SLOTS))
                                    sp.dma_start(q_win[q][:, :], table_qp[bass.ds(starts[q], WIN), :]).then_inc(q_win_landed[q], 16)
                sp.wait_ge(table_stored, 16 * TILES * len(plan["stored"]) + 16)

            either(sp, program)

        @block.gpsimd
        def _(pool):
            def program(near):
                for r in plan["edge"]:
                    kind = ROUNDS[r][0]
                    if kind == ATTEND and near:
                        pool.wait_ge(chunk_summed, chunk_of(r - 1, TILES - 1))
                        nc.gpsimd.memset(acc[:, :], 0.0).then_inc(acc_cleared, 1)
                    if kind == ATTEND:
                        pool.wait_ge(kv_stored, 16 * TILES + 16)
                        pool.wait_ge(q_stored, 16 * TILES + 16)
                    elif r:
                        pool.wait_ge(table_stored, 16 * TILES * (plan["stored"].index(r - 1) + 1) + 16)
                    width = 2 * D if kind == ATTEND else D
                    with pool.Fori(0, BODIES) as b:
                        for q in per:
                            pool.wait_ge(idx_staged, group(r, b, q))
                            passed(pool)
                            for t in range(T):
                                pool.indirect_dma_start(
                                    out=rows[q][:, t * width:(t + 1) * width], out_offset=None, in_=gathered_from[r],
                                    in_offset=bass.IndirectOffsetOnAxis(ap=staged[q][:, t:t + 1], axis=0),
                                ).then_inc(rows_landed[q], 16)
                            if kind == ATTEND and not near:
                                pool.wait_ge(products_made, group(r, b, q, [r], 1))
                                passed(pool)
                                for t in range(T):
                                    pool.indirect_dma_start(
                                        out=q_rows[:, t * D:(t + 1) * D], out_offset=None, in_=table_q,
                                        in_offset=bass.IndirectOffsetOnAxis(ap=staged_dst[q][:, t:t + 1], axis=0),
                                    ).then_inc(q_rows_landed, 16)

            either(pool, program)

        @block.scalar
        def _(act):
            start(act, idx_staged, exp_made, acc_staged, acc_zeroed, x_staged,
                  x_turn_made, root_made, node_kept, new_turn_made, kvq_made, block_kept, served_kept)
            for s in (table_stored, kv_stored, q_stored):
                act.sem_inc(s, 16)

            def at(j, size):
                return slice(j * size, (j + 1) * size) if isinstance(j, int) else bass.ds(j * size, size)

            def deviation(r, j):
                if r in NORMED:
                    act.wait_ge(moments_made, tile(r, j, NORMED))
                    act.wait_ge(node_made, tile(r, j, back=1))
                    nc.scalar.activation(root[:, :], moments[:, 1:2], ACT.Sqrt, bias=con[:, C_EPS:C_EPS + 1]).then_inc(root_made, 1)

            def keep(r, j, near):
                what = ROUNDS[r][1]
                act.wait_ge(node_made, tile(r, j))
                if r in plan["kept"]:
                    passed(act)
                    kept = hs_all if what == "hidden" else xs_all
                    nc.scalar.copy(kept[:, at(j, D)], new_tile[:, :]).then_inc(node_kept, 1)
                if r in plan["stored"]:
                    k = N - j * P if isinstance(j, int) and what == "output" and j == TILES - 1 else P
                    act.dma_start(stored_to[r][slice(j * P, j * P + k) if isinstance(j, int) else bass.ds(j * P, k), :],
                                  new_tile[0:k, :]).then_inc(table_stored, 16)

            def turn(r, j):
                act.wait_ge(new_turned, tile(r, j, plan["turned"]))
                nc.scalar.copy(new_turn[0:D, :], TURN[0:D, 0:P]).then_inc(new_turn_made, 1)

            def serve(r, j, near):
                if r in SERVED:
                    act.wait_ge(served_summed, tile(r, j, list(SERVED)))
                    act.wait_ge(y_part_made, y_step(r, j, -1))
                    passed(act)
                    nc.scalar.copy(own_all[:, at(j, D)], NODE[:, 0:D])
                    nc.scalar.copy(y_tile[:, :], NODE[:, D:2 * D]).then_inc(served_kept, 1)
                    return
                act.wait_ge(kvq_summed, tile(r, j, [r]))
                act.wait_ge(kv_stored, 16 * j + 16)
                act.wait_ge(q_stored, 16 * j + 16)
                nc.scalar.copy(kvq_tile[:, 0:2 * D], NODE[:, 0:2 * D])
                nc.scalar.mul(kvq_tile[:, 2 * D:3 * D], NODE[:, 2 * D:3 * D], float(HD) ** -0.5).then_inc(kvq_made, 1)
                act.wait_ge(kvq_made, tile(r, j, [r]))
                act.dma_start(table_kv[at(j, P), :], kvq_tile[:, 0:2 * D]).then_inc(kv_stored, 16)
                if not near:
                    act.dma_start(table_q[at(j, P), :], kvq_tile[:, 2 * D:3 * D]).then_inc(q_stored, 16)

            def store_q(j):
                act.wait_ge(q_part_made, q_part(j, 4))
                act.dma_start(table_qp[at(j, P), :], q_parts[:, :, :].rearrange("p k d -> p (k d)")).then_inc(q_stored, 16)

            def served(r, near):
                def run(place, j):
                    if r in plan["turned"] and place == 0:
                        turn(r, j)
                    if r in plan["turned"] and place == 1:
                        serve(r, j, near)
                return run

            def strips(r):
                def step(j, lag):
                    for g in range(BLOCKS):
                        done, ready_tile = j(lag + 1), j(lag + 2)
                        if g == 1 and ready_tile and r in plan["turned"]:
                            turn(r, ready_tile[0])
                        if g == 3 and done:
                            deviation(r, done[0])
                        if g == 4 and ready_tile and r in plan["turned"]:
                            serve(r, ready_tile[0], True)
                        if g == 6 and done:
                            keep(r, done[0], True)
                        if r == BUILD and j(0):
                            n, p, half = j(0)
                            if g == 0:
                                if not isinstance(n, int) or n >= 2:
                                    act.wait_ge(chunk_summed, chunk_of(r, n) - 2 * CHUNKS)
                                    act.wait_ge(strip_stored[p], half * 16)
                            act.wait_ge(hot_summed, hot_of(n, g, BT - 1))
                            to = strip[p].rearrange("p (k d) -> p k d", d=P)
                            for h in range(2):
                                ins = nc.scalar.copy(to[:, :, g * BLOCK + h * BLOCK // 2:g * BLOCK + (h + 1) * BLOCK // 2],
                                                     bank[2 * (g % 2) + h][:, 0:CODES // 2].rearrange("p (d k) -> p k d", k=TILES))
                            ins.then_inc(block_kept, 1)
                    if r == 2 and j(lag + 2):
                        store_q(j(lag + 2)[0])
                return step

            def groups(r, near):
                kind = ROUNDS[r][0]

                def run(b, node):
                    for q in per:
                        node(q)
                        n = q + AHEAD
                        act.wait_ge(group_summed, group(r, b, n, back=SLOTS))
                        passed(act)
                        cols = bass.ds((b * SLOTS + n) * T, T)
                        if not near:
                            nc.scalar.copy(staged_dst[n % SLOTS][:, :], dst_idx[:, cols])
                        nc.scalar.copy(staged[n % SLOTS][:, :], src_idx[:, cols]).then_inc(idx_staged, 1)
                        if kind == ATTEND:
                            act.wait_ge(capped_made, group(r, b, q, [r]))
                            act.wait_ge(group_summed, group(r, b, q, back=SLOTS))
                            nc.scalar.activation(msg[q][:, :, D:HIGH], capped[q % 2][:, :, :], ACT.Exp).then_inc(exp_made, 1)
                    node(SLOTS)
                return run

            def nodes(r, near):
                what = ROUNDS[r][1]
                operand = hs_all if LAYER_SRC.get(what) == "h" else xs_all

                def run(place, j, b):
                    cols = slice(j * P, (j + 1) * P) if isinstance(j, int) else bass.ds(j * P, P)
                    feats = slice(j * D, (j + 1) * D) if isinstance(j, int) else bass.ds(j * D, D)
                    if place == 0:
                        act.wait_ge(group_added, group(r, b, 0, back=1))
                        act.wait_ge(node_made, tile(r, j, back=1))
                        passed(act)
                        nc.scalar.copy(acc_tile[:, :], acc[:, cols]).then_inc(acc_staged, 1)
                        if r in plan["own"]:
                            nc.scalar.copy(x_tile[:, :], operand[:, feats]).then_inc(x_staged, 1)
                    if place == 1 and not near:
                        act.wait_ge(acc_staged, tile(r, j, plan["edge"]))
                        passed(act)
                        nc.scalar.copy(acc[:, cols], zeros[0:HIGH, :]).then_inc(acc_zeroed, 1)
                    if place == 1 and r in plan["own"]:
                        act.wait_ge(x_turned, tile(r, j, plan["own"]))
                        nc.scalar.copy(x_turn[0:D, :], TURN[0:D, 0:P]).then_inc(x_turn_made, 1)
                    if place == 3:
                        deviation(r, j)
                    if place == SLOTS:
                        keep(r, j, near)
                return run

            def program(near):
                for q in range(AHEAD):
                    if not near:
                        nc.scalar.copy(staged_dst[q][:, :], dst_idx[:, q * T:(q + 1) * T])
                    nc.scalar.copy(staged[q][:, :], src_idx[:, q * T:(q + 1) * T]).then_inc(idx_staged, 1)
                act.wait_ge(x_landed, 16)
                for r in range(len(ROUNDS)):
                    if r in plan["edge"]:
                        schedule(act, r, near, groups(r, near), nodes(r, near), served(r, near))
                    else:
                        dense(act, r, strips(r))

            either(act, program)

        @block.vector
        def _(dve):
            start(dve, hidden_made, onehot_t_made, q_part_made, onehot_made, msg_made, group_added, key_scaled, products_made, score_summed, score_low,
                  capped_made, wide_rel_made, wide_hot_made, wide_added, degree_made, averaged_made, blended, resid_made, stats_made,
                  moments_made, rstd_made, denom_made, inv_denom_made, attended, node_made,
                  code_step, hot_made, folded, y_part_made)
            nc.vector.memset(zeros[:, :], 0.0)
            nc.vector.memset(x_turn[D:D + 1, :], 1.0)
            nc.vector.memset(new_turn[D:D + 1, :], 1.0)
            for i in range(2):
                nc.vector.memset(hidden[i][D:D + 1, :], 1.0)
            for q in per:
                nc.vector.memset(attr_w[q][D:D + 1, :], 1.0)
                nc.vector.memset(msg[q][:, :, D:D + 1], 1.0)
            nc.vector.memset(worst[:, 6:7], 0.0).then_inc(cleared, 1)
            dve.wait_ge(cleared, 1)

            steps = [0]

            def then(ins):
                steps[0] += 1
                ins.then_inc(prep, 1)
                dve.wait_ge(prep, steps[0])

            dve.wait_ge(loaded, 16 * 8)
            then(nc.vector.tensor_copy(base_f[:, :], base_int[:, :]))
            then(nc.vector.tensor_scalar(base_f[:, :], base_f[:, :], float(NP - WIN), None, ALU.min))
            then(nc.vector.tensor_copy(base_int[:, :], base_f[:, :]))
            then(nc.vector.tensor_scalar(win_node[:, :], base_f[0:WIN, :], con[0:WIN, C_NODE:C_NODE + 1], None, ALU.add))
            then(nc.vector.tensor_copy(dst_f[:, :], dst_idx[:, 0:GROUPS * T]))
            by_body = [P, BODIES, SLOTS * T]
            then(nc.vector.tensor_tensor(rel[:, :].rearrange("p (b t) -> p b t", t=SLOTS * T),
                                         dst_f[:, :].rearrange("p (b t) -> p b t", t=SLOTS * T),
                                         con[:, C_LIMIT:C_LIMIT + BODIES].unsqueeze(2).to_broadcast(by_body), ALU.subtract))
            then(nc.vector.tensor_reduce(worst[:, 0:1], rel[:, :], AX.X, ALU.min))
            then(nc.vector.tensor_tensor(rel[:, :].rearrange("p (g t) -> p g t", t=T),
                                         dst_f[:, :].rearrange("p (g t) -> p g t", t=T),
                                         base_f[:, :].unsqueeze(2).to_broadcast([P, GROUPS, T]), ALU.subtract))
            then(nc.vector.tensor_reduce(worst[:, 1:2], rel[:, :], AX.X, ALU.min))
            then(nc.vector.tensor_reduce(worst[:, 2:3], rel[:, :], AX.X, ALU.max))
            then(nc.vector.tensor_scalar(worst[:, 2:3], worst[:, 2:3], -1.0, float(WIN - 1), ALU.mult, ALU.add))
            ordered = shared_y[:, 0:GROUPS * T]
            then(nc.vector.tensor_tensor(ordered, dst_next_idx, dst_f[:, :], ALU.subtract))
            then(nc.vector.tensor_reduce(worst[:, 3:4], ordered, AX.X, ALU.min))
            for k, (tiles, least) in enumerate(((BT, BLOCK), (2, 1))):
                span = GROUPS * T - tiles
                then(nc.vector.tensor_tensor(ordered[:, 0:span], dst_f[:, tiles:], dst_f[:, 0:span], ALU.subtract))
                then(nc.vector.tensor_reduce(worst[:, 4 + k:5 + k], ordered[:, 0:span], AX.X, ALU.min))
                then(nc.vector.tensor_scalar(worst[:, 4 + k:5 + k], worst[:, 4 + k:5 + k], float(-least), None, ALU.add))
            then(nc.vector.tensor_reduce(worst[:, 6:7], worst[:, 0:6], AX.X, ALU.min))
            then(nc.vector.memset(acc[:, :], 0.0))
            then(nc.vector.tensor_tensor(w("self0"), w("self0"), w("bias0"), ALU.add))
            dve.wait_ge(worst_turned, 1)
            then(nc.vector.tensor_reduce(worst_row[:, 0:1], TURN[0:1, 0:P], AX.X, ALU.min))
            then(nc.vector.tensor_scalar(worst_row[:, 1:2], worst_row[:, 0:1], 0.0, None, ALU.is_ge))
            nc.vector.tensor_copy(near_flag[:, :], worst_row[:, 1:2]).then_inc(ready, 1)

            iota = con[:, C_IOTA:C_IOTA + WIDE]

            def groups(r, near):
                kind = ROUNDS[r][0]
                high = {GATED: D + 1, SAGE: D, ATTEND: HIGH}[kind]

                def hot(b, q):
                    dve.wait_ge(group_summed, group(r, b, q, back=SLOTS))
                    nc.vector.tensor_tensor(
                        onehot[q][:, :, :], iota[:, 0:WIN].unsqueeze(1).to_broadcast([P, T, WIN]),
                        rel[:, bass.ds((b * SLOTS + q) * T, T)].unsqueeze(2).to_broadcast([P, T, WIN]),
                        ALU.is_equal).then_inc(onehot_made, 1)

                def hide(b, q):
                    dve.wait_ge(hidden_summed, group(r, b, q, [0]))
                    dve.wait_ge(weights_summed, group(r, b, q, WEIGHTED, 2))
                    nc.vector.tensor_scalar(hidden[q % 2][0:D, :], bank[q % 2][0:D, :], wts[0:D, W_WIDTH - 1:W_WIDTH],
                                            0.0, ALU.add, ALU.max).then_inc(hidden_made, 1)

                def hot_t(b, q):
                    dve.wait_ge(dst_wide_landed[q], body(r, b, [r]) * 16)
                    dve.wait_ge(query_summed, group(r, b, q, [r], 2))
                    nc.vector.tensor_scalar(onehot_t[q % 2][:, :], dst_wide[q][:, :], win_node[:, bass.ds(b * SLOTS + q, 1)],
                                            None, ALU.is_equal).then_inc(onehot_t_made, 1)

                def gate(b, q):
                    dve.wait_ge(weights_summed, group(r, b, q, WEIGHTED))
                    dve.wait_ge(rows_landed[q], body(r, b) * (16 * T))
                    dve.wait_ge(group_summed, group(r, b, q, back=SLOTS))
                    nc.vector.tensor_tensor(msg[q][:, :, 0:D], bank[2 + q % 2][:, 0:T * D].rearrange("p (t d) -> p t d", d=D),
                                            rows[q][:, 0:T * D].rearrange("p (t d) -> p t d", d=D),
                                            ALU.mult).then_inc(msg_made, 1)

                def attend_scores(b, q):
                    kv = rows[q][:, :].rearrange("p (t d) -> p t d", d=2 * D)
                    dve.wait_ge(weights_summed, group(r, b, q, WEIGHTED))
                    dve.wait_ge(rows_landed[q], body(r, b) * (16 * T))
                    nc.vector.tensor_tensor(prod[:, :, :], bank[q % 2][:, 0:T * D].rearrange("p (t d) -> p t d", d=D),
                                            kv[:, :, 0:D], ALU.mult).then_inc(key_scaled, 1)
                    if near:
                        queries = bank[2 + q % 2][:, 0:T * D]
                        dve.wait_ge(query_summed, group(r, b, q, [r]))
                    else:
                        queries = q_rows[:, :]
                        dve.wait_ge(q_rows_landed, (b * SLOTS + q + 1) * (16 * T))
                    dve.wait_ge(key_scaled, group(r, b, q, [r]))
                    nc.vector.tensor_tensor(prod[:, :, :], prod[:, :, :], queries.rearrange("p (t d) -> p t d", d=D),
                                            ALU.mult).then_inc(products_made, 1)
                    dve.wait_ge(products_made, group(r, b, q, [r]))
                    nc.vector.tensor_reduce(score[:, :, :], prod[:, :, :].rearrange("p t (h d) -> p t h d", d=HD),
                                            AX.X, ALU.add).then_inc(score_summed, 1)
                    dve.wait_ge(score_summed, group(r, b, q, [r]))
                    nc.vector.tensor_scalar(capped[q % 2][:, :, :], score[:, :, :], 5.0, -5.0, ALU.min,
                                            ALU.max).then_inc(capped_made, 1)

                def attend_values(b, q):
                    kv = rows[q][:, :].rearrange("p (t d) -> p t d", d=2 * D)
                    dve.wait_ge(exp_made, group(r, b, q, [r]))
                    nc.vector.tensor_tensor(
                        msg[q][:, :, 0:D].rearrange("p t (h d) -> p t h d", d=HD),
                        kv[:, :, D:2 * D].rearrange("p t (h d) -> p t h d", d=HD),
                        msg[q][:, :, D:HIGH].unsqueeze(3).to_broadcast([P, T, HEADS, HD]), ALU.mult).then_inc(msg_made, 1)

                def add(b, q, starts):
                    dve.wait_ge(group_summed, group(r, b, q))
                    dve.wait_ge(group_added, group(r, b, q, back=1))
                    at = acc[0:high, bass.ds(starts[q], WIN)]
                    nc.vector.tensor_tensor(at, at, bank[4 + q % 2][0:high, 0:WIN], ALU.add).then_inc(group_added, 1)

                def add_wide(b, q):
                    with dve.Fori(0, WIDES) as v:
                        dve.wait_ge(wide_summed, window(r, b, q, v, 1))
                        nc.vector.tensor_scalar(wide_rel[:, :], dst_f[:, bass.ds((b * SLOTS + q) * T, T)],
                                                con[:, bass.ds(v + C_WIDE, 1)], None, ALU.subtract).then_inc(wide_rel_made, 1)
                        dve.wait_ge(wide_rel_made, window(r, b, q, v))
                        nc.vector.tensor_tensor(wide_hot[:, :, :], iota.unsqueeze(1).to_broadcast([P, T, WIDE]),
                                                wide_rel[:, :].unsqueeze(2).to_broadcast([P, T, WIDE]),
                                                ALU.is_equal).then_inc(wide_hot_made, 1)
                        dve.wait_ge(wide_summed, window(r, b, q, v))
                        dve.wait_ge(wide_added, window(r, b, q, v, 1))
                        at = acc[0:high, bass.ds(v * WIDE, WIDE)]
                        nc.vector.tensor_tensor(at, at, bank[4][0:high, 0:WIDE], ALU.add).then_inc(wide_added, 1)
                    dve.wait_ge(wide_added, window(r, b, q, WIDES - 1))
                    dve.sem_inc(group_added, 1)

                def run(b, node):
                    starts = window_starts(dve, b) if near else None
                    def ahead(q):
                        if near and kind == ATTEND:
                            hot_t(b, q)
                        if kind == GATED:
                            hide(b, q)
                        if near:
                            hot(b, q)

                    ahead(0)
                    for q in per:
                        if q + 1 < SLOTS:
                            ahead(q + 1)
                        if kind == GATED:
                            gate(b, q)
                        if kind == ATTEND:
                            attend_scores(b, q)
                        if kind == ATTEND and near and q:
                            attend_values(b, q - 1)
                        behind = 2 if kind == ATTEND else 1
                        if near and q >= behind:
                            add(b, q - behind, starts)
                        if not near:
                            if kind == ATTEND:
                                attend_values(b, q)
                            add_wide(b, q)
                        node(q)
                    if near:
                        if kind == ATTEND:
                            attend_values(b, SLOTS - 1)
                            add(b, SLOTS - 2, starts)
                        add(b, SLOTS - 1, starts)
                    node(SLOTS)
                return run

            def nodes(r, near):
                what = ROUNDS[r][1]

                def sums(j, parity=None):
                    one = slice(j, j + 1) if isinstance(j, int) else bass.ds(j, 1)
                    feats = slice(j * D, (j + 1) * D) if isinstance(j, int) else bass.ds(j * D, D)
                    if r in plan["edge"]:
                        dve.wait_ge(node_summed, tile(r, j, plan["edge"]))
                    else:
                        dve.wait_ge(chunk_summed, chunk_of(r, j))
                        nc.vector.tensor_reduce(folded_sum[:, :], PRODUCT[parity][:, 0:PARTS * D].rearrange("p (k d) -> p d k", k=PARTS),
                                                AX.X, ALU.add).then_inc(folded, 1)
                        dve.wait_ge(folded, tile(r, j, BLENDED))
                        if what == "hidden":
                            nc.vector.scalar_tensor_tensor(out=blend[:, :], in0=folded_sum[:, :], scalar=inv_deg[:, one],
                                                           in1=own_all[:, feats], op0=ALU.mult, op1=ALU.add).then_inc(blended, 1)
                            dve.wait_ge(blended, tile(r, j, HIDDEN))
                            return
                        nc.vector.scalar_tensor_tensor(out=averaged[:, :], in0=folded_sum[:, :], scalar=inv_deg[:, one],
                                                       in1=xs_all[:, feats], op0=ALU.mult, op1=ALU.add).then_inc(averaged_made, 1)
                        dve.wait_ge(averaged_made, tile(r, j, SUMMED if near else BLENDED))
                        nc.vector.tensor_tensor(resid[:, :], averaged[:, :], own_all[:, feats], ALU.add).then_inc(resid_made, 1)
                        moments_of(j)
                        return
                    if what == "first":
                        if near:
                            nc.vector.tensor_copy(deg_all[:, one], NODE[:, D:D + 1])
                        nc.vector.tensor_scalar(degree[:, :], NODE[:, D:D + 1], 1.0, None, ALU.max).then_inc(degree_made, 1)
                        nc.vector.scalar_tensor_tensor(out=resid[:, :], in0=NODE[:, 0:D], scalar=0.0, in1=x_tile[:, :],
                                                       op0=ALU.max, op1=ALU.add).then_inc(resid_made, 1)
                        dve.wait_ge(degree_made, tile(r, j, [0]))
                        nc.vector.reciprocal(inv_deg[:, one], degree[:, :])
                    elif what == "attended":
                        nc.vector.tensor_scalar(denom[:, :], NODE[:, D:HIGH], 1e-6, None, ALU.add).then_inc(denom_made, 1)
                        dve.wait_ge(denom_made, tile(r, j, [r]))
                        nc.vector.reciprocal(inv_denom[:, :], denom[:, :]).then_inc(inv_denom_made, 1)
                        dve.wait_ge(inv_denom_made, tile(r, j, [r]))
                        nc.vector.tensor_tensor(blend[:, :].rearrange("p (h d) -> p h d", d=HD),
                                                NODE[:, 0:D].rearrange("p (h d) -> p h d", d=HD),
                                                inv_denom[:, :].unsqueeze(2).to_broadcast([P, HEADS, HD]),
                                                ALU.mult).then_inc(attended, 1)
                        dve.wait_ge(attended, tile(r, j, [r]))
                        nc.vector.tensor_tensor(resid[:, :], blend[:, :], xs_all[:, feats], ALU.add).then_inc(resid_made, 1)
                    else:
                        if what == "hidden":
                            nc.vector.tensor_scalar(averaged[:, :], NODE[:, D:2 * D], inv_deg[:, one], None,
                                                    ALU.mult).then_inc(averaged_made, 1)
                            dve.wait_ge(averaged_made, tile(r, j, BLENDED))
                            nc.vector.tensor_tensor(blend[:, :], averaged[:, :], NODE[:, 0:D], ALU.add).then_inc(blended, 1)
                            dve.wait_ge(blended, tile(r, j, HIDDEN))
                        else:
                            nc.vector.scalar_tensor_tensor(out=averaged[:, :], in0=NODE[:, D:2 * D], scalar=inv_deg[:, one],
                                                           in1=xs_all[:, feats], op0=ALU.mult,
                                                           op1=ALU.add).then_inc(averaged_made, 1)
                            dve.wait_ge(averaged_made, tile(r, j, BLENDED))
                            nc.vector.tensor_tensor(resid[:, :], averaged[:, :], NODE[:, 0:D], ALU.add).then_inc(resid_made, 1)
                    moments_of(j)

                def moments_of(j):
                    if r in NORMED:
                        dve.wait_ge(resid_made, tile(r, j, NORMED))
                        nc.vector.bn_stats(stats[:, :], resid[:, :]).then_inc(stats_made, 1)
                        dve.wait_ge(stats_made, tile(r, j, NORMED))
                        passed(dve)
                        nc.vector.bn_aggr(moments[:, :], stats[:, :]).then_inc(moments_made, 1)
                        dve.wait_ge(moments_made, tile(r, j, NORMED))

                def finish(j):
                    if r in NORMED:
                        dve.wait_ge(root_made, tile(r, j, NORMED))
                        nc.vector.reciprocal(rstd[:, :], root[:, :]).then_inc(rstd_made, 1)
                        dve.wait_ge(rstd_made, tile(r, j, NORMED))
                    stored_now = stored_before(plan["stored"], r, j)
                    dve.wait_ge(table_stored, stored_now)
                    dve.wait_ge(node_kept, kept_before(plan["kept"], r, j))
                    if r in plan["turned"]:
                        dve.wait_ge(new_turned, tile(r, j, plan["turned"], 1))
                    elif near:
                        dve.wait_ge(new_turned, TILES * len(plan["turned"]) + CREDIT)
                    if what == "hidden":
                        nc.vector.tensor_scalar(new_tile[:, :], blend[:, :], 0.0, None, ALU.max).then_inc(node_made, 1)
                    else:
                        nc.vector.tensor_scalar(new_tile[:, :], resid[:, :], moments[:, 0:1], rstd[:, 0:1],
                                                ALU.subtract, ALU.mult).then_inc(node_made, 1)

                def split_q(j):
                    def step(ins, n):
                        ins.then_inc(q_part_made, 1)
                        dve.wait_ge(q_part_made, q_part(j, n))

                    q_all = kvq_tile[:, 2 * D:3 * D]
                    dve.wait_ge(kvq_made, tile(r, j, [r]))
                    dve.wait_ge(q_stored, j * 16 + 16)
                    step(nc.vector.tensor_copy(q_parts[:, 0, :], q_all), 0)
                    step(nc.vector.tensor_tensor(q_rest[:, 0, :], q_all, q_parts[:, 0, :], ALU.subtract), 1)
                    step(nc.vector.tensor_copy(q_parts[:, 1, :], q_rest[:, 0, :]), 2)
                    step(nc.vector.tensor_tensor(q_rest[:, 1, :], q_rest[:, 0, :], q_parts[:, 1, :], ALU.subtract), 3)
                    step(nc.vector.tensor_copy(q_parts[:, 2, :], q_rest[:, 1, :]), 4)

                def split_y(j):
                    def step(ins, n):
                        ins.then_inc(y_part_made, 1)
                        dve.wait_ge(y_part_made, y_step(r, j, n))

                    y = y_of[SERVED[r]]
                    part = [y[:, slice((j * PARTS + k) * D, (j * PARTS + k + 1) * D) if isinstance(j, int)
                              else bass.ds(j * (PARTS * D) + k * D, D)] for k in range(PARTS)]
                    dve.wait_ge(served_kept, tile(r, j, list(SERVED)))
                    step(nc.vector.tensor_copy(part[0], y_tile[:, :]), 0)
                    step(nc.vector.tensor_tensor(y_rest[:, :], y_tile[:, :], part[0], ALU.subtract), 1)
                    step(nc.vector.tensor_copy(part[1], y_rest[:, :]), 2)
                    step(nc.vector.tensor_tensor(part[2], y_rest[:, :], part[1], ALU.subtract), 3)

                def served(j):
                    if what == "project":
                        split_q(j)
                    elif r in SERVED:
                        split_y(j)

                def run(place, j, b):
                    if place == 2:
                        sums(j)
                    if place == 3:
                        finish(j)

                run.sums, run.finish, run.served = sums, finish, served
                return run

            def find_starts():
                def then_start(ins, n):
                    ins.then_inc(starts_made, 1)
                    dve.wait_ge(starts_made, n)

                dve.wait_ge(degrees_turned, 1)
                nc.vector.tensor_copy(before[:, :], TURN[0:TILES, 0:BLOCKS + 1]).then_inc(starts_made, 1)
                dve.wait_ge(degrees_turned, 2)
                nc.vector.tensor_copy(tiles_before[:, :], TURN[0:TILES, 0:1]).then_inc(starts_made, 1)
                dve.wait_ge(starts_made, 2)
                nc.vector.tensor_scalar(starts_int[:, :], before[:, 0:BLOCKS], tiles_before[:, 0:1], 2.0, ALU.add,
                                        ALU.mult).then_inc(starts_made, 1)

            def code_edges(n, p, half):
                count = [0]

                def step(ins):
                    count[0] += 1
                    ins.then_inc(code_step, 1)
                    dve.wait_ge(code_step, n * CODE_STEPS + (CREDIT + count[0]))

                edges = pair[p][:, :].rearrange("p (e c) -> p e c", c=2)
                shift = slice(C_SHIFT + n * BLOCKS, C_SHIFT + (n + 1) * BLOCKS) if isinstance(n, int) else bass.ds(n * BLOCKS + C_SHIFT, BLOCKS)
                dve.wait_ge(pair_landed[p], half * (16 * BLOCKS) + 16 * BLOCKS)
                step(nc.vector.tensor_scalar(high_int[:, :], edges[:, :, 0], 7, None, ALU.arith_shift_right))
                step(nc.vector.tensor_scalar(low_int[:, :], edges[:, :, 0], P - 1, None, ALU.bitwise_and))
                step(nc.vector.tensor_copy(low[p][:, :], low_int[:, :]))
                step(nc.vector.scalar_tensor_tensor(out=code_raw[:, :], in0=edges[:, :, 1], scalar=float(TILES), in1=high_int[:, :],
                                                    op0=ALU.mult, op1=ALU.add))
                step(nc.vector.tensor_tensor(code[p][:, :].rearrange("p (g i) -> p g i", i=BT),
                                             code_raw[:, :].rearrange("p (g i) -> p g i", i=BT),
                                             con[:, shift].unsqueeze(2).to_broadcast([P, BLOCKS, BT]), ALU.subtract))

            def strips(r):
                node = nodes(r, True)

                def step(j, lag):
                    if r == BUILD and j(0):
                        code_edges(*j(0))
                    for g in range(BLOCKS):
                        done, ready_tile = j(lag + 1), j(lag + 2)
                        if g == 0 and done:
                            node.sums(done[0], done[1])
                        if g == 4 and done:
                            node.finish(done[0])
                        if g == 6 and ready_tile:
                            node.served(ready_tile[0])
                        if r == BUILD and j(0):
                            n, p, half = j(0)
                            for i in range(BT):
                                slot, e = (g * BT + i) % RING, g * BT + i
                                dve.wait_ge(hot_summed, hot_of(n, g, i, RING))
                                nc.vector.tensor_scalar(low_hot[slot], con[:, C_IOTA:C_IOTA + P], low[p][:, e:e + 1], None, ALU.is_equal)
                                nc.vector.tensor_scalar(code_hot[slot], code_iota[:, :], code[p][:, e:e + 1], None,
                                                        ALU.is_equal).then_inc(hot_made, 1)
                return step

            def program(near):
                for r in range(len(ROUNDS)):
                    if near and r == BUILD:
                        find_starts()
                    if r not in plan["edge"]:
                        dense(dve, r, strips(r))
                        continue
                    if near:
                        if r:
                            dve.wait_ge(acc_cleared, 1)
                    elif r:
                        dve.wait_ge(acc_zeroed, TILES * r + CREDIT)
                    node = nodes(r, near)
                    schedule(dve, r, near, groups(r, near), node,
                             lambda place, j: node.served(j) if near and place == 3 else None)

            either(dve, program)

        @block.tensor
        def _(pe):
            start(pe, hidden_summed, weights_summed, group_summed, query_summed, wide_summed,
                  x_turned, node_summed, new_turned, kvq_summed, hot_summed, served_summed)
            pe.wait_ge(prep, 22)
            nc.tensor.transpose(TURN[0:1, 0:P], worst[:, 6:7], ident).then_inc(worst_turned, 1)

            def groups(r, near):
                kind = ROUNDS[r][0]
                high = {GATED: D + 1, SAGE: D, ATTEND: HIGH}[kind]

                def edge_hidden(b, q):
                    pe.wait_ge(attr_landed[q], body(r, b, WEIGHTED) * 16)
                    pe.wait_ge(hidden_made, group(r, b, q, [0], 2))
                    nc.tensor.matmul(bank[q % 2][0:D, :], w_gate1[:, :], attr_n[q][:, :], start=True,
                                     stop=True).then_inc(hidden_summed, 1)

                def edge_weights(b, q):
                    if kind == GATED:
                        pe.wait_ge(hidden_made, group(r, b, q, [0]))
                        pe.wait_ge(msg_made, group(r, b, q, WEIGHTED, 2))
                        lhs, rhs, to = hidden[q % 2], w("gate2"), bank[2 + q % 2]
                    else:
                        pe.wait_ge(attr_landed[q], body(r, b, WEIGHTED) * 16)
                        pe.wait_ge(key_scaled, group(r, b, q, [r], 2))
                        lhs, rhs, to = attr_w[q], w("edge"), bank[q % 2]
                    for t in range(T):
                        mm = nc.tensor.matmul(to[:, t * D:(t + 1) * D], lhs[:, t * P:(t + 1) * P], rhs, start=True, stop=True)
                    mm.then_inc(weights_summed, 1)

                def edge_queries(b, q):
                    pe.wait_ge(onehot_t_made, group(r, b, q, [r]))
                    pe.wait_ge(q_win_landed[q], body(r, b, [r]) * 16)
                    pe.wait_ge(products_made, group(r, b, q, [r], 2))
                    for t in range(T):
                        for k in range(PARTS):
                            mm = nc.tensor.matmul(bank[2 + q % 2][:, t * D:(t + 1) * D], onehot_t[q % 2][:, t * P:(t + 1) * P],
                                                  q_win[q][:, k * D:(k + 1) * D], start=(k == 0), stop=(k == PARTS - 1))
                    mm.then_inc(query_summed, 1)

                def summed(q, t):
                    return rows[q][:, t * D:(t + 1) * D] if kind == SAGE else msg[q][:, t, 0:high]

                def have_messages(b, q):
                    if kind == SAGE:
                        pe.wait_ge(rows_landed[q], body(r, b) * (16 * T))
                    else:
                        pe.wait_ge(msg_made, group(r, b, q, WEIGHTED))

                def sum_group(b, q):
                    have_messages(b, q)
                    pe.wait_ge(onehot_made, group(r, b, q))
                    pe.wait_ge(group_added, group(r, b, q, back=2))
                    for t in range(T):
                        mm = nc.tensor.matmul(bank[4 + q % 2][0:high, 0:WIN], summed(q, t), onehot[q][:, t, :],
                                              start=(t == 0), stop=(t == T - 1))
                    mm.then_inc(group_summed, 1)

                def sum_wide(b, q):
                    have_messages(b, q)
                    passed(pe)
                    with pe.Fori(0, WIDES) as v:
                        pe.wait_ge(wide_hot_made, window(r, b, q, v))
                        pe.wait_ge(wide_added, window(r, b, q, v, 1))
                        for t in range(T):
                            mm = nc.tensor.matmul(bank[4][0:high, 0:WIDE], summed(q, t), wide_hot[:, t, :],
                                                  start=(t == 0), stop=(t == T - 1))
                        mm.then_inc(wide_summed, 1)
                    pe.wait_ge(wide_summed, window(r, b, q, WIDES - 1))
                    pe.sem_inc(group_summed, 1)

                def ahead(b, q):
                    if kind == GATED:
                        edge_hidden(b, q)
                    if kind == ATTEND:
                        edge_weights(b, q)
                        if near:
                            edge_queries(b, q)

                def run(b, node):
                    ahead(b, 0)
                    for q in per:
                        node(q)
                        if q + 1 < SLOTS:
                            ahead(b, q + 1)
                        if kind == GATED:
                            edge_weights(b, q)
                        if near and kind != SAGE and q:
                            sum_group(b, q - 1)
                        if near and kind == SAGE:
                            sum_group(b, q)
                        if not near:
                            sum_wide(b, q)
                    if near and kind != SAGE:
                        sum_group(b, SLOTS - 1)
                    node(SLOTS)
                return run

            def nodes(r, near):
                what = ROUNDS[r][1]

                def run(place, j, b):
                    if place == 1 and r in plan["own"]:
                        pe.wait_ge(x_staged, tile(r, j, plan["own"]))
                        nc.tensor.transpose(TURN[0:D, 0:P], x_tile[:, :], ident).then_inc(x_turned, 1)
                    if place == 2:
                        pe.wait_ge(acc_staged, tile(r, j, plan["edge"]))
                        pe.wait_ge(node_made, tile(r, j, back=1))
                        if near and r in SERVED:
                            pe.wait_ge(served_kept, tile(r, j, list(SERVED), 1))
                        if what == "attended":
                            nc.tensor.transpose(NODE[:, 0:HIGH], acc_tile[:, :], ident[0:HIGH, 0:HIGH]).then_inc(node_summed, 1)
                            return
                        pe.wait_ge(x_turn_made, tile(r, j, plan["own"]))
                        if what == "first":
                            nc.tensor.matmul(NODE[:, 0:D + 1], x_turn[:, :], w("self0", n=D + 1), start=True, stop=False)
                            nc.tensor.matmul(NODE[:, 0:D + 1], acc_tile[0:D + 1, :], w("neigh0", n=D + 1), start=False,
                                             stop=True).then_inc(node_summed, 1)
                        else:
                            if what == "project":
                                pe.wait_ge(kvq_made, tile(r, j, [r], 1))
                            own, neigh = ROUND_W[r]
                            nc.tensor.matmul(NODE[:, 0:D], x_turn[:, :], w(own), start=True, stop=True)
                            nc.tensor.matmul(NODE[:, D:2 * D], acc_tile[0:D, :], w(neigh, k=D), start=True,
                                             stop=True).then_inc(node_summed, 1)
                return run

            def served(r, near):
                def run(place, j):
                    if r in plan["turned"] and place == 0:
                        turn(r, j)
                    if r in plan["turned"] and place == 1:
                        serve(r, j)
                return run

            def turn(r, j):
                pe.wait_ge(node_made, tile(r, j))
                pe.wait_ge(new_turn_made, tile(r, j, plan["turned"], 1))
                nc.tensor.transpose(TURN[0:D, 0:P], new_tile[:, :], ident).then_inc(new_turned, 1)

            def serve(r, j):
                pe.wait_ge(new_turn_made, tile(r, j, plan["turned"]))
                if r in SERVED:
                    pe.wait_ge(served_kept, tile(r, j, list(SERVED), 1))
                    own, neigh = ROUND_W[SERVED[r]]
                    nc.tensor.matmul(NODE[:, 0:D], new_turn[:, :], w(own), start=True, stop=True)
                    nc.tensor.matmul(NODE[:, D:2 * D], new_turn[:, :], w(neigh), start=True, stop=True).then_inc(served_summed, 1)
                    return
                pe.wait_ge(kvq_made, tile(r, j, [r], 1))
                for i, name in enumerate(("key", "value", "query")):
                    mm = nc.tensor.matmul(NODE[:, i * D:(i + 1) * D], new_turn[:, :], w(name), start=True, stop=True)
                mm.then_inc(kvq_summed, 1)

            def find_starts():
                pe.wait_ge(degree_made, TILES + CREDIT)
                nc.tensor.matmul(TURN[0:TILES, 0:BLOCKS + 1], deg_all[:, :], con[:, C_CUM:C_CUM + BLOCKS + 1], start=True,
                                 stop=True).then_inc(degrees_turned, 1)
                pe.wait_ge(starts_made, 1)
                nc.tensor.matmul(TURN[0:TILES, 0:1], con[0:TILES, C_TRI:C_TRI + TILES], before[:, BLOCKS:BLOCKS + 1], start=True,
                                 stop=True).then_inc(degrees_turned, 1)

            def strips(r):
                def build_block(n, p, g):
                    pe.wait_ge(block_kept, block_of(n, g) - 2)
                    for i in range(BT):
                        slot = (g * BT + i) % RING
                        pe.wait_ge(hot_made, hot_of(n, g, i))
                        for h in range(2):
                            mm = nc.tensor.matmul(bank[2 * (g % 2) + h][:, 0:CODES // 2], low_hot[slot],
                                                  code_hot[slot][:, h * CODES // 2:(h + 1) * CODES // 2], start=(i == 0), stop=(i == BT - 1))
                        mm.then_inc(hot_summed, 1)

                def multiply(n, p, half, piece):
                    if piece == 0:
                        if isinstance(n, int) and n == 0:
                            pe.wait_ge(y_part_made, y_step(BEFORE[r], TILES - 1, 3))
                        pe.wait_ge(folded, tile(r, n, BLENDED, 2))
                        if r == BUILD:
                            pe.wait_ge(block_kept, block_of(n, BLOCKS - 1))
                    if r != BUILD and piece % 2 == 0:
                        pe.wait_ge(chunk_landed[p][piece // 2], loads_of(r, p, half))
                    for k in range(PIECE_K[piece], PIECE_K[piece + 1]):
                        mm = nc.tensor.matmul(PRODUCT[p][:, 0:PARTS * D], strip[p][:, k * P:(k + 1) * P],
                                              y_of[r][:, k * PARTS * D:(k + 1) * PARTS * D], start=(k == 0), stop=(k == TILES - 1))
                    if piece % 2:
                        mm.then_inc(chunk_summed, 1)

                def step(j, lag):
                    ready_tile = j(lag + 2) if r in plan["turned"] else None
                    for g in range(PIECES):
                        if r == BUILD and j(0):
                            build_block(j(0)[0], j(0)[1], g)
                        if g == 0 and ready_tile:
                            turn(r, ready_tile[0])
                        if g == 3 and ready_tile:
                            serve(r, ready_tile[0])
                        if j(lag):
                            multiply(*j(lag), g)
                return step

            def program(near):
                for r in range(len(ROUNDS)):
                    if near and r == BUILD:
                        find_starts()
                    if r in plan["edge"]:
                        schedule(pe, r, near, groups(r, near), nodes(r, near), served(r, near))
                    else:
                        dense(pe, r, strips(r))

            either(pe, program)


def before_tile(of, r, j):
    whole = len([k for k in of if k < r]) * TILES
    return j + whole if r in of else whole


def stored_before(of, r, j):
    n = before_tile(of, r, j)
    return n * 16 + 16


def kept_before(of, r, j):
    return before_tile(of, r, j) + CREDIT


def kernel(**inputs):
    import numpy as np
    import concourse.bacc as _bacc
    from concourse.bass_utils import run_bass_kernel_spmd as _run

    v = {k: np.asarray(a) for k, a in inputs.items()}
    f = np.float32

    def by_tile(a, fill):
        a = np.concatenate([a, np.full(EP - E, fill, a.dtype)])
        a = a.reshape(GROUPS * T, P).T
        return np.ascontiguousarray(np.concatenate([a, a[:, :AHEAD * T]], axis=1))

    dst = np.concatenate([v["dst"], np.full(EP - E, NP - 1, v["dst"].dtype)])
    packed = np.zeros((D + 1, W_WIDTH), f)

    def put(name, matrix, bias=None):
        packed[0:D, W_COL[name]:W_COL[name] + D] = matrix
        if bias is not None:
            packed[D, W_COL[name]:W_COL[name] + D] = bias

    put("gate2", v["L0_gnn_W2"].T, v["L0_gnn_b2"])
    put("self0", v["L0_gnn_Ws"].T, v["L0_gnn_bs"])
    packed[D, W_COL["bias0"]:W_COL["bias0"] + D] = v["L0_gnn_bn"]
    put("neigh0", v["L0_gnn_Wn"].T)
    packed[D, W_COL["neigh0"] + D] = 1.0
    put("selfs1", v["L1_gnn_W_self1"], v["L1_gnn_b1"])
    put("neigh1", v["L1_gnn_W_neigh1"])
    put("selfs2", v["L1_gnn_W_self2"], v["L1_gnn_b2"])
    put("neigh2", v["L1_gnn_W_neigh2"])
    put("edge", v["L2_gnn_We"], v["L2_gnn_be"])
    put("key", v["L2_gnn_Wk"], v["L2_gnn_bk"])
    put("value", v["L2_gnn_Wv"], v["L2_gnn_bv"])
    put("query", v["L2_gnn_Wq"], v["L2_gnn_bq"])
    put("selfs4", v["L3_gnn_Wr1"].T, v["L3_gnn_bl1"])
    put("neigh4", v["L3_gnn_Wl1"].T)
    put("selfs5", v["L3_gnn_Wr2"].T, v["L3_gnn_bl2"])
    put("neigh5", v["L3_gnn_Wl2"].T)
    packed[0:D, W_WIDTH - 1] = v["L0_gnn_b1"]

    con = np.zeros((P, C_WIDTH), f)
    con[:, C_IDENT:C_IDENT + P] = np.eye(P, dtype=f)
    con[:, C_IOTA:C_IOTA + WIDE] = np.arange(WIDE, dtype=f)
    con[:, C_WIDE:C_WIDE + WIDES] = np.arange(WIDES, dtype=f) * WIDE
    con[:, C_LIMIT:C_LIMIT + BODIES] = (np.arange(BODIES, dtype=f) - (TILE_LAG - 1)) * P

    con[:, C_EPS] = EPS
    con[:, C_NODE] = np.arange(P, dtype=f)

    con[:, C_SHIFT:C_SHIFT + TILES * BLOCKS] = np.arange(TILES * BLOCKS, dtype=f) * CODES
    con[:, C_CUM:C_CUM + BLOCKS] = np.arange(P)[:, None] < np.arange(BLOCKS)[None, :] * BLOCK
    con[:, C_CUM + BLOCKS] = 1.0
    con[0:TILES, C_TRI:C_TRI + TILES] = np.arange(TILES)[:, None] < np.arange(TILES)[None, :]
    pairs = np.zeros((EP + BT * P, 2), v["dst"].dtype)
    pairs[:, 1] = 2 * NP
    pairs[:E, 0] = v["src"]
    pairs[:EP, 1] = dst

    arrays = {
        "x": np.concatenate([v["x"], np.zeros((NP - N, D), f)]),
        "src": by_tile(v["src"], 0),
        "dst": by_tile(v["dst"], NP - 1),
        "dst_next": np.ascontiguousarray(np.append(dst[1:], dst[-1]).reshape(GROUPS * T, P).T),
        "pairs": pairs.reshape(1, -1),
        "codes": np.tile(np.arange(CODES, dtype=np.float16), (P, 1)),
        "dst_row": dst.reshape(1, EP),
        "base": np.ascontiguousarray(dst[::GE].reshape(1, GROUPS)),
        "attr17": np.ascontiguousarray(np.concatenate([v["edge_attr_17"].T, np.zeros((ATTR, EP - E), f)], axis=1)),
        "attr96": np.ascontiguousarray(np.concatenate([v["edge_attr_96"].T, np.zeros((D, EP - E), f)], axis=1)),
        "gate1": np.ascontiguousarray(v["L0_gnn_W1"].T),
        "weights": packed,
        "consts": con,
    }
    nc = _bacc.Bacc("TRN2", target_bir_lowering=False, num_devices=1)
    args = {n: nc.dram_tensor(f"in_{n}", a.shape, mybir.dt.from_np(a.dtype), kind="ExternalInput").ap()
            for n, a in arrays.items()}
    out = nc.dram_tensor("out_x", (N, D), F32, kind="ExternalOutput").ap()
    build(nc, out=out, **args)
    r = _run(nc, [{f"in_{n}": a for n, a in arrays.items()}], core_ids=[0])
    return r.results[0]["out_x"]
```

```python
import concourse.bass as bass
from concourse import mybir
from contextlib import ExitStack

F32 = mybir.dt.float32
BF16 = mybir.dt.bfloat16
I32 = mybir.dt.int32
ALU = mybir.AluOpType
ACT = mybir.ActivationFunctionType
AX = mybir.AxisListType

P = 128
D = 96
ATTR = 17
HEADS = 8
HD = D // HEADS
N = 6250
E = 106250
TILES = -(-N // P)
NP = TILES * P
T = 4
GE = T * P
SLOTS = 4
BODIES = -(-E // (GE * SLOTS))
GROUPS = BODIES * SLOTS
EP = GROUPS * GE
WIN = 48
WIDE = 448
WIDES = NP // WIDE
TILE_LAG = 5
OVERLAP = 2
AHEAD = 2
HIGH = D + HEADS
EPS = 1e-5
BLOCK = 8
BLOCKS = P // BLOCK
BT = 2
CODES = BLOCK * TILES
RING = 8
CHUNKS = 4
PIECES = 8
PER_PIECE = BLOCKS // PIECES
PIECE_K = [TILES * g // PIECES for g in range(PIECES + 1)]
PARTS = 3
CREDIT = 4

GATED, SAGE, ATTEND = "gated", "sage", "attend"
ROUNDS = [(GATED, "first"), (SAGE, "hidden"), (SAGE, "project"), (ATTEND, "attended"),
          (SAGE, "hidden"), (SAGE, "output")]
LAYER_SRC = {"first": "x", "hidden": "x", "project": "h", "output": "h"}
NORMED = [r for r, (_, n) in enumerate(ROUNDS) if n != "hidden"]
BLENDED = [r for r, (_, n) in enumerate(ROUNDS) if n in ("hidden", "project", "output")]
SUMMED = [2, 5]
HIDDEN = [r for r, (_, n) in enumerate(ROUNDS) if n == "hidden"]
WEIGHTED = [r for r, (k, _) in enumerate(ROUNDS) if k != SAGE]
BUILD = 1
LOADING = [2, 4, 5]
BEFORE = {1: 0, 2: 1, 4: 3, 5: 4}
Y_AT = {5: [0], 6: [1], 7: [2, 3]}
TURN_AT = {0: 2, 2: 1, 3: 1}
CODE_STEPS = 5
SERVED = {0: 1, 1: 2, 3: 4, 4: 5}
RUNS = {
    True: dict(edge=WEIGHTED, own=[0], kept=[0, 2, 3], stored=[5], turned=[0, 1, 2, 3, 4]),
    False: dict(edge=list(range(6)), own=[r for r, (_, n) in enumerate(ROUNDS) if n != "attended"],
                kept=[0, 1, 2, 3, 4], stored=[0, 1, 3, 4, 5], turned=[2]),
}

W_NAMES = ["gate2", "self0", "bias0", "neigh0", "selfs1", "neigh1", "selfs2", "neigh2", "edge",
           "key", "value", "query", "selfs4", "neigh4", "selfs5", "neigh5"]
W_COL = {n: i * (D + 1) for i, n in enumerate(W_NAMES)}
W_WIDTH = len(W_NAMES) * (D + 1) + 1
ROUND_W = {1: ("selfs1", "neigh1"), 2: ("selfs2", "neigh2"), 4: ("selfs4", "neigh4"), 5: ("selfs5", "neigh5")}
C_IDENT, C_IOTA, C_WIDE, C_LIMIT = 0, P, P + WIDE, P + WIDE + WIDES
C_EPS = C_LIMIT + GROUPS
C_NODE = C_EPS + 1
C_SHIFT = C_NODE + 1
C_CUM = C_SHIFT + TILES * BLOCKS
C_TRI = C_CUM + BLOCKS + 1
C_WIDTH = C_TRI + TILES


def build(nc, x, src, dst, dst_next, pairs, codes, dst_row, base, attr17, attr96, gate1, weights, consts, out):
    with ExitStack() as ctx:
        def sb(name, shape, dt=F32):
            return ctx.enter_context(nc.sbuf_tensor(name, shape, dt))

        def sem(name):
            return ctx.enter_context(nc.semaphore(name))

        table = {r: nc.dram_tensor(f"table{r}", (NP, D), F32).ap() for r in (0, 1, 3, 4)}
        table_kv = nc.dram_tensor("table_kv", (NP, 2 * D), F32).ap()
        table_q = nc.dram_tensor("table_q", (NP, D), F32).ap()
        table_qp = nc.dram_tensor("table_qp", (NP, PARTS * D), BF16).ap()
        matrix = nc.dram_tensor("matrix", (NP, NP), BF16).ap()
        block_starts = nc.dram_tensor("block_starts", (TILES, BLOCKS), I32).ap()
        gathered_from = {0: x, 1: table[0], 2: table[1], 3: table_kv, 4: table[3], 5: table[4]}
        stored_to = {**table, 5: out}

        y_a = sb("y_a", [P, TILES * PARTS * D], BF16)
        shared_y = sb("shared_y", [P, TILES * PARTS * D // 2])
        y_b = shared_y[:, :].bitcast(BF16)
        acc = shared_y[0:HIGH, 0:NP]
        y_of = {1: y_a, 2: y_b, 4: y_a, 5: y_b}
        xs_all = sb("x_all", [P, TILES * D])
        hs_all = sb("h_all", [P, TILES * D])
        own_all = hs_all
        inv_deg = sb("inv_deg", [P, TILES])
        src_idx = sb("src_idx", [P, (GROUPS + AHEAD) * T], I32)
        dst_idx = sb("dst_idx", [P, (GROUPS + AHEAD) * T], I32)
        dst_f = sb("dst_f", [P, GROUPS * T])
        rel = sb("rel", [P, GROUPS * T])
        base_int = sb("base_int", [P, GROUPS], I32)
        base_f = sb("base_f", [P, GROUPS])
        wts = sb("wts", [D + 1, W_WIDTH])
        w_gate1 = sb("w_gate1", [ATTR, D])
        con = sb("con", [P, C_WIDTH])
        zeros = sb("zeros", [P, P])
        worst = sb("worst", [P, 7])
        worst_row = sb("worst_row", [1, 2])
        near_flag = sb("near_flag", [1, 1], I32)
        per = range(SLOTS)
        shared_strip = [sb(f"shared_strip{i}", [P, TILES * P // 2]) for i in range(2)]
        strip = [t[:, :].bitcast(BF16) for t in shared_strip]
        staged = [sb(f"staged{q}", [P, T], I32) for q in per]
        staged_dst = [sb(f"staged_dst{q}", [P, T], I32) for q in per]
        rows = [sb(f"rows{q}", [P, T * 2 * D]) for q in per]
        msg = [sb(f"msg{q}", [P, T, HIGH]) for q in per]
        onehot = [sb(f"onehot{q}", [P, T, WIN]) for q in per]
        attr_n = [shared_strip[1][0:ATTR, q * GE:(q + 1) * GE] for q in per]
        attr_w = [sb(f"attr_w{q}", [D + 1, GE]) for q in per]
        q_win = [sb(f"q_win{q}", [WIN, PARTS * D], BF16) for q in per]
        dst_wide = [shared_strip[0][0:WIN, q * GE:(q + 1) * GE].bitcast(I32) for q in per]
        win_node = sb("win_node", [WIN, GROUPS])
        q_rows = y_a[:, 0:2 * T * D].bitcast(F32)
        hidden = [sb(f"hidden{i}", [D + 1, GE]) for i in range(2)]
        onehot_t = [sb(f"onehot_t{i}", [WIN, GE], BF16) for i in range(2)]
        prod = sb("prod", [P, T, D])
        score = sb("score", [P, T, HEADS])
        capped = [sb(f"capped{i}", [P, T, HEADS]) for i in range(2)]
        wide_rel = sb("wide_rel", [P, T])
        ring_words = max(T * WIDE, RING * (CODES + P) // 2)
        shared_hot = sb("shared_hot", [P, ring_words])
        wide_hot = shared_hot[:, 0:T * WIDE].rearrange("p (t n) -> p t n", t=T)
        ring = shared_hot[:, :].bitcast(BF16)
        code_hot = [ring[:, i * CODES:(i + 1) * CODES] for i in range(RING)]
        low_hot = [ring[:, RING * CODES + i * P:RING * CODES + (i + 1) * P] for i in range(RING)]
        dst_next_idx = shared_hot[:, 0:GROUPS * T].bitcast(I32)
        code_iota = sb("code_iota", [P, CODES], mybir.dt.float16)
        deg_all = sb("deg_all", [P, TILES])
        before = sb("before", [TILES, BLOCKS + 1])
        tiles_before = sb("tiles_before", [TILES, 1])
        starts_int = sb("starts_int", [TILES, BLOCKS], I32)
        starts_row = sb("starts_row", [1, TILES * BLOCKS], I32)
        pair = [sb(f"pair{i}", [P, BLOCKS * BT * 2], I32) for i in range(2)]
        high_int = sb("high_int", [P, BLOCKS * BT], I32)
        low_int = sb("low_int", [P, BLOCKS * BT], I32)
        distance = sb("distance", [P, P])
        code_raw = sb("code_raw", [P, BLOCKS * BT])
        code = [sb(f"code{i}", [P, BLOCKS * BT]) for i in range(2)]
        low = [sb(f"low{i}", [P, BLOCKS * BT]) for i in range(2)]
        folded_sum = sb("folded_sum", [P, D])
        y_tile = sb("y_tile", [P, D])
        y_rest = sb("y_rest", [P, D])
        acc_tile = sb("acc_tile", [HIGH, P])
        x_tile = sb("x_tile", [P, D])
        x_turn = sb("x_turn", [D + 1, P])
        new_turn = sb("new_turn", [D + 1, P])
        degree = sb("degree", [P, 1])
        averaged = sb("averaged", [P, D])
        blend = sb("blend", [P, D])
        resid = sb("resid", [P, D])
        stats = sb("stats", [P, 6])
        moments = sb("moments", [P, 2])
        root = sb("root", [P, 1])
        rstd = sb("rstd", [P, 1])
        denom = sb("denom", [P, HEADS])
        inv_denom = sb("inv_denom", [P, HEADS])
        new_tile = sb("new_tile", [P, D])
        kvq_tile = sb("kvq_tile", [P, 3 * D])
        q_rest = sb("q_rest", [P, 2, D])
        q_parts = sb("q_parts", [P, PARTS, D], BF16)

        bank = [ctx.enter_context(nc.psum_tensor(f"bank{i}", [P, 512], F32)) for i in range(8)]
        PRODUCT = [bank[4], bank[5]]
        SERVE = bank[6][:, P:P + 3 * D]
        TURN, NODE = bank[6], bank[7]

        loaded = sem("loaded"); x_landed = sem("x_landed"); cleared = sem("cleared")
        prep = sem("prep"); worst_turned = sem("worst_turned"); ready = sem("ready")
        rows_landed = [sem(f"rows_landed{q}") for q in per]
        q_rows_landed = sem("q_rows_landed")
        attr_landed = [sem(f"attr_landed{q}") for q in per]
        q_win_landed = [sem(f"q_win_landed{q}") for q in per]
        idx_staged = sem("idx_staged")
        waits_passed = {e.engine: sem(f"waits_passed_{n}") for n, e in (("pe", nc.tensor), ("act", nc.scalar), ("dve", nc.vector), ("pool", nc.gpsimd))}
        onehot_made = sem("onehot_made"); hidden_summed = sem("hidden_summed"); hidden_made = sem("hidden_made")
        weights_summed = sem("weights_summed"); msg_made = sem("msg_made")
        group_summed = sem("group_summed"); group_added = sem("group_added")
        onehot_t_made = sem("onehot_t_made")
        dst_wide_landed = [sem(f"dst_wide_landed{q}") for q in per]; q_part_made = sem("q_part_made")
        query_summed = sem("query_summed"); key_scaled = sem("key_scaled"); products_made = sem("products_made")
        score_summed = sem("score_summed"); capped_made = sem("capped_made")
        exp_made = sem("exp_made")
        wide_rel_made = sem("wide_rel_made"); wide_hot_made = sem("wide_hot_made")
        wide_summed = sem("wide_summed"); wide_added = sem("wide_added")
        acc_staged = sem("acc_staged"); acc_zeroed = sem("acc_zeroed"); x_staged = sem("x_staged")
        x_turned = sem("x_turned"); x_turn_made = sem("x_turn_made"); node_summed = sem("node_summed")
        degree_made = sem("degree_made"); averaged_made = sem("averaged_made"); blended = sem("blended"); resid_made = sem("resid_made")
        stats_made = sem("stats_made"); moments_made = sem("moments_made"); root_made = sem("root_made"); rstd_made = sem("rstd_made")
        denom_made = sem("denom_made"); inv_denom_made = sem("inv_denom_made"); attended = sem("attended")
        node_made = sem("node_made"); node_kept = sem("node_kept"); table_stored = sem("table_stored")
        new_turned = sem("new_turned"); new_turn_made = sem("new_turn_made")
        kvq_summed = sem("kvq_summed"); kvq_made = sem("kvq_made")
        degrees_turned = sem("degrees_turned"); starts_made = sem("starts_made"); starts_stored = sem("starts_stored")
        starts_landed = sem("starts_landed"); pair_landed = [sem(f"pair_landed{i}") for i in range(2)]
        code_step = sem("code_step"); hot_made = sem("hot_made"); distance_made = sem("distance_made"); low_by_act = sem("low_by_act"); hot_summed = sem("hot_summed")
        block_kept = sem("block_kept"); strip_stored = [sem(f"strip_stored{i}") for i in range(2)]
        chunk_landed = [[sem(f"chunk_landed{i}_{c}") for c in range(CHUNKS)] for i in range(2)]
        chunk_summed = sem("chunk_summed"); folded = sem("folded"); acc_cleared = sem("acc_cleared")
        served_summed = sem("served_summed"); served_kept = sem("served_kept"); y_part_made = sem("y_part_made")
        kv_stored = sem("kv_stored"); q_stored = sem("q_stored")

        ident = con[:, C_IDENT:C_IDENT + P]

        def w(name, k=D + 1, n=D):
            return wts[0:k, W_COL[name]:W_COL[name] + n]

        plan = {}

        def group(r, b, q, of=None, back=0):
            k = (of or plan["edge"]).index(r)
            return b * SLOTS + (k * GROUPS + q + 1 + CREDIT - back)

        def tile(r, j, of=None, back=0):
            k = r if of is None else of.index(r)
            return j + (k * TILES + 1 + CREDIT - back)

        def body(r, b, of=None, back=0):
            k = (of or plan["edge"]).index(r)
            return b + (k * BODIES + 1 - back)

        def block_of(j, g):
            return j * BLOCKS + (g + 1 + CREDIT)

        def hot_of(j, g, i, back=0):
            return j * (BLOCKS * BT) + (g * BT + i + 1 + RING - back)

        def piece_of(j, g):
            return j * PIECES + (g + 1)

        def code_of(j, k=CODE_STEPS - 1):
            return j * CODE_STEPS + (CREDIT + 1 + k)

        def chunk_of(r, j, c=CHUNKS - 1):
            return j * CHUNKS + (BLENDED.index(r) * TILES * CHUNKS + c + 1)

        def loads_of(r, p, half):
            return half * 16 + (LOADING.index(r) * ((TILES + 1 - p) // 2) + 1) * 16

        def y_step(r, j, n):
            return j * 4 + (list(SERVED).index(r) * TILES * 4 + CREDIT + 1 + n)

        def q_part(j, step):
            return j * 5 + (CREDIT + 1 + step)

        def window(r, b, q, v, back=0):
            return b * (SLOTS * WIDES) + v + ((r * GROUPS + q) * WIDES + 1 + CREDIT - back)

        def start(eng, *sems):
            for s in sems:
                eng.sem_inc(s, CREDIT)

        def passed(eng):
            eng.sem_inc(waits_passed[eng.engine], 1)

        def schedule(eng, r, near, groups, nodes, served):
            if near:
                def places(j, b):
                    def run(place):
                        nodes(place, j, b)
                        if not isinstance(j, int) or j:
                            served(place, j - 1)
                    return run

                with eng.Fori(0, 1) as b:
                    groups(b, lambda place: None, True, False)
                with eng.Fori(1, TILE_LAG) as b:
                    groups(b, lambda place: None, False, False)
                with eng.Fori(TILE_LAG, TILE_LAG + 1) as b:
                    groups(b, lambda place: nodes(place, b - TILE_LAG, b), False, False)
                with eng.Fori(TILE_LAG + 1, BODIES - 1) as b:
                    groups(b, places(b - TILE_LAG, b), False, False)
                with eng.Fori(BODIES - 1, BODIES) as b:
                    groups(b, places(b - TILE_LAG, b), False, True)
                for j in range(BODIES - TILE_LAG, TILES):
                    for place in range(SLOTS + 1):
                        places(j, BODIES)(place)
                for place in range(SLOTS + 1):
                    served(place, TILES - 1)
            else:
                def whole(j):
                    for place in range(SLOTS + 1):
                        nodes(place, j, BODIES)
                    for place in range(SLOTS + 1):
                        served(place, j)

                with eng.Fori(0, BODIES) as b:
                    groups(b, lambda place: None, True, True)
                with eng.Fori(0, TILES - 1) as j:
                    whole(j)
                whole(TILES - 1)

        def dense(eng, r, step):
            lag = 1 if r == BUILD else 0

            def at(s, parity, half):
                def j(back):
                    if isinstance(s, int) and not 0 <= s - back < TILES:
                        return None
                    n = s - back if isinstance(s, int) else half * 2 + (parity - back)
                    return n, (parity - back) % 2, half + (parity - back) // 2
                step(j, lag)

            for s in range(4):
                at(s, s % 2, s // 2)
            with eng.Fori(2, TILES // 2) as half:
                for parity in range(2):
                    at(half * 2 + parity, parity, half)
            for s in range(TILES - TILES % 2, TILES + lag + 2):
                at(s, s % 2, s // 2)

        def with_body(b, q):
            return (b + 1, q - SLOTS) if q >= SLOTS else (b, q)

        def window_starts(eng, b, back=0):
            _, starts = nc.values_load_multi_w_load_instructions(
                base_int[0:1, bass.ds(b * SLOTS - back, SLOTS)], engines=[eng.engine], min_val=0, max_val=NP - WIN)
            return starts

        def either(eng, program):
            eng.wait_ge(ready, 1)
            near = eng.value_load(near_flag[0:1, 0:1], min_val=0, max_val=1)
            with eng.If(near):
                plan.update(RUNS[True])
                program(True)
            with eng.Else():
                plan.update(RUNS[False])
                program(False)

        block = ctx.enter_context(nc.Block())

        @block.sync
        def _(sp):
            sp.dma_start(dst_idx[:, :], dst).then_inc(loaded, 16)
            sp.dma_start(base_int[:, :], base.partition_broadcast(P)).then_inc(loaded, 16)
            sp.dma_start(con[:, :], consts).then_inc(loaded, 16)
            sp.dma_start(dst_next_idx, dst_next).then_inc(loaded, 16)
            sp.dma_start(code_iota[:, :], codes).then_inc(loaded, 16)
            sp.dma_start(src_idx[:, :], src).then_inc(loaded, 16)
            sp.dma_start(wts[:, :], weights).then_inc(loaded, 16)
            sp.dma_start(w_gate1[:, :], gate1).then_inc(loaded, 16)
            sp.dma_start(xs_all[:, :].rearrange("p (j d) -> p j d", d=D),
                         x.rearrange("(j p) d -> p j d", p=P)).then_inc(x_landed, 16)

            last_use = {2: (chunk_summed, chunk_of(1, TILES - 1)), 4: (onehot_t_made, GROUPS + CREDIT),
                        5: (chunk_summed, chunk_of(4, TILES - 1))}

            def find_starts():
                sp.wait_ge(starts_made, 3)
                sp.dma_start(block_starts, starts_int[:, :]).then_inc(starts_stored, 16)
                sp.wait_ge(starts_stored, 16)
                sp.dma_start(starts_row[:, :], block_starts.rearrange("(o j) b -> o (j b)", o=1)).then_inc(starts_landed, 16)
                sp.wait_ge(starts_landed, 16)

            def build(j, lag):
                if j(0):
                    n, p, half = j(0)
                    if not isinstance(n, int) or n >= 2:
                        sp.wait_ge(code_step, code_of(n) - 2 * CODE_STEPS)
                    for g in range(0, BLOCKS, 4):
                        _, four = nc.values_load_multi_w_load_instructions(
                            starts_row[0:1, slice(n * BLOCKS + g, n * BLOCKS + g + 4) if isinstance(n, int) else bass.ds(n * BLOCKS + g, 4)],
                            engines=[sp.engine], min_val=0, max_val=2 * EP)
                        for i in range(4):
                            sp.dma_start(pair[p][:, (g + i) * 2 * BT:(g + i + 1) * 2 * BT],
                                         pairs[0:1, bass.ds(four[i], 2 * BT * P)].rearrange("o (p c) -> (o p) c", p=P)).then_inc(pair_landed[p], 16)
                if j(2):
                    store(*j(2))

            def store(n, p, half):
                sp.wait_ge(block_kept, block_of(n, BLOCKS - 1))
                rows_at = slice(n * P, (n + 1) * P) if isinstance(n, int) else bass.ds(n * P, P)
                sp.dma_start(matrix[rows_at, :], strip[p][:, 0:NP]).then_inc(strip_stored[p], 16)

            def load(r):
                def step(j, lag):
                    if not j(0):
                        return
                    n, p, half = j(0)
                    rows_at = slice(n * P, (n + 1) * P) if isinstance(n, int) else bass.ds(n * P, P)
                    for c in range(CHUNKS):
                        if isinstance(n, int) and n < 2:
                            sp.wait_ge(*last_use[r])
                        else:
                            sp.wait_ge(chunk_summed, chunk_of(r, n, c) - 2 * CHUNKS)
                        cols = slice(PIECE_K[2 * c] * P, PIECE_K[2 * c + 2] * P)
                        sp.dma_start(strip[p][:, cols], matrix[rows_at, cols]).then_inc(chunk_landed[p][c], 16)
                return step

            def program(near):
                for r, (kind, _) in enumerate(ROUNDS):
                    if kind == SAGE:
                        if near and r == BUILD:
                            find_starts()
                            dense(sp, r, build)
                            for p in range(2):
                                sp.wait_ge(strip_stored[p], 16 * ((TILES + 1 - p) // 2))
                        elif near:
                            dense(sp, r, load(r))
                        continue
                    if kind == ATTEND:
                        sp.wait_ge(q_stored, 16 * TILES + 16)
                    with sp.Fori(0, BODIES) as b:
                        starts = window_starts(sp, b) if kind == ATTEND and near else None
                        for q in per:
                            if kind == GATED:
                                sp.wait_ge(hidden_summed, group(r, b, q, [0], SLOTS))
                                sp.dma_start(attr_n[q][:, :], attr17[:, bass.ds((b * SLOTS + q) * GE, GE)]).then_inc(attr_landed[q], 16)
                            else:
                                sp.wait_ge(weights_summed, group(r, b, q, WEIGHTED, SLOTS))
                                sp.dma_start(attr_w[q][0:D, :], attr96[:, bass.ds((b * SLOTS + q) * GE, GE)]).then_inc(attr_landed[q], 16)
                                if near:
                                    sp.wait_ge(onehot_t_made, group(r, b, q, [r], SLOTS))
                                    sp.dma_start(dst_wide[q][:, :], dst_row[:, bass.ds((b * SLOTS + q) * GE, GE)].partition_broadcast(WIN)).then_inc(dst_wide_landed[q], 16)
                                    sp.wait_ge(query_summed, group(r, b, q, [r], SLOTS))
                                    sp.dma_start(q_win[q][:, :], table_qp[bass.ds(starts[q], WIN), :]).then_inc(q_win_landed[q], 16)
                sp.wait_ge(table_stored, 16 * TILES * len(plan["stored"]) + 16)

            either(sp, program)

        @block.gpsimd
        def _(pool):
            def program(near):
                for r in plan["edge"]:
                    kind = ROUNDS[r][0]
                    if kind == ATTEND and near:
                        pool.wait_ge(chunk_summed, chunk_of(r - 1, TILES - 1))
                        nc.gpsimd.memset(acc[:, :], 0.0).then_inc(acc_cleared, 1)
                    if kind == ATTEND:
                        pool.wait_ge(kv_stored, 16 * TILES + 16)
                        pool.wait_ge(q_stored, 16 * TILES + 16)
                    elif r:
                        pool.wait_ge(table_stored, 16 * TILES * (plan["stored"].index(r - 1) + 1) + 16)
                    width = 2 * D if kind == ATTEND else D
                    with pool.Fori(0, BODIES) as b:
                        for q in per:
                            pool.wait_ge(idx_staged, group(r, b, q))
                            passed(pool)
                            for t in range(T):
                                pool.indirect_dma_start(
                                    out=rows[q][:, t * width:(t + 1) * width], out_offset=None, in_=gathered_from[r],
                                    in_offset=bass.IndirectOffsetOnAxis(ap=staged[q][:, t:t + 1], axis=0),
                                ).then_inc(rows_landed[q], 16)
                            if kind == ATTEND and not near:
                                pool.wait_ge(products_made, group(r, b, q, [r], 1))
                                passed(pool)
                                for t in range(T):
                                    pool.indirect_dma_start(
                                        out=q_rows[:, t * D:(t + 1) * D], out_offset=None, in_=table_q,
                                        in_offset=bass.IndirectOffsetOnAxis(ap=staged_dst[q][:, t:t + 1], axis=0),
                                    ).then_inc(q_rows_landed, 16)

            either(pool, program)

        @block.scalar
        def _(act):
            start(act, idx_staged, exp_made, acc_staged, acc_zeroed, x_staged,
                  x_turn_made, root_made, node_kept, new_turn_made, kvq_made, block_kept, served_kept)
            for s in (table_stored, kv_stored, q_stored):
                act.sem_inc(s, 16)

            def at(j, size):
                return slice(j * size, (j + 1) * size) if isinstance(j, int) else bass.ds(j * size, size)

            def deviation(r, j):
                if r in NORMED:
                    act.wait_ge(moments_made, tile(r, j, NORMED))
                    act.wait_ge(node_made, tile(r, j, back=1))
                    nc.scalar.activation(root[:, :], moments[:, 1:2], ACT.Sqrt, bias=con[:, C_EPS:C_EPS + 1]).then_inc(root_made, 1)

            def keep(r, j, near):
                what = ROUNDS[r][1]
                act.wait_ge(node_made, tile(r, j))
                if r in plan["kept"]:
                    passed(act)
                    kept = hs_all if what == "hidden" else xs_all
                    nc.scalar.copy(kept[:, at(j, D)], new_tile[:, :]).then_inc(node_kept, 1)
                if r in plan["stored"]:
                    k = N - j * P if isinstance(j, int) and what == "output" and j == TILES - 1 else P
                    act.dma_start(stored_to[r][slice(j * P, j * P + k) if isinstance(j, int) else bass.ds(j * P, k), :],
                                  new_tile[0:k, :]).then_inc(table_stored, 16)

            def turn(r, j):
                act.wait_ge(new_turned, tile(r, j, plan["turned"]))
                nc.scalar.copy(new_turn[0:D, :], TURN[0:D, 0:P]).then_inc(new_turn_made, 1)

            def serve(r, j, near):
                if r in SERVED:
                    act.wait_ge(served_summed, tile(r, j, list(SERVED)))
                    act.wait_ge(y_part_made, y_step(r, j, -1))
                    passed(act)
                    nc.scalar.copy(own_all[:, at(j, D)], SERVE[:, 0:D])
                    nc.scalar.copy(y_tile[:, :], SERVE[:, D:2 * D]).then_inc(served_kept, 1)
                    return
                act.wait_ge(kvq_summed, tile(r, j, [r]))
                act.wait_ge(kv_stored, 16 * j + 16)
                act.wait_ge(q_stored, 16 * j + 16)
                nc.scalar.copy(kvq_tile[:, 0:2 * D], SERVE[:, 0:2 * D])
                nc.scalar.mul(kvq_tile[:, 2 * D:3 * D], SERVE[:, 2 * D:3 * D], float(HD) ** -0.5).then_inc(kvq_made, 1)
                act.wait_ge(kvq_made, tile(r, j, [r]))
                act.dma_start(table_kv[at(j, P), :], kvq_tile[:, 0:2 * D]).then_inc(kv_stored, 16)
                if not near:
                    act.dma_start(table_q[at(j, P), :], kvq_tile[:, 2 * D:3 * D]).then_inc(q_stored, 16)

            def store_q(j):
                act.wait_ge(q_part_made, q_part(j, 4))
                act.dma_start(table_qp[at(j, P), :], q_parts[:, :, :].rearrange("p k d -> p (k d)")).then_inc(q_stored, 16)

            def served(r, near):
                def run(place, j):
                    if r in plan["turned"] and place == TURN_AT[r]:
                        turn(r, j)
                    if r in plan["turned"] and place == TURN_AT[r] + 1:
                        serve(r, j, near)
                return run

            def low_hot_of(n, p, half, g):
                e = (g + 1) * PER_PIECE * BT - 1
                act.wait_ge(code_step, code_of(n, 2))
                act.wait_ge(hot_summed, hot_of(n, 0, e, RING))
                if not isinstance(n, int) or n or g:
                    act.wait_ge(low_by_act, piece_of(n, g) - 1)
                nc.scalar.activation(distance[:, :], code_iota[:, 0:P], ACT.Abs, bias=low[p][:, e:e + 1],
                                     scale=-1.0).then_inc(distance_made, 1)
                act.wait_ge(distance_made, piece_of(n, g))
                nc.scalar.activation(low_hot[e % RING], distance[:, :], ACT.Relu, bias=con[:, C_CUM + BLOCKS:C_CUM + BLOCKS + 1],
                                     scale=-1.0).then_inc(low_by_act, 1)

            def strips(r):
                def step(j, lag):
                    for g in range(PIECES):
                        done, ready_tile = j(lag + 1), j(lag + 2)
                        if g == 1 and ready_tile and r in plan["turned"]:
                            turn(r, ready_tile[0])
                        if g == 3 and done:
                            deviation(r, done[0])
                        if g == 4 and ready_tile and r in plan["turned"]:
                            serve(r, ready_tile[0], True)
                        if g == 6 and done:
                            keep(r, done[0], True)
                        if r == BUILD:
                            if g == 0 and j(0) and isinstance(j(0)[0], int) and j(0)[0] == 0:
                                low_hot_of(*j(0), 0)
                            if g + 1 < PIECES and j(0):
                                low_hot_of(*j(0), g + 1)
                            if g + 1 == PIECES and j(0) and j(-1):
                                low_hot_of(*j(-1), 0)
                        if r == BUILD and j(0):
                            n, p, half = j(0)
                            if g == 0:
                                if not isinstance(n, int) or n >= 2:
                                    act.wait_ge(chunk_summed, chunk_of(r, n) - 2 * CHUNKS)
                                    act.wait_ge(strip_stored[p], half * 16)
                            to = strip[p].rearrange("p (k d) -> p k d", d=P)
                            for block in range(g * PER_PIECE, (g + 1) * PER_PIECE):
                                act.wait_ge(hot_summed, hot_of(n, block, BT - 1))
                                nc.scalar.copy(to[:, :, block * BLOCK:(block + 1) * BLOCK],
                                               bank[block % 4][:, 0:CODES].rearrange("p (d k) -> p k d", k=TILES)).then_inc(block_kept, 1)
                    if r == 2 and j(lag + 2):
                        store_q(j(lag + 2)[0])
                return step

            def groups(r, near):
                kind = ROUNDS[r][0]

                def run(b, node, first, last):
                    for q in per:
                        n = q + AHEAD
                        if not near:
                            act.wait_ge(group_summed, group(r, b, n, back=SLOTS))
                        else:
                            act.wait_ge(msg_made, group(r, b, n, WEIGHTED, SLOTS))
                        passed(act)
                        cols = bass.ds((b * SLOTS + n) * T, T)
                        if not near:
                            nc.scalar.copy(staged_dst[n % SLOTS][:, :], dst_idx[:, cols])
                        nc.scalar.copy(staged[n % SLOTS][:, :], src_idx[:, cols]).then_inc(idx_staged, 1)
                        node(q)
                        if kind == ATTEND:
                            act.wait_ge(capped_made, group(r, b, q, [r]))
                            act.wait_ge(group_summed, group(r, b, q, back=SLOTS))
                            nc.scalar.activation(msg[q][:, :, D:HIGH], capped[q % 2][:, :, :], ACT.Exp).then_inc(exp_made, 1)
                    node(SLOTS)
                return run

            def nodes(r, near):
                what = ROUNDS[r][1]
                operand = hs_all if LAYER_SRC.get(what) == "h" else xs_all

                def run(place, j, b):
                    cols = slice(j * P, (j + 1) * P) if isinstance(j, int) else bass.ds(j * P, P)
                    feats = slice(j * D, (j + 1) * D) if isinstance(j, int) else bass.ds(j * D, D)
                    if place == 0:
                        act.wait_ge(group_added, group(r, b, 0, back=1 + (OVERLAP if near and b is not BODIES else 0)))
                        act.wait_ge(node_made, tile(r, j, back=1))
                        passed(act)
                        nc.scalar.copy(acc_tile[:, :], acc[:, cols]).then_inc(acc_staged, 1)
                        if r in plan["own"]:
                            nc.scalar.copy(x_tile[:, :], operand[:, feats]).then_inc(x_staged, 1)
                    if place == 1 and not near:
                        act.wait_ge(acc_staged, tile(r, j, plan["edge"]))
                        passed(act)
                        nc.scalar.copy(acc[:, cols], zeros[0:HIGH, :]).then_inc(acc_zeroed, 1)
                    if place == 1 and r in plan["own"]:
                        act.wait_ge(x_turned, tile(r, j, plan["own"]))
                        nc.scalar.copy(x_turn[0:D, :], TURN[0:D, 0:P]).then_inc(x_turn_made, 1)
                    if place == 3:
                        deviation(r, j)
                    if place == SLOTS:
                        keep(r, j, near)
                return run

            def program(near):
                for q in range(AHEAD):
                    if not near:
                        nc.scalar.copy(staged_dst[q][:, :], dst_idx[:, q * T:(q + 1) * T])
                    nc.scalar.copy(staged[q][:, :], src_idx[:, q * T:(q + 1) * T]).then_inc(idx_staged, 1)
                act.wait_ge(x_landed, 16)
                for r in range(len(ROUNDS)):
                    if r in plan["edge"]:
                        schedule(act, r, near, groups(r, near), nodes(r, near), served(r, near))
                    else:
                        dense(act, r, strips(r))

            either(act, program)

        @block.vector
        def _(dve):
            start(dve, hidden_made, onehot_t_made, q_part_made, onehot_made, msg_made, group_added, key_scaled, products_made, score_summed,
                  capped_made, wide_rel_made, wide_hot_made, wide_added, degree_made, averaged_made, blended, resid_made, stats_made,
                  moments_made, rstd_made, denom_made, inv_denom_made, attended, node_made,
                  code_step, folded, y_part_made)
            nc.vector.memset(zeros[:, :], 0.0)
            nc.vector.memset(x_turn[D:D + 1, :], 1.0)
            nc.vector.memset(new_turn[D:D + 1, :], 1.0)
            for i in range(2):
                nc.vector.memset(hidden[i][D:D + 1, :], 1.0)
            for q in per:
                nc.vector.memset(attr_w[q][D:D + 1, :], 1.0)
                nc.vector.memset(msg[q][:, :, D:D + 1], 1.0)
            nc.vector.memset(worst[:, 6:7], 0.0).then_inc(cleared, 1)
            dve.wait_ge(cleared, 1)

            steps = [0]

            def then(ins):
                steps[0] += 1
                ins.then_inc(prep, 1)
                dve.wait_ge(prep, steps[0])

            dve.wait_ge(loaded, 16 * 8)
            then(nc.vector.tensor_copy(base_f[:, :], base_int[:, :]))
            then(nc.vector.tensor_scalar(base_f[:, :], base_f[:, :], float(NP - WIN), None, ALU.min))
            then(nc.vector.tensor_copy(base_int[:, :], base_f[:, :]))
            then(nc.vector.tensor_scalar(win_node[:, :], base_f[0:WIN, :], con[0:WIN, C_NODE:C_NODE + 1], None, ALU.add))
            then(nc.vector.tensor_copy(dst_f[:, :], dst_idx[:, 0:GROUPS * T]))
            by_group = [P, GROUPS, T]
            then(nc.vector.tensor_tensor(rel[:, :].rearrange("p (g t) -> p g t", t=T),
                                         dst_f[:, :].rearrange("p (g t) -> p g t", t=T),
                                         con[:, C_LIMIT:C_LIMIT + GROUPS].unsqueeze(2).to_broadcast(by_group), ALU.subtract))
            then(nc.vector.tensor_reduce(worst[:, 0:1], rel[:, :], AX.X, ALU.min))
            then(nc.vector.tensor_tensor(rel[:, :].rearrange("p (g t) -> p g t", t=T),
                                         dst_f[:, :].rearrange("p (g t) -> p g t", t=T),
                                         base_f[:, :].unsqueeze(2).to_broadcast(by_group), ALU.subtract))
            then(nc.vector.tensor_reduce(worst[:, 1:2], rel[:, :], AX.X, ALU.min))
            then(nc.vector.tensor_reduce(worst[:, 2:3], rel[:, :], AX.X, ALU.max))
            then(nc.vector.tensor_scalar(worst[:, 2:3], worst[:, 2:3], -1.0, float(WIN - 1), ALU.mult, ALU.add))
            ordered = shared_y[:, 0:GROUPS * T]
            then(nc.vector.tensor_tensor(ordered, dst_next_idx, dst_f[:, :], ALU.subtract))
            then(nc.vector.tensor_reduce(worst[:, 3:4], ordered, AX.X, ALU.min))
            for k, (tiles, least) in enumerate(((BT, BLOCK), (1, 1))):
                span = GROUPS * T - tiles
                then(nc.vector.tensor_tensor(ordered[:, 0:span], dst_f[:, tiles:], dst_f[:, 0:span], ALU.subtract))
                then(nc.vector.tensor_reduce(worst[:, 4 + k:5 + k], ordered[:, 0:span], AX.X, ALU.min))
                then(nc.vector.tensor_scalar(worst[:, 4 + k:5 + k], worst[:, 4 + k:5 + k], float(-least), None, ALU.add))
            then(nc.vector.tensor_reduce(worst[:, 6:7], worst[:, 0:6], AX.X, ALU.min))
            then(nc.vector.memset(acc[:, :], 0.0))
            then(nc.vector.tensor_tensor(w("self0"), w("self0"), w("bias0"), ALU.add))
            dve.wait_ge(worst_turned, 1)
            then(nc.vector.tensor_reduce(worst_row[:, 0:1], TURN[0:1, 0:P], AX.X, ALU.min))
            then(nc.vector.tensor_scalar(worst_row[:, 1:2], worst_row[:, 0:1], 0.0, None, ALU.is_ge))
            nc.vector.tensor_copy(near_flag[:, :], worst_row[:, 1:2]).then_inc(ready, 1)

            iota = con[:, C_IOTA:C_IOTA + WIDE]

            def groups(r, near):
                kind = ROUNDS[r][0]
                high = {GATED: D + 1, SAGE: D, ATTEND: HIGH}[kind]

                def hot(b, q):
                    dve.wait_ge(group_summed, group(r, b, q, back=SLOTS))
                    nc.vector.tensor_tensor(
                        onehot[q][:, :, :], iota[:, 0:WIN].unsqueeze(1).to_broadcast([P, T, WIN]),
                        rel[:, bass.ds((b * SLOTS + q) * T, T)].unsqueeze(2).to_broadcast([P, T, WIN]),
                        ALU.is_equal).then_inc(onehot_made, 1)

                def hide(b, q):
                    dve.wait_ge(hidden_summed, group(r, b, q, [0]))
                    dve.wait_ge(weights_summed, group(r, b, q, WEIGHTED, 2))
                    nc.vector.tensor_scalar(hidden[q % 2][0:D, :], bank[q % 2][0:D, :], wts[0:D, W_WIDTH - 1:W_WIDTH],
                                            0.0, ALU.add, ALU.max).then_inc(hidden_made, 1)

                def hot_t(b, q):
                    dve.wait_ge(dst_wide_landed[q], body(r, b, [r]) * 16)
                    dve.wait_ge(query_summed, group(r, b, q, [r], 2))
                    nc.vector.tensor_scalar(onehot_t[q % 2][:, :], dst_wide[q][:, :], win_node[:, bass.ds(b * SLOTS + q, 1)],
                                            None, ALU.is_equal).then_inc(onehot_t_made, 1)

                def gate(b, q):
                    dve.wait_ge(weights_summed, group(r, b, q, WEIGHTED))
                    dve.wait_ge(rows_landed[q], body(r, b) * (16 * T))
                    dve.wait_ge(group_summed, group(r, b, q, back=SLOTS))
                    nc.vector.tensor_tensor(msg[q][:, :, 0:D], bank[2 + q % 2][:, 0:T * D].rearrange("p (t d) -> p t d", d=D),
                                            rows[q][:, 0:T * D].rearrange("p (t d) -> p t d", d=D),
                                            ALU.mult).then_inc(msg_made, 1)

                def attend_scores(b, q):
                    kv = rows[q][:, :].rearrange("p (t d) -> p t d", d=2 * D)
                    dve.wait_ge(weights_summed, group(r, b, q, WEIGHTED))
                    dve.wait_ge(rows_landed[q], body(r, b) * (16 * T))
                    nc.vector.tensor_tensor(prod[:, :, :], bank[q % 2][:, 0:T * D].rearrange("p (t d) -> p t d", d=D),
                                            kv[:, :, 0:D], ALU.mult).then_inc(key_scaled, 1)
                    if near:
                        queries = bank[2 + q % 2][:, 0:T * D]
                        dve.wait_ge(query_summed, group(r, b, q, [r]))
                    else:
                        queries = q_rows[:, :]
                        dve.wait_ge(q_rows_landed, (b * SLOTS + q + 1) * (16 * T))
                    dve.wait_ge(key_scaled, group(r, b, q, [r]))
                    nc.vector.tensor_tensor(prod[:, :, :], prod[:, :, :], queries.rearrange("p (t d) -> p t d", d=D),
                                            ALU.mult).then_inc(products_made, 1)
                    dve.wait_ge(products_made, group(r, b, q, [r]))
                    nc.vector.tensor_reduce(score[:, :, :], prod[:, :, :].rearrange("p t (h d) -> p t h d", d=HD),
                                            AX.X, ALU.add).then_inc(score_summed, 1)
                    dve.wait_ge(score_summed, group(r, b, q, [r]))
                    nc.vector.tensor_scalar(capped[q % 2][:, :, :], score[:, :, :], 5.0, -5.0, ALU.min,
                                            ALU.max).then_inc(capped_made, 1)

                def attend_values(b, q):
                    kv = rows[q][:, :].rearrange("p (t d) -> p t d", d=2 * D)
                    dve.wait_ge(exp_made, group(r, b, q, [r]))
                    nc.vector.tensor_tensor(
                        msg[q][:, :, 0:D].rearrange("p t (h d) -> p t h d", d=HD),
                        kv[:, :, D:2 * D].rearrange("p t (h d) -> p t h d", d=HD),
                        msg[q][:, :, D:HIGH].unsqueeze(3).to_broadcast([P, T, HEADS, HD]), ALU.mult).then_inc(msg_made, 1)

                def add(b, q, first_node):
                    dve.wait_ge(group_summed, group(r, b, q))
                    dve.wait_ge(group_added, group(r, b, q, back=1))
                    at = acc[0:high, bass.ds(first_node, WIN)]
                    nc.vector.tensor_tensor(at, at, bank[4 + q % 2][0:high, 0:WIN], ALU.add).then_inc(group_added, 1)

                def add_wide(b, q):
                    with dve.Fori(0, WIDES) as v:
                        dve.wait_ge(wide_summed, window(r, b, q, v, 1))
                        nc.vector.tensor_scalar(wide_rel[:, :], dst_f[:, bass.ds((b * SLOTS + q) * T, T)],
                                                con[:, bass.ds(v + C_WIDE, 1)], None, ALU.subtract).then_inc(wide_rel_made, 1)
                        dve.wait_ge(wide_rel_made, window(r, b, q, v))
                        nc.vector.tensor_tensor(wide_hot[:, :, :], iota.unsqueeze(1).to_broadcast([P, T, WIDE]),
                                                wide_rel[:, :].unsqueeze(2).to_broadcast([P, T, WIDE]),
                                                ALU.is_equal).then_inc(wide_hot_made, 1)
                        dve.wait_ge(wide_summed, window(r, b, q, v))
                        dve.wait_ge(wide_added, window(r, b, q, v, 1))
                        at = acc[0:high, bass.ds(v * WIDE, WIDE)]
                        nc.vector.tensor_tensor(at, at, bank[4][0:high, 0:WIDE], ALU.add).then_inc(wide_added, 1)
                    dve.wait_ge(wide_added, window(r, b, q, WIDES - 1))
                    dve.sem_inc(group_added, 1)

                def run(b, node, first, last):
                    behind = OVERLAP if kind == ATTEND else 1

                    def ahead(b, q):
                        if near and kind == ATTEND:
                            hot_t(b, q)
                        if kind == GATED:
                            hide(b, q)
                        if near:
                            hot(b, q)

                    if first:
                        ahead(b, 0)
                    for q in per:
                        if q + 1 < SLOTS or not last:
                            ahead(*with_body(b, q + 1))
                        if kind == GATED:
                            gate(b, q)
                        if kind == ATTEND:
                            attend_scores(b, q)
                        if kind == ATTEND and near and (q or not first):
                            attend_values(b, q - 1)
                        if near and q == 0:
                            starts = window_starts(dve, b, 0 if first else behind)
                        if near and (q >= behind or not first):
                            add(b, q - behind, starts[q - behind if first else q])
                        if not near:
                            if kind == ATTEND:
                                attend_values(b, q)
                            add_wide(b, q)
                        node(q)
                    if near and last:
                        starts = window_starts(dve, b)
                        if kind == ATTEND:
                            attend_values(b, SLOTS - 1)
                        for q in range(SLOTS - behind, SLOTS):
                            add(b, q, starts[q])
                    node(SLOTS)
                return run

            def nodes(r, near):
                what = ROUNDS[r][1]

                def fold(j, parity):
                    dve.wait_ge(chunk_summed, chunk_of(r, j))
                    nc.vector.tensor_reduce(folded_sum[:, :], PRODUCT[parity][:, 0:PARTS * D].rearrange("p (k d) -> p d k", k=PARTS),
                                            AX.X, ALU.add).then_inc(folded, 1)

                def sums(j):
                    one = slice(j, j + 1) if isinstance(j, int) else bass.ds(j, 1)
                    feats = slice(j * D, (j + 1) * D) if isinstance(j, int) else bass.ds(j * D, D)
                    if r in plan["edge"]:
                        dve.wait_ge(node_summed, tile(r, j, plan["edge"]))
                    else:
                        dve.wait_ge(folded, tile(r, j, BLENDED))
                        if what == "hidden":
                            nc.vector.scalar_tensor_tensor(out=blend[:, :], in0=folded_sum[:, :], scalar=inv_deg[:, one],
                                                           in1=own_all[:, feats], op0=ALU.mult, op1=ALU.add).then_inc(blended, 1)
                            dve.wait_ge(blended, tile(r, j, HIDDEN))
                            return
                        nc.vector.scalar_tensor_tensor(out=averaged[:, :], in0=folded_sum[:, :], scalar=inv_deg[:, one],
                                                       in1=xs_all[:, feats], op0=ALU.mult, op1=ALU.add).then_inc(averaged_made, 1)
                        dve.wait_ge(averaged_made, tile(r, j, SUMMED if near else BLENDED))
                        nc.vector.tensor_tensor(resid[:, :], averaged[:, :], own_all[:, feats], ALU.add).then_inc(resid_made, 1)
                        moments_of(j)
                        return
                    if what == "first":
                        if near:
                            nc.vector.tensor_copy(deg_all[:, one], NODE[:, D:D + 1])
                        nc.vector.tensor_scalar(degree[:, :], NODE[:, D:D + 1], 1.0, None, ALU.max).then_inc(degree_made, 1)
                        nc.vector.scalar_tensor_tensor(out=resid[:, :], in0=NODE[:, 0:D], scalar=0.0, in1=x_tile[:, :],
                                                       op0=ALU.max, op1=ALU.add).then_inc(resid_made, 1)
                        dve.wait_ge(degree_made, tile(r, j, [0]))
                        nc.vector.reciprocal(inv_deg[:, one], degree[:, :])
                    elif what == "attended":
                        nc.vector.tensor_scalar(denom[:, :], NODE[:, D:HIGH], 1e-6, None, ALU.add).then_inc(denom_made, 1)
                        dve.wait_ge(denom_made, tile(r, j, [r]))
                        nc.vector.reciprocal(inv_denom[:, :], denom[:, :]).then_inc(inv_denom_made, 1)
                        dve.wait_ge(inv_denom_made, tile(r, j, [r]))
                        nc.vector.tensor_tensor(blend[:, :].rearrange("p (h d) -> p h d", d=HD),
                                                NODE[:, 0:D].rearrange("p (h d) -> p h d", d=HD),
                                                inv_denom[:, :].unsqueeze(2).to_broadcast([P, HEADS, HD]),
                                                ALU.mult).then_inc(attended, 1)
                        dve.wait_ge(attended, tile(r, j, [r]))
                        nc.vector.tensor_tensor(resid[:, :], blend[:, :], xs_all[:, feats], ALU.add).then_inc(resid_made, 1)
                    else:
                        if what == "hidden":
                            nc.vector.tensor_scalar(averaged[:, :], NODE[:, D:2 * D], inv_deg[:, one], None,
                                                    ALU.mult).then_inc(averaged_made, 1)
                            dve.wait_ge(averaged_made, tile(r, j, BLENDED))
                            nc.vector.tensor_tensor(blend[:, :], averaged[:, :], NODE[:, 0:D], ALU.add).then_inc(blended, 1)
                            dve.wait_ge(blended, tile(r, j, HIDDEN))
                        else:
                            nc.vector.scalar_tensor_tensor(out=averaged[:, :], in0=NODE[:, D:2 * D], scalar=inv_deg[:, one],
                                                           in1=xs_all[:, feats], op0=ALU.mult,
                                                           op1=ALU.add).then_inc(averaged_made, 1)
                            dve.wait_ge(averaged_made, tile(r, j, BLENDED))
                            nc.vector.tensor_tensor(resid[:, :], averaged[:, :], NODE[:, 0:D], ALU.add).then_inc(resid_made, 1)
                    moments_of(j)

                def moments_of(j):
                    if r in NORMED:
                        dve.wait_ge(resid_made, tile(r, j, NORMED))
                        nc.vector.bn_stats(stats[:, :], resid[:, :]).then_inc(stats_made, 1)
                        dve.wait_ge(stats_made, tile(r, j, NORMED))
                        passed(dve)
                        nc.vector.bn_aggr(moments[:, :], stats[:, :]).then_inc(moments_made, 1)
                        dve.wait_ge(moments_made, tile(r, j, NORMED))

                def finish(j):
                    if r in NORMED:
                        dve.wait_ge(root_made, tile(r, j, NORMED))
                        nc.vector.reciprocal(rstd[:, :], root[:, :]).then_inc(rstd_made, 1)
                        dve.wait_ge(rstd_made, tile(r, j, NORMED))
                    dve.wait_ge(table_stored, stored_before(plan["stored"], r, j))
                    dve.wait_ge(node_kept, kept_before(plan["kept"], r, j))
                    if r in plan["turned"]:
                        dve.wait_ge(new_turned, tile(r, j, plan["turned"], 1))
                    elif near:
                        dve.wait_ge(new_turned, TILES * len(plan["turned"]) + CREDIT)
                    if what == "hidden":
                        nc.vector.tensor_scalar(new_tile[:, :], blend[:, :], 0.0, None, ALU.max).then_inc(node_made, 1)
                    else:
                        nc.vector.tensor_scalar(new_tile[:, :], resid[:, :], moments[:, 0:1], rstd[:, 0:1],
                                                ALU.subtract, ALU.mult).then_inc(node_made, 1)

                def split_q(j):
                    def step(ins, n):
                        ins.then_inc(q_part_made, 1)
                        dve.wait_ge(q_part_made, q_part(j, n))

                    q_all = kvq_tile[:, 2 * D:3 * D]
                    dve.wait_ge(kvq_made, tile(r, j, [r]))
                    dve.wait_ge(q_stored, j * 16 + 16)
                    step(nc.vector.tensor_copy(q_parts[:, 0, :], q_all), 0)
                    step(nc.vector.tensor_tensor(q_rest[:, 0, :], q_all, q_parts[:, 0, :], ALU.subtract), 1)
                    step(nc.vector.tensor_copy(q_parts[:, 1, :], q_rest[:, 0, :]), 2)
                    step(nc.vector.tensor_tensor(q_rest[:, 1, :], q_rest[:, 0, :], q_parts[:, 1, :], ALU.subtract), 3)
                    step(nc.vector.tensor_copy(q_parts[:, 2, :], q_rest[:, 1, :]), 4)

                def split_y(j, which):
                    y = y_of[SERVED[r]]
                    part = [y[:, slice((j * PARTS + k) * D, (j * PARTS + k + 1) * D) if isinstance(j, int)
                              else bass.ds(j * (PARTS * D) + k * D, D)] for k in range(PARTS)]
                    for k in which:
                        if k == 0:
                            dve.wait_ge(served_kept, tile(r, j, list(SERVED)))
                            ins = nc.vector.tensor_copy(part[0], y_tile[:, :])
                        else:
                            dve.wait_ge(y_part_made, y_step(r, j, k - 1))
                        if k == 1:
                            ins = nc.vector.tensor_tensor(y_rest[:, :], y_tile[:, :], part[0], ALU.subtract)
                        if k == 2:
                            ins = nc.vector.tensor_copy(part[1], y_rest[:, :])
                        if k == 3:
                            ins = nc.vector.tensor_tensor(part[2], y_rest[:, :], part[1], ALU.subtract)
                        ins.then_inc(y_part_made, 1)

                def served(j, which=range(4)):
                    if what == "project":
                        split_q(j)
                    elif r in SERVED:
                        split_y(j, which)

                def run(place, j, b):
                    if place == 2:
                        sums(j)
                    if place == 3:
                        finish(j)

                run.fold, run.sums, run.finish, run.served = fold, sums, finish, served
                return run

            def find_starts():
                def then_start(ins, n):
                    ins.then_inc(starts_made, 1)
                    dve.wait_ge(starts_made, n)

                dve.wait_ge(degrees_turned, 1)
                nc.vector.tensor_copy(before[:, :], NODE[0:TILES, 0:BLOCKS + 1]).then_inc(starts_made, 1)
                dve.wait_ge(degrees_turned, 2)
                nc.vector.tensor_copy(tiles_before[:, :], NODE[0:TILES, 0:1]).then_inc(starts_made, 1)
                dve.wait_ge(starts_made, 2)
                nc.vector.tensor_scalar(starts_int[:, :], before[:, 0:BLOCKS], tiles_before[:, 0:1], 2.0, ALU.add,
                                        ALU.mult).then_inc(starts_made, 1)

            def code_edges(n, p, half, which=range(CODE_STEPS)):
                edges = pair[p][:, :].rearrange("p (e c) -> p e c", c=2)
                shift = slice(C_SHIFT + n * BLOCKS, C_SHIFT + (n + 1) * BLOCKS) if isinstance(n, int) else bass.ds(n * BLOCKS + C_SHIFT, BLOCKS)
                for k in which:
                    if k == 0:
                        dve.wait_ge(pair_landed[p], half * (16 * BLOCKS) + 16 * BLOCKS)
                        ins = nc.vector.tensor_scalar(high_int[:, :], edges[:, :, 0], 7, None, ALU.arith_shift_right)
                    elif k == 1:
                        ins = nc.vector.tensor_scalar(low_int[:, :], edges[:, :, 0], P - 1, None, ALU.bitwise_and)
                    elif k == 2:
                        ins = nc.vector.tensor_copy(low[p][:, :], low_int[:, :])
                    elif k == 3:
                        ins = nc.vector.scalar_tensor_tensor(out=code_raw[:, :], in0=edges[:, :, 1], scalar=float(TILES), in1=high_int[:, :],
                                                             op0=ALU.mult, op1=ALU.add)
                    else:
                        ins = nc.vector.tensor_tensor(code[p][:, :].rearrange("p (g i) -> p g i", i=BT),
                                                      code_raw[:, :].rearrange("p (g i) -> p g i", i=BT),
                                                      con[:, shift].unsqueeze(2).to_broadcast([P, BLOCKS, BT]), ALU.subtract)
                    ins.then_inc(code_step, 1)
                    if k + 1 in which:
                        dve.wait_ge(code_step, code_of(n, k))

            def strips(r):
                node = nodes(r, True)

                def step(j, lag):
                    if r == BUILD and j(0) and isinstance(j(0)[0], int) and j(0)[0] == 0:
                        code_edges(*j(0))
                    for g in range(PIECES):
                        done, ready_tile = j(lag + 1), j(lag + 2)
                        if g == (1 if r == BUILD else 0) and done:
                            node.fold(done[0], done[1])
                        if g == (2 if r == BUILD else 1) and done:
                            node.sums(done[0])
                        if g == 4 and done:
                            node.finish(done[0])
                        if g == 6 and ready_tile and r == 2:
                            node.served(ready_tile[0])
                        if g in Y_AT and ready_tile and r in SERVED:
                            node.served(ready_tile[0], Y_AT[g])
                        if r == BUILD and g >= 3 and j(-1) and j(0):
                            if g > 3:
                                dve.wait_ge(code_step, code_of(j(-1)[0], g - 4))
                            code_edges(*j(-1), [g - 3])
                        if r == BUILD and j(0):
                            n, p, half = j(0)
                            if g == 0:
                                dve.wait_ge(code_step, code_of(n))
                            for e in range(g * PER_PIECE * BT, (g + 1) * PER_PIECE * BT):
                                slot = e % RING
                                dve.wait_ge(hot_summed, hot_of(n, 0, e, RING))
                                if (e + 1) % (PER_PIECE * BT):
                                    nc.vector.tensor_scalar(low_hot[slot], code_iota[:, 0:P], low[p][:, e:e + 1], None, ALU.is_equal)
                                nc.vector.tensor_scalar(code_hot[slot], code_iota[:, :], code[p][:, e:e + 1], None,
                                                        ALU.is_equal).then_inc(hot_made, 1)
                return step

            def program(near):
                for r in range(len(ROUNDS)):
                    if near and r == BUILD:
                        find_starts()
                    if r not in plan["edge"]:
                        dense(dve, r, strips(r))
                        continue
                    if near:
                        if r:
                            dve.wait_ge(acc_cleared, 1)
                    elif r:
                        dve.wait_ge(acc_zeroed, TILES * r + CREDIT)
                    node = nodes(r, near)
                    schedule(dve, r, near, groups(r, near), node,
                             lambda place, j: node.served(j) if near and place == TURN_AT[r] + 2 else None)

            either(dve, program)

        @block.tensor
        def _(pe):
            pe.sem_inc(hot_summed, RING - CREDIT)
            start(pe, hidden_summed, weights_summed, group_summed, query_summed, wide_summed,
                  x_turned, node_summed, new_turned, kvq_summed, hot_summed, served_summed)
            pe.wait_ge(prep, 22)
            nc.tensor.transpose(TURN[0:1, 0:P], worst[:, 6:7], ident).then_inc(worst_turned, 1)

            def groups(r, near):
                kind = ROUNDS[r][0]
                high = {GATED: D + 1, SAGE: D, ATTEND: HIGH}[kind]

                def edge_hidden(b, q):
                    pe.wait_ge(attr_landed[q], body(r, b, WEIGHTED) * 16)
                    pe.wait_ge(hidden_made, group(r, b, q, [0], 2))
                    nc.tensor.matmul(bank[q % 2][0:D, :], w_gate1[:, :], attr_n[q][:, :], start=True,
                                     stop=True).then_inc(hidden_summed, 1)

                def edge_weights(b, q):
                    if kind == GATED:
                        pe.wait_ge(hidden_made, group(r, b, q, [0]))
                        pe.wait_ge(msg_made, group(r, b, q, WEIGHTED, 2))
                        lhs, rhs, to = hidden[q % 2], w("gate2"), bank[2 + q % 2]
                    else:
                        pe.wait_ge(attr_landed[q], body(r, b, WEIGHTED) * 16)
                        pe.wait_ge(key_scaled, group(r, b, q, [r], 2))
                        lhs, rhs, to = attr_w[q], w("edge"), bank[q % 2]
                    for t in range(T):
                        mm = nc.tensor.matmul(to[:, t * D:(t + 1) * D], lhs[:, t * P:(t + 1) * P], rhs, start=True, stop=True)
                    mm.then_inc(weights_summed, 1)

                def edge_queries(b, q):
                    pe.wait_ge(onehot_t_made, group(r, b, q, [r]))
                    pe.wait_ge(q_win_landed[q], body(r, b, [r]) * 16)
                    pe.wait_ge(products_made, group(r, b, q, [r], 2))
                    for t in range(T):
                        for k in range(PARTS):
                            mm = nc.tensor.matmul(bank[2 + q % 2][:, t * D:(t + 1) * D], onehot_t[q % 2][:, t * P:(t + 1) * P],
                                                  q_win[q][:, k * D:(k + 1) * D], start=(k == 0), stop=(k == PARTS - 1))
                    mm.then_inc(query_summed, 1)

                def summed(q, t):
                    return rows[q][:, t * D:(t + 1) * D] if kind == SAGE else msg[q][:, t, 0:high]

                def have_messages(b, q):
                    if kind == SAGE:
                        pe.wait_ge(rows_landed[q], body(r, b) * (16 * T))
                    else:
                        pe.wait_ge(msg_made, group(r, b, q, WEIGHTED))

                def sum_group(b, q):
                    have_messages(b, q)
                    pe.wait_ge(onehot_made, group(r, b, q))
                    pe.wait_ge(group_added, group(r, b, q, back=2))
                    for t in range(T):
                        mm = nc.tensor.matmul(bank[4 + q % 2][0:high, 0:WIN], summed(q, t), onehot[q][:, t, :],
                                              start=(t == 0), stop=(t == T - 1))
                    mm.then_inc(group_summed, 1)

                def sum_wide(b, q):
                    have_messages(b, q)
                    passed(pe)
                    with pe.Fori(0, WIDES) as v:
                        pe.wait_ge(wide_hot_made, window(r, b, q, v))
                        pe.wait_ge(wide_added, window(r, b, q, v, 1))
                        for t in range(T):
                            mm = nc.tensor.matmul(bank[4][0:high, 0:WIDE], summed(q, t), wide_hot[:, t, :],
                                                  start=(t == 0), stop=(t == T - 1))
                        mm.then_inc(wide_summed, 1)
                    pe.wait_ge(wide_summed, window(r, b, q, WIDES - 1))
                    pe.sem_inc(group_summed, 1)

                def ahead(b, q):
                    if kind == GATED:
                        edge_hidden(b, q)
                    if kind == ATTEND:
                        edge_weights(b, q)
                        if near:
                            edge_queries(b, q)

                def run(b, node, first, last):
                    if first:
                        ahead(b, 0)
                    for q in per:
                        node(q)
                        if q + 1 < SLOTS or not last:
                            ahead(*with_body(b, q + 1))
                        if kind == GATED:
                            edge_weights(b, q)
                        if near and (q or not first):
                            sum_group(b, q - 1)
                        if not near:
                            sum_wide(b, q)
                    if near and last:
                        sum_group(b, SLOTS - 1)
                    node(SLOTS)
                return run

            def nodes(r, near):
                what = ROUNDS[r][1]

                def run(place, j, b):
                    if place == 1 and r in plan["own"]:
                        if near and r in SERVED:
                            pe.wait_ge(served_kept, before_tile(list(SERVED), r, j) + (CREDIT - 1))
                        if not near and r in plan["turned"]:
                            pe.wait_ge(kvq_made, tile(r, j, [r], 1))
                        pe.wait_ge(x_staged, tile(r, j, plan["own"]))
                        nc.tensor.transpose(TURN[0:D, 0:P], x_tile[:, :], ident).then_inc(x_turned, 1)
                    if place == 2:
                        pe.wait_ge(acc_staged, tile(r, j, plan["edge"]))
                        pe.wait_ge(node_made, tile(r, j, back=1))
                        if what == "attended":
                            nc.tensor.transpose(NODE[:, 0:HIGH], acc_tile[:, :], ident[0:HIGH, 0:HIGH]).then_inc(node_summed, 1)
                            return
                        pe.wait_ge(x_turn_made, tile(r, j, plan["own"]))
                        if what == "first":
                            nc.tensor.matmul(NODE[:, 0:D + 1], x_turn[:, :], w("self0", n=D + 1), start=True, stop=False)
                            nc.tensor.matmul(NODE[:, 0:D + 1], acc_tile[0:D + 1, :], w("neigh0", n=D + 1), start=False,
                                             stop=True).then_inc(node_summed, 1)
                        else:
                            own, neigh = ROUND_W[r]
                            nc.tensor.matmul(NODE[:, 0:D], x_turn[:, :], w(own), start=True, stop=True)
                            nc.tensor.matmul(NODE[:, D:2 * D], acc_tile[0:D, :], w(neigh, k=D), start=True,
                                             stop=True).then_inc(node_summed, 1)
                return run

            def served(r, near):
                def run(place, j):
                    if r in plan["turned"] and place == TURN_AT[r]:
                        turn(r, j, near)
                    if r in plan["turned"] and place == TURN_AT[r] + 1:
                        serve(r, j)
                return run

            def turn(r, j, near=True):
                pe.wait_ge(node_made, tile(r, j))
                if near and r in plan["own"]:
                    pe.wait_ge(x_turn_made, tile(r, j if isinstance(j, int) and j == TILES - 1 else j + 1, plan["own"]))
                if not near:
                    pe.wait_ge(x_turn_made, tile(r, j, plan["own"]))
                if r in SERVED:
                    pe.wait_ge(served_kept, tile(r, j, list(SERVED), 1))
                else:
                    pe.wait_ge(kvq_made, tile(r, j, [r], 1))
                nc.tensor.transpose(TURN[0:D, 0:P], new_tile[:, :], ident).then_inc(new_turned, 1)

            def serve(r, j):
                pe.wait_ge(new_turn_made, tile(r, j, plan["turned"]))
                if r in SERVED:
                    own, neigh = ROUND_W[SERVED[r]]
                    nc.tensor.matmul(SERVE[:, 0:D], new_turn[:, :], w(own), start=True, stop=True)
                    nc.tensor.matmul(SERVE[:, D:2 * D], new_turn[:, :], w(neigh), start=True, stop=True).then_inc(served_summed, 1)
                    return
                pe.wait_ge(kvq_made, tile(r, j, [r], 1))
                for i, name in enumerate(("key", "value", "query")):
                    mm = nc.tensor.matmul(SERVE[:, i * D:(i + 1) * D], new_turn[:, :], w(name), start=True, stop=True)
                mm.then_inc(kvq_summed, 1)

            def find_starts():
                pe.wait_ge(degree_made, TILES + CREDIT)
                pe.wait_ge(node_made, TILES + CREDIT)
                nc.tensor.matmul(NODE[0:TILES, 0:BLOCKS + 1], deg_all[:, :], con[:, C_CUM:C_CUM + BLOCKS + 1], start=True,
                                 stop=True).then_inc(degrees_turned, 1)
                pe.wait_ge(starts_made, 1)
                nc.tensor.matmul(NODE[0:TILES, 0:1], con[0:TILES, C_TRI:C_TRI + TILES], before[:, BLOCKS:BLOCKS + 1], start=True,
                                 stop=True).then_inc(degrees_turned, 1)

            def strips(r):
                def build_block(n, g):
                    pe.wait_ge(block_kept, block_of(n, g) - 4)
                    for i in range(BT):
                        slot = (g * BT + i) % RING
                        pe.wait_ge(hot_made, hot_of(n, g, i, RING))
                        if i == BT - 1 and (g + 1) % PER_PIECE == 0:
                            pe.wait_ge(low_by_act, piece_of(n, g // PER_PIECE))
                        nc.tensor.matmul(bank[g % 4][:, 0:CODES], low_hot[slot], code_hot[slot], start=(i == 0),
                                         stop=(i == BT - 1)).then_inc(hot_summed, 1)

                def multiply(n, p, half, piece):
                    if piece == 0:
                        if isinstance(n, int) and n == 0:
                            pe.wait_ge(y_part_made, y_step(BEFORE[r], TILES - 1, 3))
                        pe.wait_ge(folded, tile(r, n, BLENDED, 2))
                        if r == BUILD:
                            pe.wait_ge(block_kept, block_of(n, BLOCKS - 1))
                    if r != BUILD and piece % 2 == 0:
                        pe.wait_ge(chunk_landed[p][piece // 2], loads_of(r, p, half))
                    for k in range(PIECE_K[piece], PIECE_K[piece + 1]):
                        mm = nc.tensor.matmul(PRODUCT[p][:, 0:PARTS * D], strip[p][:, k * P:(k + 1) * P],
                                              y_of[r][:, k * PARTS * D:(k + 1) * PARTS * D], start=(k == 0), stop=(k == TILES - 1))
                    if piece % 2:
                        mm.then_inc(chunk_summed, 1)

                def step(j, lag):
                    ready_tile = j(lag + 2) if r in plan["turned"] else None
                    for g in range(PIECES):
                        if r == BUILD and j(0):
                            for block in range(g * PER_PIECE, (g + 1) * PER_PIECE):
                                build_block(j(0)[0], block)
                        if g == 0 and ready_tile:
                            turn(r, ready_tile[0])
                        if g == 3 and ready_tile:
                            serve(r, ready_tile[0])
                        if j(lag):
                            multiply(*j(lag), g)
                return step

            def program(near):
                for r in range(len(ROUNDS)):
                    if near and r == BUILD:
                        find_starts()
                    if r in plan["edge"]:
                        schedule(pe, r, near, groups(r, near), nodes(r, near), served(r, near))
                    else:
                        dense(pe, r, strips(r))

            either(pe, program)


def before_tile(of, r, j):
    whole = len([k for k in of if k < r]) * TILES
    return j + whole if r in of else whole


def stored_before(of, r, j):
    n = before_tile(of, r, j)
    return n * 16 + 16


def kept_before(of, r, j):
    return before_tile(of, r, j) + CREDIT


def kernel(**inputs):
    import numpy as np
    import concourse.bacc as _bacc
    from concourse.bass_utils import run_bass_kernel_spmd as _run

    v = {k: np.asarray(a) for k, a in inputs.items()}
    f = np.float32

    def by_tile(a):
        a = a.reshape(GROUPS * T, P).T
        return np.ascontiguousarray(np.concatenate([a, a[:, :AHEAD * T]], axis=1))

    dst = np.concatenate([v["dst"], (N + np.arange(EP - E) * (NP - N) // (EP - E)).astype(v["dst"].dtype)])
    packed = np.zeros((D + 1, W_WIDTH), f)

    def put(name, matrix, bias=None):
        packed[0:D, W_COL[name]:W_COL[name] + D] = matrix
        if bias is not None:
            packed[D, W_COL[name]:W_COL[name] + D] = bias

    put("gate2", v["L0_gnn_W2"].T, v["L0_gnn_b2"])
    put("self0", v["L0_gnn_Ws"].T, v["L0_gnn_bs"])
    packed[D, W_COL["bias0"]:W_COL["bias0"] + D] = v["L0_gnn_bn"]
    put("neigh0", v["L0_gnn_Wn"].T)
    packed[D, W_COL["neigh0"] + D] = 1.0
    put("selfs1", v["L1_gnn_W_self1"], v["L1_gnn_b1"])
    put("neigh1", v["L1_gnn_W_neigh1"])
    put("selfs2", v["L1_gnn_W_self2"], v["L1_gnn_b2"])
    put("neigh2", v["L1_gnn_W_neigh2"])
    put("edge", v["L2_gnn_We"], v["L2_gnn_be"])
    put("key", v["L2_gnn_Wk"], v["L2_gnn_bk"])
    put("value", v["L2_gnn_Wv"], v["L2_gnn_bv"])
    put("query", v["L2_gnn_Wq"], v["L2_gnn_bq"])
    put("selfs4", v["L3_gnn_Wr1"].T, v["L3_gnn_bl1"])
    put("neigh4", v["L3_gnn_Wl1"].T)
    put("selfs5", v["L3_gnn_Wr2"].T, v["L3_gnn_bl2"])
    put("neigh5", v["L3_gnn_Wl2"].T)
    packed[0:D, W_WIDTH - 1] = v["L0_gnn_b1"]

    con = np.zeros((P, C_WIDTH), f)
    con[:, C_IDENT:C_IDENT + P] = np.eye(P, dtype=f)
    con[:, C_IOTA:C_IOTA + WIDE] = np.arange(WIDE, dtype=f)
    con[:, C_WIDE:C_WIDE + WIDES] = np.arange(WIDES, dtype=f) * WIDE
    con[:, C_LIMIT:C_LIMIT + GROUPS] = ((np.arange(GROUPS) + OVERLAP) // SLOTS - (TILE_LAG - 1)) * P

    con[:, C_EPS] = EPS
    con[:, C_NODE] = np.arange(P, dtype=f)

    con[:, C_SHIFT:C_SHIFT + TILES * BLOCKS] = np.arange(TILES * BLOCKS, dtype=f) * CODES
    con[:, C_CUM:C_CUM + BLOCKS] = np.arange(P)[:, None] < np.arange(BLOCKS)[None, :] * BLOCK
    con[:, C_CUM + BLOCKS] = 1.0
    con[0:TILES, C_TRI:C_TRI + TILES] = np.arange(TILES)[:, None] < np.arange(TILES)[None, :]
    pairs = np.zeros((EP + BT * P, 2), v["dst"].dtype)
    pairs[:, 1] = 2 * NP
    pairs[:E, 0] = v["src"]
    pairs[:EP, 1] = dst

    arrays = {
        "x": np.concatenate([v["x"], np.zeros((NP - N, D), f)]),
        "src": by_tile(np.append(v["src"], np.zeros(EP - E, v["src"].dtype))),
        "dst": by_tile(dst),
        "dst_next": np.ascontiguousarray(np.append(dst[1:], dst[-1]).reshape(GROUPS * T, P).T),
        "pairs": pairs.reshape(1, -1),
        "codes": np.tile(np.arange(CODES, dtype=np.float16), (P, 1)),
        "dst_row": dst.reshape(1, EP),
        "base": np.ascontiguousarray(dst[::GE].reshape(1, GROUPS)),
        "attr17": np.ascontiguousarray(np.concatenate([v["edge_attr_17"].T, np.zeros((ATTR, EP - E), f)], axis=1)),
        "attr96": np.ascontiguousarray(np.concatenate([v["edge_attr_96"].T, np.zeros((D, EP - E), f)], axis=1)),
        "gate1": np.ascontiguousarray(v["L0_gnn_W1"].T),
        "weights": packed,
        "consts": con,
    }
    nc = _bacc.Bacc("TRN2", target_bir_lowering=False, num_devices=1)
    args = {n: nc.dram_tensor(f"in_{n}", a.shape, mybir.dt.from_np(a.dtype), kind="ExternalInput").ap()
            for n, a in arrays.items()}
    out = nc.dram_tensor("out_x", (N, D), F32, kind="ExternalOutput").ap()
    build(nc, out=out, **args)
    r = _run(nc, [{f"in_{n}": a for n, a in arrays.items()}], core_ids=[0])
    return r.results[0]["out_x"]
```
